# Optimizing a Trainium2 kernel written in Bass

```python
import numpy as np
import jax
import jax.numpy as jnp

def _softmax(x, axis=-1):
    return jax.nn.softmax(x, axis=axis)
def _gelu(x):
    return jax.nn.gelu(x, approximate=True)
def _silu(x):
    return jax.nn.silu(x)
def _sigmoid(x):
    return jax.nn.sigmoid(x)
def _layernorm(x, axis=-1, eps=1e-5):
    m = jnp.mean(x, axis=axis, keepdims=True)
    v = jnp.var(x, axis=axis, keepdims=True)
    return (x - m) / jnp.sqrt(v + eps)
def _scatter_add(tgt, idx, src, axis=0):
    return tgt.at[idx].add(src)
def _segment_sum(src, seg, n):
    return jax.ops.segment_sum(src, seg, n)

kernel_name = 'mk_conv_seq_d2_conv_nhwc256_fc5789'

def setup_inputs(seed: int = 0):
    np.random.seed(seed)
    _w = jnp.asarray
    def _rec_inputs():
        import jax
        import jax.numpy as jnp
        _gk = jax.random.key(seed)
        x = -0.0005207 + 1.001 * jax.random.normal(jax.random.fold_in(_gk, 1), (2, 64, 64, 256), jnp.float32)
        return x
    x = _rec_inputs()
    def _L0_conv_setup():
        import jax, jax.numpy as jnp
        import numpy as np
        EPS = 1e-05

        def _layer_norm(x, g, b):
            m = jnp.mean(x, axis=-1, keepdims=True)
            v = jnp.var(x, axis=-1, keepdims=True)
            return (x - m) * jax.lax.rsqrt(v + EPS) * g + b
        key = jax.random.key(seed)
        ks = jax.random.split(key, 16)
        B, N, E, H = (2, 64, 256, 8)
        F = 2 * E
        s = 1.0 / np.sqrt(E)
        return {'x_in': jax.random.normal(ks[0], (B, N, N, E), jnp.float32), 'Wq': jax.random.normal(ks[1], (E, E), jnp.float32) * s, 'Wk': jax.random.normal(ks[2], (E, E), jnp.float32) * s, 'Wv1': jax.random.normal(ks[3], (E, E), jnp.float32) * s, 'Wv2': jax.random.normal(ks[4], (E, E), jnp.float32) * s, 'Wo': jax.random.normal(ks[5], (E, E), jnp.float32) * s, 'ln_agg_g': jnp.ones((E,), jnp.float32), 'ln_agg_b': jnp.zeros((E,), jnp.float32), 'W1': jax.random.normal(ks[6], (E, F), jnp.float32) * s, 'b1': jnp.zeros((F,), jnp.float32), 'W2': jax.random.normal(ks[7], (F, E), jnp.float32) * (1.0 / np.sqrt(F)), 'b2': jnp.zeros((E,), jnp.float32), 'ln_out_g': jnp.ones((E,), jnp.float32), 'ln_out_b': jnp.zeros((E,), jnp.float32)}
    _L0_conv_all = _L0_conv_setup()
    _L0_conv_in = {k: v for k, v in _L0_conv_all.items() if k in ('Wq', 'Wk', 'Wv1', 'Wv2', 'Wo', 'ln_agg_g', 'ln_agg_b', 'W1', 'b1', 'W2', 'b2', 'ln_out_g', 'ln_out_b', )}
    del _L0_conv_all

    def _L1_conv_setup():
        import jax, jax.numpy as jnp
        import numpy as np
        D_MODEL = 256
        D_STATE = 64
        D_CONV = 4
        EXPAND = 2
        HEADDIM = 64
        D_INNER = EXPAND * D_MODEL
        NHEADS = D_INNER // HEADDIM
        CONV_CH = D_INNER + 2 * D_STATE
        D_IN_PROJ = 2 * D_INNER + 2 * D_STATE + NHEADS

        def _dwconv_causal(x, w, b):
            out = jax.lax.conv_general_dilated(x.transpose(0, 2, 1), w, (1,), [(D_CONV - 1, 0)], dimension_numbers=('NCH', 'OIH', 'NCH'), feature_group_count=CONV_CH)
            return out.transpose(0, 2, 1) + b

        def _mamba2(u, in_w, conv_w, conv_b, dt_bias, A_log, D, norm_w, out_w):
            b, L, _ = u.shape
            zxbcdt = u @ in_w.T
            z = zxbcdt[..., :D_INNER]
            xBC = zxbcdt[..., D_INNER:D_INNER + CONV_CH]
            dt = zxbcdt[..., D_INNER + CONV_CH:]
            xBC = jax.nn.silu(_dwconv_causal(xBC, conv_w, conv_b))
            x = xBC[..., :D_INNER].reshape(b, L, NHEADS, HEADDIM)
            Bm = xBC[..., D_INNER:D_INNER + D_STATE]
            Cm = xBC[..., D_INNER + D_STATE:]
            dt = jax.nn.softplus(dt + dt_bias)
            dA = jnp.exp(dt * -jnp.exp(A_log))

            def step(h, inp):
                dA_t, x_t, B_t, dt_t, C_t = inp
                h = h * dA_t[:, :, None, None] + (dt_t[:, :, None] * x_t)[..., None] * B_t[:, None, None, :]
                return (h, jnp.einsum('bhpn,bn->bhp', h, C_t))
            h0 = jnp.zeros((b, NHEADS, HEADDIM, D_STATE), u.dtype)
            xs = (dA.transpose(1, 0, 2), x.transpose(1, 0, 2, 3), Bm.transpose(1, 0, 2), dt.transpose(1, 0, 2), Cm.transpose(1, 0, 2))
            _, ys = jax.lax.scan(step, h0, xs)
            y = ys.transpose(1, 0, 2, 3) + x * D[None, None, :, None]
            y = y.reshape(b, L, D_INNER) * jax.nn.silu(z)
            y = y * jax.lax.rsqrt(jnp.mean(y * y, axis=-1, keepdims=True) + 1e-05) * norm_w
            return y @ out_w.T
        key = jax.random.key(seed)
        ks = jax.random.split(key, 20)

        def mk(i, shape, s=0.02):
            return jax.random.normal(ks[i], shape, jnp.float32) * s
        inp = {'x': jax.random.normal(ks[0], (8, 64, 64, D_MODEL), jnp.float32)}
        for pre, off in (('mh', 1), ('mv', 9)):
            inp[pre + '_in_w'] = mk(off, (D_IN_PROJ, D_MODEL))
            inp[pre + '_conv_w'] = mk(off + 1, (CONV_CH, 1, D_CONV), 0.2)
            inp[pre + '_conv_b'] = jnp.zeros((CONV_CH,), jnp.float32)
            inp[pre + '_dt_bias'] = mk(off + 3, (NHEADS,), 0.5)
            inp[pre + '_A_log'] = jnp.log(jax.random.uniform(ks[off + 4], (NHEADS,), jnp.float32, 1.0, 16.0))
            inp[pre + '_D'] = jnp.ones((NHEADS,), jnp.float32)
            inp[pre + '_norm_w'] = jnp.ones((D_INNER,), jnp.float32)
            inp[pre + '_out_w'] = mk(off + 7, (D_MODEL, D_INNER))
        inp['fc_w'] = mk(17, (D_MODEL, 4 * D_MODEL))
        inp['fc_b'] = jnp.zeros((D_MODEL,), jnp.float32)
        return inp
    _L1_conv_all = _L1_conv_setup()
    _L1_conv_in = {k: v for k, v in _L1_conv_all.items() if k in ('mh_in_w', 'mh_conv_w', 'mh_conv_b', 'mh_dt_bias', 'mh_A_log', 'mh_D', 'mh_norm_w', 'mh_out_w', 'mv_in_w', 'mv_conv_w', 'mv_conv_b', 'mv_dt_bias', 'mv_A_log', 'mv_D', 'mv_norm_w', 'mv_out_w', 'fc_w', 'fc_b', )}
    del _L1_conv_all

    return {
        "x": x,
        "L0_conv_Wq": _L0_conv_in["Wq"],
        "L0_conv_Wk": _L0_conv_in["Wk"],
        "L0_conv_Wv1": _L0_conv_in["Wv1"],
        "L0_conv_Wv2": _L0_conv_in["Wv2"],
        "L0_conv_Wo": _L0_conv_in["Wo"],
        "L0_conv_ln_agg_g": _L0_conv_in["ln_agg_g"],
        "L0_conv_ln_agg_b": _L0_conv_in["ln_agg_b"],
        "L0_conv_W1": _L0_conv_in["W1"],
        "L0_conv_b1": _L0_conv_in["b1"],
        "L0_conv_W2": _L0_conv_in["W2"],
        "L0_conv_b2": _L0_conv_in["b2"],
        "L0_conv_ln_out_g": _L0_conv_in["ln_out_g"],
        "L0_conv_ln_out_b": _L0_conv_in["ln_out_b"],
        "L1_conv_mh_in_w": _L1_conv_in["mh_in_w"],
        "L1_conv_mh_conv_w": _L1_conv_in["mh_conv_w"],
        "L1_conv_mh_conv_b": _L1_conv_in["mh_conv_b"],
        "L1_conv_mh_dt_bias": _L1_conv_in["mh_dt_bias"],
        "L1_conv_mh_A_log": _L1_conv_in["mh_A_log"],
        "L1_conv_mh_D": _L1_conv_in["mh_D"],
        "L1_conv_mh_norm_w": _L1_conv_in["mh_norm_w"],
        "L1_conv_mh_out_w": _L1_conv_in["mh_out_w"],
        "L1_conv_mv_in_w": _L1_conv_in["mv_in_w"],
        "L1_conv_mv_conv_w": _L1_conv_in["mv_conv_w"],
        "L1_conv_mv_conv_b": _L1_conv_in["mv_conv_b"],
        "L1_conv_mv_dt_bias": _L1_conv_in["mv_dt_bias"],
        "L1_conv_mv_A_log": _L1_conv_in["mv_A_log"],
        "L1_conv_mv_D": _L1_conv_in["mv_D"],
        "L1_conv_mv_norm_w": _L1_conv_in["mv_norm_w"],
        "L1_conv_mv_out_w": _L1_conv_in["mv_out_w"],
        "L1_conv_fc_w": _L1_conv_in["fc_w"],
        "L1_conv_fc_b": _L1_conv_in["fc_b"],
    }

def reference(x, L0_conv_Wq, L0_conv_Wk, L0_conv_Wv1, L0_conv_Wv2, L0_conv_Wo, L0_conv_ln_agg_g, L0_conv_ln_agg_b, L0_conv_W1, L0_conv_b1, L0_conv_W2, L0_conv_b2, L0_conv_ln_out_g, L0_conv_ln_out_b, L1_conv_mh_in_w, L1_conv_mh_conv_w, L1_conv_mh_conv_b, L1_conv_mh_dt_bias, L1_conv_mh_A_log, L1_conv_mh_D, L1_conv_mh_norm_w, L1_conv_mh_out_w, L1_conv_mv_in_w, L1_conv_mv_conv_w, L1_conv_mv_conv_b, L1_conv_mv_dt_bias, L1_conv_mv_A_log, L1_conv_mv_D, L1_conv_mv_norm_w, L1_conv_mv_out_w, L1_conv_fc_w, L1_conv_fc_b):
    import jax
    import jax.numpy as jnp
    def _L0_conv_ref(x_in, Wq, Wk, Wv1, Wv2, Wo, ln_agg_g, ln_agg_b, W1, b1, W2, b2, ln_out_g, ln_out_b):
        import jax, jax.numpy as jnp
        import numpy as np
        EPS = 1e-05

        def _layer_norm(x, g, b):
            m = jnp.mean(x, axis=-1, keepdims=True)
            v = jnp.var(x, axis=-1, keepdims=True)
            return (x - m) * jax.lax.rsqrt(v + EPS) * g + b
        B, N, _, E = x_in.shape
        H = 8
        d_k = E // H
        q = (x_in @ Wq).reshape(B, N, N, H, d_k)
        k = (x_in @ Wk).reshape(B, N, N, H, d_k)
        v1 = (x_in @ Wv1).reshape(B, N, N, H, d_k)
        v2 = (x_in @ Wv2).reshape(B, N, N, H, d_k)
        scores = jnp.einsum('bilhd,bljhd->biljh', q, k) / np.sqrt(d_k)
        att = jax.nn.softmax(scores, axis=2)
        out = jnp.einsum('biljh,bilhd,bljhd->bijhd', att, v1, v2)
        attn_out = out.reshape(B, N, N, E) @ Wo
        h = x_in + attn_out
        h = _layer_norm(h, ln_agg_g, ln_agg_b)
        mlp = jax.nn.relu(h @ W1 + b1) @ W2 + b2
        h = mlp + h
        return _layer_norm(h, ln_out_g, ln_out_b)

    def _L1_conv_ref(x, mh_in_w, mh_conv_w, mh_conv_b, mh_dt_bias, mh_A_log, mh_D, mh_norm_w, mh_out_w, mv_in_w, mv_conv_w, mv_conv_b, mv_dt_bias, mv_A_log, mv_D, mv_norm_w, mv_out_w, fc_w, fc_b):
        import jax, jax.numpy as jnp
        import numpy as np
        D_MODEL = 256
        D_STATE = 64
        D_CONV = 4
        EXPAND = 2
        HEADDIM = 64
        D_INNER = EXPAND * D_MODEL
        NHEADS = D_INNER // HEADDIM
        CONV_CH = D_INNER + 2 * D_STATE
        D_IN_PROJ = 2 * D_INNER + 2 * D_STATE + NHEADS

        def _dwconv_causal(x, w, b):
            out = jax.lax.conv_general_dilated(x.transpose(0, 2, 1), w, (1,), [(D_CONV - 1, 0)], dimension_numbers=('NCH', 'OIH', 'NCH'), feature_group_count=CONV_CH)
            return out.transpose(0, 2, 1) + b

        def _mamba2(u, in_w, conv_w, conv_b, dt_bias, A_log, D, norm_w, out_w):
            b, L, _ = u.shape
            zxbcdt = u @ in_w.T
            z = zxbcdt[..., :D_INNER]
            xBC = zxbcdt[..., D_INNER:D_INNER + CONV_CH]
            dt = zxbcdt[..., D_INNER + CONV_CH:]
            xBC = jax.nn.silu(_dwconv_causal(xBC, conv_w, conv_b))
            x = xBC[..., :D_INNER].reshape(b, L, NHEADS, HEADDIM)
            Bm = xBC[..., D_INNER:D_INNER + D_STATE]
            Cm = xBC[..., D_INNER + D_STATE:]
            dt = jax.nn.softplus(dt + dt_bias)
            dA = jnp.exp(dt * -jnp.exp(A_log))

            def step(h, inp):
                dA_t, x_t, B_t, dt_t, C_t = inp
                h = h * dA_t[:, :, None, None] + (dt_t[:, :, None] * x_t)[..., None] * B_t[:, None, None, :]
                return (h, jnp.einsum('bhpn,bn->bhp', h, C_t))
            h0 = jnp.zeros((b, NHEADS, HEADDIM, D_STATE), u.dtype)
            xs = (dA.transpose(1, 0, 2), x.transpose(1, 0, 2, 3), Bm.transpose(1, 0, 2), dt.transpose(1, 0, 2), Cm.transpose(1, 0, 2))
            _, ys = jax.lax.scan(step, h0, xs)
            y = ys.transpose(1, 0, 2, 3) + x * D[None, None, :, None]
            y = y.reshape(b, L, D_INNER) * jax.nn.silu(z)
            y = y * jax.lax.rsqrt(jnp.mean(y * y, axis=-1, keepdims=True) + 1e-05) * norm_w
            return y @ out_w.T
        B, H, W, C = x.shape
        mh = (mh_in_w, mh_conv_w, mh_conv_b, mh_dt_bias, mh_A_log, mh_D, mh_norm_w, mh_out_w)
        mv = (mv_in_w, mv_conv_w, mv_conv_b, mv_dt_bias, mv_A_log, mv_D, mv_norm_w, mv_out_w)
        x_h = x.reshape(B * H, W, C)
        h1 = _mamba2(x_h, *mh)
        h2 = jnp.flip(_mamba2(jnp.flip(x_h, axis=0), *mh), axis=0)
        h = jnp.concatenate([h1, h2], axis=-1).reshape(B, H, W, -1)
        x_v = x.transpose(0, 2, 1, 3).reshape(B * W, H, C)
        v1 = _mamba2(x_v, *mv)
        v2 = jnp.flip(_mamba2(jnp.flip(x_v, axis=0), *mv), axis=0)
        v = jnp.concatenate([v1, v2], axis=-1).reshape(B, W, H, -1).transpose(0, 2, 1, 3)
        out = jnp.concatenate([v, h], axis=-1)
        return out @ fc_w.T + fc_b

    def _gn(v, G=32, eps=1e-5):
        B_, H_, W_, C_ = v.shape
        g = v.reshape(B_, H_, W_, G, C_ // G)
        m = jnp.mean(g, axis=(1, 2, 4), keepdims=True)
        s = jnp.var(g, axis=(1, 2, 4), keepdims=True)
        return ((g - m) / jnp.sqrt(s + eps)).reshape(v.shape)

    def _ln_c(v, eps=1e-6):
        m = jnp.mean(v, axis=-1, keepdims=True)
        s = jnp.var(v, axis=-1, keepdims=True)
        return (v - m) / jnp.sqrt(s + eps)

    def _ln_t(v, eps=1e-5):
        m = jnp.mean(v, axis=-1, keepdims=True)
        s = jnp.var(v, axis=-1, keepdims=True)
        return (v - m) / jnp.sqrt(s + eps)

    def _to_tokens(v):
        B_, H_, W_, C_ = v.shape
        return v.reshape(B_, H_ * W_, C_)
    def _from_tokens(t, like):
        return t.reshape(like.shape)

    x = _L0_conv_ref(x, L0_conv_Wq, L0_conv_Wk, L0_conv_Wv1, L0_conv_Wv2, L0_conv_Wo, L0_conv_ln_agg_g, L0_conv_ln_agg_b, L0_conv_W1, L0_conv_b1, L0_conv_W2, L0_conv_b2, L0_conv_ln_out_g, L0_conv_ln_out_b)
    x = _L1_conv_ref(x, L1_conv_mh_in_w, L1_conv_mh_conv_w, L1_conv_mh_conv_b, L1_conv_mh_dt_bias, L1_conv_mh_A_log, L1_conv_mh_D, L1_conv_mh_norm_w, L1_conv_mh_out_w, L1_conv_mv_in_w, L1_conv_mv_conv_w, L1_conv_mv_conv_b, L1_conv_mv_dt_bias, L1_conv_mv_A_log, L1_conv_mv_D, L1_conv_mv_norm_w, L1_conv_mv_out_w, L1_conv_fc_w, L1_conv_fc_b)
    return x


_drawn_inputs = setup_inputs


def setup_inputs(seed=0):
    import zlib

    import numpy as np

    out = dict(_drawn_inputs(seed))
    spreads = {'L0_conv_ln_agg_g': (1.0, 0.2),
     'L0_conv_ln_agg_b': (0.0, 0.1),
     'L0_conv_b1': (0.0, 0.1),
     'L0_conv_b2': (0.0, 0.1),
     'L0_conv_ln_out_g': (1.0, 0.2),
     'L0_conv_ln_out_b': (0.0, 0.1),
     'L1_conv_mh_conv_b': (0.0, 0.1),
     'L1_conv_mh_D': (1.0, 0.2),
     'L1_conv_mh_norm_w': (1.0, 0.2),
     'L1_conv_mv_conv_b': (0.0, 0.1),
     'L1_conv_mv_D': (1.0, 0.2),
     'L1_conv_mv_norm_w': (1.0, 0.2),
     'L1_conv_fc_b': (0.0, 0.1)}
    factors = {'L1_conv_mh_dt_bias': 4.947,
     'L1_conv_mh_A_log': 64.0,
     'L1_conv_mv_dt_bias': 8.0,
     'L1_conv_mv_A_log': 8.0}
    for name, (base, spread) in spreads.items():
        noise = np.random.default_rng([zlib.crc32(name.encode()), seed]).standard_normal(out[name].shape)
        drawn = base * np.exp(spread * noise) if base else spread * noise
        out[name] = jnp.asarray(drawn.astype(out[name].dtype))
    for name, factor in factors.items():
        out[name] = (out[name] * factor).astype(out[name].dtype)
    return out
```

```python
from contextlib import ExitStack

import concourse.bass as bass
from concourse import mybir

F32 = mybir.dt.float32
ALU = mybir.AluOpType
ACT = mybir.ActivationFunctionType
AX_X = mybir.AxisListType.X

P = 128
BANK = 512
B, N, E = 2, 64, 256
H = 8
DK = E // H
PAIRS = H // 2
TOK = B * N * N
KT = E // P
F = 2 * E
FT = F // P
STRIPS = 4
STRIP_D = DK // (2 * STRIPS)
EPS = 1e-5
SCALE = DK ** -0.5

DI = 2 * E
DS = 64
NH = 8
HD = DI // NH
CT = DI // P
TAPS = 4
XB0 = DI
DT0 = DI + DI + 2 * DS
DPROJ = DT0 + NH
L = 64
CHUNK = 512
TT = CHUNK // P
SEQS = CHUNK // L
NCHUNK = TOK // CHUNK
A_LOG_MAX = 80.0


def need(eng, sem, value):
    if isinstance(value, int) and value <= 0:
        return
    eng.wait_ge(sem, value)


def need_apart(eng, passed, *waits):
    for sem, value in waits:
        need(eng, sem, value)
    eng.sem_inc(passed, 1)


def pairs_of_steps(eng, n, step):
    step(0, 0)
    step(1, 1)
    with eng.Fori(1, n // 2) as r:
        step(r * 2, 0)
        step(r * 2 + 1, 1)


class Tools:

    def __init__(self, nc, ctx, tag):
        self.nc, self.ctx, self.tag = nc, ctx, tag

    def sb(self, name, shape, dt=F32):
        return self.ctx.enter_context(self.nc.sbuf_tensor(f"{self.tag}_{name}", shape, dt))

    def banks(self, n=8):
        return [self.ctx.enter_context(self.nc.psum_tensor(f"{self.tag}_bank{i}", [P, BANK], F32)) for i in range(n)]

    def sem(self, name):
        return self.nc.alloc_semaphore(name=f"{self.tag}_{name}")


class Chain:

    def __init__(self, eng, sem, base=0):
        self.eng, self.sem, self.base, self.n = eng, sem, base, 0

    def mark(self, ins):
        self.n += 1
        ins.then_inc(self.sem, 1)

    def value(self):
        return self.base + self.n

    def wait(self):
        self.eng.wait_ge(self.sem, self.value())

    def link(self, ins):
        self.mark(ins)
        self.wait()


def make_identity(pool, ident, sem):
    pool.memset(ident[:, :], 0.0).then_inc(sem, 1)
    pool.wait_ge(sem, 1)
    pool.affine_select(out=ident[:, :], in_=ident[:, :], compare_op=ALU.not_equal, fill=1.0, base=0,
                       pattern=[[-1, P]], channel_multiplier=1).then_inc(sem, 1)




def block_projections(nc, x, W, qk_dram, v_dram):
    G = CHUNK // N
    STEPS = N // G * B
    with ExitStack() as ctx:
        t_ = Tools(nc, ctx, "prj")
        sb, sem = t_.sb, t_.sem
        bank = t_.banks()
        T_, Q_, V_ = bank[0:2], bank[2:6], bank[6:8]
        ident = sb("ident", [P, P])
        wqk = sb("wqk", [P, 2, KT, E])
        wv = sb("wv", [P, 2, KT, E])
        xin = [sb(f"xin{u}", [P, TT, E]) for u in range(2)]
        xT = [sb(f"xT{u}", [P, KT, CHUNK]) for u in range(2)]
        qk = [sb(f"qk{u}", [P, 4, CHUNK]) for u in range(2)]
        vs = [sb(f"vs{u}", [P, PAIRS, G, DK]) for u in range(2)]
        ident_set, w_loaded = sem("ident_set"), sem("w_loaded")
        x_loaded = [sem(f"x_loaded{u}") for u in range(2)]
        transposed, xT_by_act, xT_by_dve = sem("transposed"), sem("xT_by_act"), sem("xT_by_dve")
        qk_done, qk_by_act, qk_by_dve = sem("qk_done"), sem("qk_by_act"), sem("qk_by_dve")
        v_done, v_by_act, v_by_dve = sem("v_done"), sem("v_by_act"), sem("v_by_dve")
        qk_stored = [sem(f"qk_stored{u}") for u in range(2)]
        v_stored = [sem(f"v_stored{u}") for u in range(2)]
        block = ctx.enter_context(nc.Block())

        rows = x.rearrange("(g t p) c -> g p t c", t=TT, p=P)
        cols = x.rearrange("(b l g t jj) c -> b jj l g t c", b=B, l=N, g=STEPS, t=2)
        STORES = PAIRS * 16

        @block.sync
        def _(sp):
            for m, name in enumerate(("Wq", "Wk")):
                sp.dma_start(wqk[:, m], W[name].rearrange("(k p) n -> p k n", p=P)).then_inc(w_loaded, 16)
            for m, name in enumerate(("Wv1", "Wv2")):
                sp.dma_start(wv[:, m], W[name].rearrange("(k p) n -> p k n", p=P)).then_inc(w_loaded, 16)

            def load_rows(t, u):
                need(sp, transposed, 2 * t - 2)
                sp.dma_start(xin[u][:, :, :], rows[t]).then_inc(x_loaded[u], 16)

            def load_cols(t, u):
                sp.wait_ge(transposed, 2 * t - 2 + 2 * STEPS)
                for b in range(B):
                    for jj in range(2):
                        sp.dma_start(xin[u][jj * N:(jj + 1) * N, 2 * b:2 * b + 2, :],
                                     cols[b, jj, :, t]).then_inc(x_loaded[u], 16)

            pairs_of_steps(sp, STEPS, load_rows)
            pairs_of_steps(sp, STEPS, load_cols)

        @block.gpsimd
        def _(pool):
            make_identity(pool, ident, ident_set)

            def store_rows(t, u):
                pool.wait_ge(qk_by_act, 2 * t + 2)
                pool.wait_ge(qk_by_dve, 2 * t + 2)
                for m in range(4):
                    pool.dma_start(qk_dram[m // 2, (m % 2) * P:(m % 2 + 1) * P, bass.ds(t * CHUNK, CHUNK)],
                                   qk[u][:, m, :]).then_inc(qk_stored[u], 16)
                store_v(0, t, u)

            def store_v(v, t, u):
                pool.wait_ge(v_by_act, t + 1 + v * STEPS)
                pool.wait_ge(v_by_dve, t + 1 + v * STEPS)
                for pr in range(PAIRS):
                    if v == 0:
                        dst = v_dram[0, pr].rearrange("p b i d -> p (b i) d")[:, bass.ds(t * G, G), :]
                        pool.dma_start(dst, vs[u][:, pr]).then_inc(v_stored[u], 16)
                    else:
                        dst = v_dram[1, pr, :, :, bass.ds(t * (G // 2), G // 2), :]
                        pool.dma_start(dst, vs[u][:, pr].rearrange("p (b j) d -> p b j d", b=B))\
                            .then_inc(v_stored[u], 16)

            pairs_of_steps(pool, STEPS, store_rows)
            pairs_of_steps(pool, STEPS, lambda t, u: store_v(1, t, u))
            for u in range(2):
                pool.wait_ge(qk_stored[u], 64 * STEPS // 2)
                pool.wait_ge(v_stored[u], STORES * STEPS)

        def base(v):
            return v * STEPS

        @block.tensor
        def _(pe):
            pe.wait_ge(ident_set, 2)
            pe.wait_ge(w_loaded, 64)

            def step(v, t, u):
                need(pe, xT_by_act, t + base(v))
                need(pe, xT_by_dve, t + base(v))
                for k in range(KT):
                    for tile in range(TT):
                        mm = pe.transpose(T_[k][:, tile * P:(tile + 1) * P], xin[u][:, tile, k * P:(k + 1) * P],
                                          ident[:, :])
                    mm.then_inc(transposed, 1)
                pe.wait_ge(xT_by_act, t + 1 + base(v))
                pe.wait_ge(xT_by_dve, t + 1 + base(v))
                if v == 0:
                    need(pe, qk_by_act, 2 * t)
                    need(pe, qk_by_dve, 2 * t)
                    for m in range(4):
                        for k in range(KT):
                            mm = pe.matmul(Q_[m][:, :], wqk[:, m // 2, k, (m % 2) * P:(m % 2 + 1) * P],
                                           xT[u][:, k, :], start=(k == 0), stop=(k == KT - 1))
                        mm.then_inc(qk_done, 1)
                need(pe, v_by_act, t + base(v))
                need(pe, v_by_dve, t + base(v))
                for g in range(G):
                    for k in range(KT):
                        for h2 in range(2):
                            mm = pe.matmul(V_[g // 4][h2 * N:(h2 + 1) * N, (g % 4) * P:(g % 4 + 1) * P],
                                           xT[u][:, k, g * N:(g + 1) * N], wv[:, v, k, h2 * P:(h2 + 1) * P],
                                           start=(k == 0), stop=(k == KT - 1))
                    if g % 4 == 3:
                        mm.then_inc(v_done, 1)

            def loaded(v, r, u):
                per = 16 if v == 0 else 64
                pe.wait_ge(x_loaded[u], (r + 1) * per + (0 if v == 0 else STEPS // 2 * 16))

            for v in range(2):
                for u in range(2):
                    loaded(v, 0, u)
                    step(v, u, u)
                with pe.Fori(1, STEPS // 2) as r:
                    for u in range(2):
                        loaded(v, r, u)
                        step(v, r * 2 + u, u)

        def evacuate(eng, copy, mine, v, t, r, u):
            by_xT, by_qk, by_v = ((xT_by_act, qk_by_act, v_by_act), (xT_by_dve, qk_by_dve, v_by_dve))[mine]
            eng.wait_ge(transposed, 2 * (t + base(v)) + 1 + mine)
            if v == 0:
                need(eng, v_done, 2 * t - 2)
            else:
                eng.wait_ge(v_done, 2 * t - 2 + 2 * STEPS)
            copy(xT[u][:, mine, :], T_[mine][:, :]).then_inc(by_xT, 1)
            if v == 0:
                need(eng, qk_stored[u], r * 64)
                for m in (2 * mine, 2 * mine + 1):
                    eng.wait_ge(qk_done, 4 * t + m + 1)
                    copy(qk[u][:, m, :], Q_[m][:, :]).then_inc(by_qk, 1)
            need(eng, v_stored[u], r * STORES + v * STEPS // 2 * STORES)
            eng.wait_ge(v_done, 2 * (t + base(v)) + 1 + mine)
            copy(vs[u][:, :, mine * 4:mine * 4 + 4, :].rearrange("p r g d -> p g r d"),
                 V_[mine][:, :].rearrange("p (g r d) -> p g r d", g=4, r=PAIRS)).then_inc(by_v, 1)

        def all_steps(eng, copy, mine):
            for v in range(2):
                for u in range(2):
                    evacuate(eng, copy, mine, v, u, 0, u)
                with eng.Fori(1, STEPS // 2) as r:
                    for u in range(2):
                        evacuate(eng, copy, mine, v, r * 2 + u, r, u)

        @block.scalar
        def _(act):
            all_steps(act, lambda o, i: act.activation(o, i, ACT.Copy), 0)

        @block.vector
        def _(dve):
            all_steps(dve, lambda o, i: dve.tensor_copy(o, i), 1)


def steps(eng, n, step):
    step(0)
    with eng.Fori(1, n) as t:
        step(t)


def block_softmax(nc, qk_dram, att):
    LB = 4
    NB = N // LB
    KL = 16
    JB = 4
    HL = N // 2
    with ExitStack() as ctx:
        t_ = Tools(nc, ctx, "smx")
        sb, sem = t_.sb, t_.sem
        bank = t_.banks()
        S_, T_ = bank[0:4], bank[4:8]
        ident = sb("ident", [P, P])
        q = sb("q", [P, N * N])
        kb = [sb(f"kb{u}", [P, KL, 2, N]) for u in range(2)]
        raw = sb("raw", [P, 2, N, N])
        mx = sb("mx", [P, 2, N])
        rsum = sb("rsum", [P, 2, N])
        rinv = sb("rinv", [P, 2, N])
        ident_set, kb_zeroed, q_loaded = sem("ident_set"), sem("kb_zeroed"), sem("q_loaded")
        k_loaded = [sem(f"k_loaded{u}") for u in range(2)]
        scored, s_by_act, s_by_dve = sem("scored"), sem("s_by_act"), sem("s_by_dve")
        maxed, shifted, exped = sem("maxed"), sem("shifted"), sem("exped")
        summed, inverted, normed = sem("summed"), sem("inverted"), [sem("normed0"), sem("normed1")]
        passed = sem("passed")
        turned, t_by_act, t_by_dve = sem("turned"), sem("t_by_act"), sem("t_by_dve")
        block = ctx.enter_context(nc.Block())

        @block.sync
        def _(sp):
            def load(pr):
                need(sp, scored, pr * (2 * NB))
                for b in range(B):
                    sp.dma_start(q[b * 64:(b + 1) * 64, :],
                                 qk_dram[0, bass.ds(pr * 64, 64), b * N * N:(b + 1) * N * N]).then_inc(q_loaded, 16)
                for c in range(N // KL):
                    need(sp, scored, pr * (2 * NB) + (c - 1) * (2 * KL // LB))
                    for b in range(B):
                        for h2 in range(2):
                            lo = (2 * b + h2) * DK
                            src = qk_dram[1, bass.ds(pr * 64 + h2 * DK, DK),
                                          b * N * N + c * KL * N:b * N * N + (c + 1) * KL * N]
                            sp.dma_start(kb[c % 2][lo:lo + DK, :, h2, :], src.rearrange("p (l j) -> p l j", l=KL))\
                                .then_inc(k_loaded[c % 2], 16)

            sp.wait_ge(kb_zeroed, 2)
            steps(sp, PAIRS, load)

        @block.gpsimd
        def _(pool):
            for u in range(2):
                pool.memset(kb[u][:, :, :, :], 0.0).then_inc(kb_zeroed, 1)
            make_identity(pool, ident, ident_set)

            def step(pr):
                pool.wait_ge(inverted, pr * 2 + 1)
                for half in range(2):
                    v = raw[:, 0, half * HL:(half + 1) * HL, :]
                    pool.tensor_tensor(v, v, rinv[:, 0, :].unsqueeze(1).broadcast_to((P, HL, N)), ALU.mult)\
                        .then_inc(normed[0], 1)

            steps(pool, PAIRS, step)

        @block.tensor
        def _(pe):
            pe.wait_ge(ident_set, 2)
            qv = q[:, :].rearrange("p (i l) -> p l i", l=N)

            def step(pr):
                pe.wait_ge(q_loaded, pr * 32 + 32)
                for g in range(NB):
                    c = g * LB // KL
                    if g * LB % KL == 0:
                        pe.wait_ge(k_loaded[c % 2], pr * 128 + (c // 2) * 64 + 64)
                    need_apart(pe, passed, (s_by_act, pr * NB + g - 1), (s_by_dve, pr * NB + g - 1))
                    for l4 in range(LB):
                        for b in range(B):
                            r = slice(b * 64, (b + 1) * 64)
                            mm = pe.matmul(S_[2 * (g % 2) + b][r, l4 * P:(l4 + 1) * P], qv[r, g * LB + l4, :],
                                           kb[c % 2][r, (g * LB + l4) % KL, :, :], start=True, stop=True)
                            if l4 == LB - 1:
                                mm.then_inc(scored, 1)
                pe.wait_ge(normed[0], pr * 2 + 2)
                pe.wait_ge(normed[1], pr * 2 + 2)
                for g in range(N // JB):
                    need(pe, (t_by_act, t_by_dve)[g % 2], pr * 8 + g // 2 - 1)
                    for j in range(JB):
                        mm = pe.transpose(T_[g % 4][:, j * P:(j + 1) * P],
                                          raw[:, :, :, g * JB + j].rearrange("p h l -> p (h l)"), ident[:, :])
                    mm.then_inc(turned, 1)

            steps(pe, PAIRS, step)

        def copy_scores(eng, copy, b, pr, done):
            need(eng, turned, pr * 16)
            r = slice(b * 64, (b + 1) * 64)
            for g in range(NB):
                eng.wait_ge(scored, pr * (2 * NB) + 2 * g + 1 + b)
                copy(raw[r, :, g * LB:(g + 1) * LB, :],
                     S_[2 * (g % 2) + b][r, :].rearrange("p (l h j) -> p h l j", l=LB, h=2)).then_inc(done, 1)

        def copy_att(eng, copy, parity, pr, done):
            for g in range(parity, N // JB, 2):
                eng.wait_ge(turned, pr * 16 + g + 1)
                dst = att[:, bass.ds(pr, 1), :, g * JB:(g + 1) * JB].rearrange("p o m j -> p (o m) j")
                copy(dst.rearrange("p m j -> p j m"), T_[g % 4][:, :].rearrange("p (j m) -> p j m", j=JB))\
                    .then_inc(done, 1)

        @block.scalar
        def _(act):
            def copy(o, i):
                return act.activation(o, i, ACT.Copy)

            def step(pr):
                copy_scores(act, copy, 0, pr, s_by_act)
                for h in range(2):
                    for half in range(2):
                        act.wait_ge(shifted, pr * 4 + 2 * h + half + 1)
                        v = raw[:, h, half * HL:(half + 1) * HL, :]
                        act.activation(v, v, ACT.Exp, scale=SCALE).then_inc(exped, 1)
                copy_att(act, copy, 0, pr, t_by_act)

            steps(act, PAIRS, step)

        @block.vector
        def _(dve):
            def copy(o, i):
                return dve.tensor_copy(o, i)

            def step(pr):
                copy_scores(dve, copy, 1, pr, s_by_dve)
                dve.wait_ge(s_by_act, pr * NB + NB)
                dve.wait_ge(s_by_dve, pr * NB + NB)
                for h in range(2):
                    dve.tensor_reduce(mx[:, h, :], raw[:, h, :, :].rearrange("p l j -> p j l"), AX_X, ALU.max)\
                        .then_inc(maxed, 1)
                    dve.wait_ge(maxed, pr * 2 + h + 1)
                    for half in range(2):
                        v = raw[:, h, half * HL:(half + 1) * HL, :]
                        dve.tensor_tensor(v, v, mx[:, h, :].unsqueeze(1).broadcast_to((P, HL, N)), ALU.subtract)\
                            .then_inc(shifted, 1)
                for h in range(2):
                    dve.wait_ge(exped, pr * 4 + 2 * h + 2)
                    if h == 0:
                        need(dve, normed[0], pr * 2)
                    dve.tensor_reduce(rsum[:, h, :], raw[:, h, :, :].rearrange("p l j -> p j l"), AX_X, ALU.add)\
                        .then_inc(summed, 1)
                    dve.wait_ge(summed, pr * 2 + h + 1)
                    dve.reciprocal(rinv[:, h, :], rsum[:, h, :]).then_inc(inverted, 1)
                dve.wait_ge(inverted, pr * 2 + 2)
                for half in range(2):
                    v = raw[:, 1, half * HL:(half + 1) * HL, :]
                    dve.tensor_tensor(v, v, rinv[:, 1, :].unsqueeze(1).broadcast_to((P, HL, N)), ALU.mult)\
                        .then_inc(normed[1], 1)
                copy_att(dve, copy, 1, pr, t_by_dve)

            steps(dve, PAIRS, step)


def block_trilinear(nc, v_dram, att, out_dram):
    G = 16
    NG = N // G
    QI = 4
    NQ = G // QI
    HI = G // 2
    M = 2 * STRIP_D
    DD = 22
    with ExitStack() as ctx:
        t_ = Tools(nc, ctx, "tri")
        sb, sem = t_.sb, t_.sem
        bank = t_.banks(NQ)
        v2ps = ctx.enter_context(nc.psum_tensor("tri_v2ps", [P, 3 * BANK], F32))
        v1 = [sb(f"v1_{u}", [P, N, DK]) for u in range(2)]
        v2in = sb("v2in", [P, N, DK])
        v2sb = [sb(f"v2sb{u}", [P, DK - DD, N]) for u in range(2)]
        av = [sb(f"av{u}", [P, DK, N]) for u in range(2)]
        sel = [sb(f"sel{u}", [P, DK // STRIP_D, STRIP_D * M]) for u in range(4)]
        ost = [sb(f"ost{u}", [P, 2, HI * N]) for u in range(2)]
        v1_loaded, v2_loaded = sem("v1_loaded"), sem("v2_loaded")
        v2_in_sb, v2_in_ps = sem("v2_in_sb"), sem("v2_in_ps")
        sel_zeroed, sums_zeroed, sel_ready = sem("sel_zeroed"), sem("sums_zeroed"), sem("sel_ready")
        av_by_dve, av_by_pool, i_done = sem("av_by_dve"), sem("av_by_pool"), sem("i_done")
        o_copied, o_stored = sem("o_copied"), [sem(f"o_stored{u}") for u in range(2)]
        block = ctx.enter_context(nc.Block())
        attf = att[:, :, :, :].rearrange("p r m j -> p (r m j)")
        v2d = v2ps[:, 0:DD * N].rearrange("p (d j) -> p d j", d=DD)

        def groups(eng, c, body):
            first = 0
            if isinstance(c, int) and c == 0:
                body(0, 0)
                first = 1
            with eng.Fori(first, NG) as g:
                body(g, c * N + g * G)

        def combinations(eng, combo):
            combo(0, 0)
            combo(0, 1)
            with eng.Fori(1, PAIRS) as pr:
                combo(pr, 0)
                combo(pr, 1)

        @block.sync
        def _(sp):
            def load(pr, b):
                c = pr * 2 + b
                need(sp, i_done, (c - 1) * N)
                sp.dma_start(v1[b][:, :, :], v_dram[0, bass.ds(pr, 1), :, b].rearrange("o p i d -> (o p) i d"))\
                    .then_inc(v1_loaded, 16)
                need(sp, v2_in_ps, c)
                sp.dma_start(v2in[:, :, :], v_dram[1, bass.ds(pr, 1), :, b].rearrange("o p j d -> (o p) j d"))\
                    .then_inc(v2_loaded, 16)

            def store(pr, b, g):
                for u in range(2):
                    sp.wait_ge(o_copied, ((pr * 2 + b) * NG + g) * NQ + (u + 1) * (NQ // 2))
                    rows = out_dram[bass.ds(pr * (2 * DK), 2 * DK),
                                    bass.ds(g * (G * N) + (b * N * N + u * HI * N), HI * N)]
                    for s in range(STRIPS):
                        sp.dma_start(rows.rearrange("(a s r) t -> s r a t", a=2, s=STRIPS)[s],
                                     ost[u][s * 32:s * 32 + M]).then_inc(o_stored[u], 16)

            def combo(pr, b, last=False):
                store(pr, b, 0)
                if not last:
                    load(*((pr, 1) if b == 0 else (pr + 1, 0)))
                with sp.Fori(1, NG) as g:
                    store(pr, b, g)

            load(0, 0)
            combo(0, 0)
            combo(0, 1)
            with sp.Fori(1, PAIRS - 1) as pr:
                combo(pr, 0)
                combo(pr, 1)
            combo(PAIRS - 1, 0)
            combo(PAIRS - 1, 1, last=True)
            for u in range(2):
                sp.wait_ge(o_stored[u], 16 * STRIPS * B * PAIRS * NG)

        def multiply(eng, v2_ready, ready, v2_of, d0, d1):
            def combo(pr, b):
                def body(g, n):
                    eng.wait_ge(v2_ready, pr * 2 + b + 1)
                    for k in range(G):
                        need(eng, i_done, n + k - 1)
                        a = attf[:, bass.ds((n + k) * N, N)]
                        eng.tensor_tensor(av[k % 2][:, d0:d1, :], a.unsqueeze(1).broadcast_to((P, d1 - d0, N)),
                                          v2_of(b), ALU.mult).then_inc(ready, 1)

                groups(eng, pr * 2 + b, body)

            combinations(eng, combo)

        @block.gpsimd
        def _(pool):
            for u in range(4):
                pool.memset(sel[u][:, :, :], 0.0).then_inc(sel_zeroed, 1)
            multiply(pool, v2_in_sb, av_by_pool, lambda b: v2sb[b][:, :, :], DD, DK)

        @block.vector
        def _(dve):
            for q in range(NQ):
                dve.memset(bank[q][:, :], 0.0).then_inc(sums_zeroed, 1)
            multiply(dve, v2_in_ps, av_by_dve, lambda b: v2d, 0, DD)

        @block.tensor
        def _(pe):
            pe.wait_ge(sums_zeroed, NQ)

            def combo(pr, b):
                def body(g, n):
                    for k in range(G):
                        q = k // QI
                        if k % QI == 0:
                            need(pe, o_copied, ((pr * 2 + b) * NG + g) * NQ + q - NQ + 1)
                        pe.wait_ge(sel_ready, (n + k) * 2 + 2)
                        pe.wait_ge(av_by_dve, n + k + 1)
                        for a in range(2):
                            if a == 1:
                                pe.wait_ge(av_by_pool, n + k + 1)
                            col = a * (QI * N) + (k % QI) * N
                            for d4 in range(STRIP_D):
                                for s in range(STRIPS):
                                    dg = a * STRIPS + s
                                    mm = pe.matmul(bank[q][s * 32:s * 32 + M, col:col + N],
                                                   sel[k % 4][:, dg, d4 * M:(d4 + 1) * M],
                                                   av[k % 2][:, dg * STRIP_D + d4, :],
                                                   start=(d4 == 0), stop=(d4 == STRIP_D - 1))
                        mm.then_inc(i_done, 1)

                groups(pe, pr * 2 + b, body)

            combinations(pe, combo)

        @block.scalar
        def _(act):
            act.wait_ge(sel_zeroed, 4)

            def turn_v2(pr, b):
                c = pr * 2 + b
                act.wait_ge(v2_loaded, c * 16 + 16)
                need(act, av_by_pool, (c - 1) * N)
                turned = v2in[:, :, :].rearrange("p j d -> p d j")
                act.activation(v2sb[b][:, :, :], turned[:, DD:], ACT.Copy).then_inc(v2_in_sb, 1)
                need(act, av_by_dve, c * N)
                for lo in range(0, DD, BANK // N):
                    hi = min(lo + BANK // N, DD)
                    ins = act.activation(v2d[:, lo:hi], turned[:, lo:hi], ACT.Copy)
                ins.then_inc(v2_in_ps, 1)

            def copy_sums(gi, q):
                u = q // 2
                need(act, o_stored[u], gi * (16 * STRIPS))
                act.wait_ge(i_done, gi * G + (q + 1) * QI)
                lo = (q % 2) * QI * N
                act.activation(ost[u][:, :, lo:lo + QI * N], bank[q][:, :].rearrange("p (a t) -> p a t", a=2),
                               ACT.Copy).then_inc(o_copied, 1)

            def combo(pr, b, last=False):
                c = pr * 2 + b

                def body(g, n):
                    gi = c * NG + g
                    act.wait_ge(v1_loaded, c * 16 + 16)
                    for k in range(G):
                        need(act, i_done, n + k - 3)
                        for h2 in range(2):
                            r = slice(h2 * N, (h2 + 1) * N)
                            src = v1[b][r, bass.ds(g * G + k, 1), :].rearrange("p o (g f) -> p (o g) f", f=STRIP_D)
                            lo = h2 * STRIP_D
                            act.activation(sel[k % 4][r, :, lo:lo + (STRIP_D - 1) * (M + 1) + 1:M + 1], src,
                                           ACT.Copy).then_inc(sel_ready, 1)
                        if k == 2 and not (isinstance(gi, int) and gi == 0):
                            copy_sums(gi - 1, NQ - 1)
                        if k in (6, 10, 14):
                            copy_sums(gi, (k - 6) // QI)

                groups(act, c, body)
                if not last:
                    turn_v2(*((pr, 1) if b == 0 else (pr + 1, 0)))

            turn_v2(0, 0)
            combo(0, 0)
            combo(0, 1)
            with act.Fori(1, PAIRS - 1) as pr:
                combo(pr, 0)
                combo(pr, 1)
            combo(PAIRS - 1, 0)
            combo(PAIRS - 1, 1, last=True)
            copy_sums(B * PAIRS * NG - 1, NQ - 1)


def pipeline(eng, n, front, back):
    front(0, 0)
    for c in (0, 1):
        front(c + 1, (c + 1) % 2)
        back(c, c % 2)
    with eng.Fori(1, n // 2 - 1) as r:
        for u in range(2):
            front(r * 2 + (u + 1), (u + 1) % 2)
            back(r * 2 + u, u)
    front(n - 1, (n - 1) % 2)
    back(n - 2, n % 2)
    back(n - 1, (n - 1) % 2)


def block_mlp(nc, x, attn_dram, W, x1):
    with ExitStack() as ctx:
        t_ = Tools(nc, ctx, "mlp")
        sb, sem = t_.sb, t_.sem
        bank = t_.banks()
        WO_, HID_, OUT_ = bank[0:2], bank[2:6], bank[6:8]
        ident = sb("ident", [P, P])
        wo, w1, w2 = sb("wo", [P, KT, E]), sb("w1", [P, KT, F]), sb("w2", [P, FT, E])
        b1 = sb("b1", [P, FT])
        row = {n: sb(n, [P, E]) for n in ("g1", "be1", "b2", "g2", "be2")}
        eps = sb("eps", [P, 1])
        att = [sb(f"att{u}", [P, KT, CHUNK]) for u in range(2)]
        xin = [sb(f"xin{u}", [P, TT, E]) for u in range(2)]
        h = [sb(f"h{u}", [P, TT, E]) for u in range(2)]
        hb = [sb(f"hb{u}", [P, TT, E]) for u in range(2)]
        hT = [sb(f"hT{u}", [P, KT, CHUNK]) for u in range(2)]
        hid = sb("hid", [P, FT, CHUNK])
        o = [sb(f"o{u}", [P, TT, E]) for u in range(2)]
        stats = [sb(f"stats{n}", [P, TT, 6]) for n in range(2)]
        mv = [sb(f"mv{n}", [P, TT, 2]) for n in range(2)]
        std = [sb(f"std{n}", [P, TT]) for n in range(2)]
        rstd = [sb(f"rstd{n}", [P, TT]) for n in range(2)]
        ident_set, w_loaded, eps_set = sem("ident_set"), sem("w_loaded"), sem("eps_set")
        in_loaded = [sem(f"in_loaded{u}") for u in range(2)]
        wo_done, added = sem("wo_done"), sem("added")
        moments, rooted = [sem(f"moments{n}") for n in range(2)], [sem(f"rooted{n}") for n in range(2)]
        f_chain, b_chain = sem("f_chain"), sem("b_chain")
        h_ready, h_turned, hT_ready = sem("h_ready"), sem("h_turned"), sem("hT_ready")
        hid_done, hid_ready, w2_done, w2_added = sem("hid_done"), sem("hid_ready"), sem("w2_done"), sem("w2_added")
        o_ready, b2_added = sem("o_ready"), sem("b2_added")
        passed = sem("passed")
        o_stored = [sem(f"o_stored{u}") for u in range(2)]
        NW = 9
        LINKS = (4, 4)
        rows_in = x.rearrange("(c t p) e -> c p t e", t=TT, p=P)
        rows_out = x1.rearrange("(c t p) e -> c p t e", t=TT, p=P)
        attv = attn_dram.rearrange("(k p) t -> p k t", p=P)
        block = ctx.enter_context(nc.Block())

        @block.sync
        def _(sp):
            def load(c, u):
                need(sp, added, 2 * c - 2)
                sp.dma_start(att[u][:, :, :], attv[:, :, bass.ds(c * CHUNK, CHUNK)]).then_inc(in_loaded[u], 16)
                sp.dma_start(xin[u][:, :, :], rows_in[c]).then_inc(in_loaded[u], 16)
                if isinstance(c, int) and c == 0:
                    sp.dma_start(w1[:, :, :], W["W1"].rearrange("(k p) n -> p k n", p=P)).then_inc(w_loaded, 16)
                    sp.dma_start(w2[:, :, :], W["W2"].rearrange("(k p) n -> p k n", p=P)).then_inc(w_loaded, 16)
                    sp.dma_start(b1[:, :], W["b1"]).then_inc(w_loaded, 16)
                    for n, name in (("g1", "ln_agg_g"), ("be1", "ln_agg_b"), ("b2", "b2"), ("g2", "ln_out_g"),
                                    ("be2", "ln_out_b")):
                        sp.dma_start(row[n][:, :], W[name].partition_broadcast(P)).then_inc(w_loaded, 16)

            def store(c, u):
                sp.wait_ge(o_ready, c + 1)
                sp.dma_start(rows_out[c], o[u][:, :, :]).then_inc(o_stored[u], 16)

            sp.dma_start(wo[:, :, :], W["Wo"].rearrange("(k p) n -> p k n", p=P)).then_inc(w_loaded, 16)
            pipeline(sp, NCHUNK, load, store)
            for u in range(2):
                sp.wait_ge(o_stored[u], NCHUNK // 2 * 16)

        @block.gpsimd
        def _(pool):
            pool.memset(eps[:, :], EPS).then_inc(eps_set, 1)
            make_identity(pool, ident, ident_set)

        @block.tensor
        def _(pe):
            pe.wait_ge(ident_set, 2)
            pe.wait_ge(w_loaded, 16 * NW)

            def times_wo(c, u):
                pe.wait_ge(in_loaded[u], (c // 2) * 32 + 32)
                need(pe, hT_ready, 2 * c)
                for t in range(TT):
                    for k in range(KT):
                        mm = pe.matmul(WO_[t // 2][:, (t % 2) * E:(t % 2 + 1) * E], att[u][:, k, t * P:(t + 1) * P],
                                       wo[:, k, :], start=(k == 0), stop=(k == KT - 1))
                    if t % 2:
                        mm.then_inc(wo_done, 1)

            def turn_h(c, u):
                pe.wait_ge(h_ready, c + 1)
                for k in range(KT):
                    for t in range(TT):
                        mm = pe.transpose(WO_[k][:, t * P:(t + 1) * P], h[u][:, t, k * P:(k + 1) * P], ident[:, :])
                    mm.then_inc(h_turned, 1)

            def mlp(c, u):
                pe.wait_ge(hT_ready, 2 * c + 2)
                for m in range(FT):
                    need(pe, hid_ready, FT * (c - 1) + m + 1)
                    for k in range(KT):
                        mm = pe.matmul(HID_[m][:, :], w1[:, k, m * P:(m + 1) * P], hT[u][:, k, :],
                                       start=(k == 0), stop=(k == KT - 1))
                    mm.then_inc(hid_done, 1)
                pe.wait_ge(hid_ready, FT * c + FT)
                need(pe, w2_added, 2 * c)
                for t in range(TT):
                    for k in range(FT):
                        mm = pe.matmul(OUT_[t // 2][:, (t % 2) * E:(t % 2 + 1) * E], hid[:, k, t * P:(t + 1) * P],
                                       w2[:, k, :], start=(k == 0), stop=(k == FT - 1))
                    if t % 2:
                        mm.then_inc(w2_done, 1)

            times_wo(0, 0)
            turn_h(0, 0)

            def step(c, u):
                times_wo(c + 1, 1 - u)
                mlp(c, u)
                turn_h(c + 1, 1 - u)

            step(0, 0)
            step(1, 1)
            with pe.Fori(1, NCHUNK // 2 - 1) as r:
                step(r * 2, 0)
                step(r * 2 + 1, 1)
            step(NCHUNK - 2, 0)
            mlp(NCHUNK - 1, 1)

        @block.scalar
        def _(act):
            act.wait_ge(eps_set, 1)
            act.wait_ge(w_loaded, 16 * NW)

            def root(n, c):
                act.wait_ge(moments[n], c + 1)
                act.activation(std[n][:, :], mv[n][:, :, 1], ACT.Sqrt, bias=eps[:, :]).then_inc(rooted[n], 1)

            def copy_hT(c, u):
                for k in range(KT):
                    act.wait_ge(h_turned, 2 * c + k + 1)
                    act.activation(hT[u][:, k, :], WO_[k][:, :], ACT.Copy).then_inc(hT_ready, 1)

            def relu(c, u):
                need(act, w2_done, 2 * c)
                for m in range(FT):
                    act.wait_ge(hid_done, FT * c + m + 1)
                    act.activation(hid[:, m, :], HID_[m][:, :], ACT.Relu, bias=b1[:, m:m + 1]).then_inc(hid_ready, 1)

            root(0, 0)
            copy_hT(0, 0)

            def step(c, u):
                relu(c, u)
                root(0, c + 1)
                copy_hT(c + 1, 1 - u)
                root(1, c)

            step(0, 0)
            step(1, 1)
            with act.Fori(1, NCHUNK // 2 - 1) as r:
                step(r * 2, 0)
                step(r * 2 + 1, 1)
            step(NCHUNK - 2, 0)
            relu(NCHUNK - 1, 1)
            root(1, NCHUNK - 1)

        @block.vector
        def _(dve):
            dve.wait_ge(w_loaded, 16 * NW)

            def wide(v):
                return v[:, :].unsqueeze(1).broadcast_to((P, TT, E))

            def layer_norm(n, c, chain, v, out, gain, bias, done):
                for t in range(TT):
                    ins = dve.bn_stats(stats[n][:, t, :], v[:, t, :])
                chain.mark(ins)
                need_apart(dve, passed, (f_chain if n == 0 else b_chain, chain.value()))
                for t in range(TT):
                    ins = dve.bn_aggr(mv[n][:, t, :], stats[n][:, t, :])
                ins.then_inc(moments[n], 1)
                dve.wait_ge(moments[n], c + 1)
                dve.wait_ge(rooted[n], c + 1)
                chain.link(dve.reciprocal(rstd[n][:, :], std[n][:, :]))
                for t in range(TT):
                    ins = dve.tensor_scalar(out[:, t, :], v[:, t, :], mv[n][:, t, 0:1], rstd[n][:, t:t + 1],
                                            ALU.subtract, ALU.mult)
                chain.link(ins)
                chain.link(dve.tensor_tensor(out[:, :, :], out[:, :, :], wide(gain), ALU.mult))
                dve.tensor_tensor(out[:, :, :], out[:, :, :], wide(bias), ALU.add).then_inc(done, 1)

            def front(c, u):
                chain = Chain(dve, f_chain, c * LINKS[0])
                dve.wait_ge(in_loaded[u], (c // 2) * 32 + 32)
                need(dve, h_turned, 2 * c - 2)
                for half in range(2):
                    dve.wait_ge(wo_done, 2 * c + half + 1)
                    s = slice(2 * half, 2 * half + 2)
                    dve.tensor_tensor(h[u][:, s, :], WO_[half][:, :].rearrange("p (t e) -> p t e", t=2),
                                      xin[u][:, s, :], ALU.add).then_inc(added, 1)
                dve.wait_ge(added, 2 * c + 2)
                layer_norm(0, c, chain, h[u], h[u], row["g1"], row["be1"], h_ready)
                dve.wait_ge(h_ready, c + 1)

            def back(c, u):
                chain = Chain(dve, b_chain, c * LINKS[1])
                dve.tensor_tensor(hb[u][:, :, :], h[u][:, :, :], wide(row["b2"]), ALU.add).then_inc(b2_added, 1)
                dve.wait_ge(b2_added, c + 1)
                for half in range(2):
                    dve.wait_ge(w2_done, 2 * c + half + 1)
                    s = slice(2 * half, 2 * half + 2)
                    dve.tensor_tensor(hb[u][:, s, :], OUT_[half][:, :].rearrange("p (t e) -> p t e", t=2),
                                      hb[u][:, s, :], ALU.add).then_inc(w2_added, 1)
                dve.wait_ge(w2_added, 2 * c + 2)
                need(dve, o_stored[u], (c // 2) * 16)
                layer_norm(1, c, chain, hb[u], o[u], row["g2"], row["be2"], o_ready)

            pipeline(dve, NCHUNK, front, back)


def block_mamba(nc, W, x1, out, prev, cols):
    with ExitStack() as ctx:
        t_ = Tools(nc, ctx, "mv" if cols else "mh")
        sb, sem = t_.sb, t_.sem
        bank = t_.banks()
        XT_ = bank[0:2]
        PR_ = bank[2:5]
        G_ = bank[5]
        Y0_ = bank[6:8]
        PAIR = SEQS // 2
        ident, ones_blk = sb("ident", [P, P]), sb("ones_blk", [P, P])
        diag, diag0 = sb("diag", [P, L]), sb("diag0", [P, L])
        ones = sb("ones", [P, 1])
        eps = sb("eps", [P, 1])
        win = sb("win", [P, KT, DPROJ])
        wf = sb("wf", [P, CT, E])
        out_w, fcw = sb("out_w", [P, KT, DI]), sb("fcw", [P, 2 * KT, E])
        cw, cb = sb("cw", [P, CT + 1, TAPS]), sb("cb", [P, CT + 1])
        dskip, normw = sb("dskip", [P, CT]), sb("normw", [P, CT])
        dtb, nega, bias = sb("dtb", [P, NH]), sb("nega", [P, NH]), sb("bias", [P, E])
        xin = [sb(f"xin{u}", [P, TT, E]) for u in range(2)]
        pv = [sb(f"pv{u}", [P, TT, E]) for u in range(2)] if cols else None
        ot = [sb(f"ot{u}", [P, TT, E]) for u in range(2)]
        xT = sb("xT", [P, KT, CHUNK])
        xp = sb("xp", [P, CT + 1, SEQS, L + TAPS - 1])
        cv = sb("cv", [P, CT + 1, CHUNK])
        xc = [sb(f"xc{u}", [P, CT, CHUNK]) for u in range(2)]
        bc = [sb(f"bc{u}", [DS, 2, CHUNK]) for u in range(2)]
        zs = [sb(f"zs{u}", [P, CT, CHUNK]) for u in range(2)]
        small = {n: sb(n, [P, TT, NH]) for n in ("x_dt", "absx", "e", "u", "iz", "den", "rden", "num", "num2", "lp",
                                                 "dt", "prod", "dA")}
        lnu = sb("lnu", [P, TT, NH])
        xtok = sb("xtok", [P, PAIR, DI])
        spread = sb("spread", [P, PAIR, NH, L])
        inj = sb("inj", [P, PAIR, NH, L])
        decay = [sb(f"decay{u}", [P, NH * L]) for u in range(2)]
        S = sb("S", [P, PAIR, NH, L])
        y, sq = sb("y", [P, CT, CHUNK]), sb("sq", [P, CT, CHUNK])
        ssr = sb("ssr", [1, CHUNK])
        lnss, rstd = sb("lnss", [P, TT]), sb("rstd", [P, TT])

        const_set, w_loaded, folded, wf_ready = sem("const_set"), sem("w_loaded"), sem("folded"), sem("wf_ready")
        fc_summed, nega_chain, xp_zeroed = sem("fc_summed"), sem("nega_chain"), sem("xp_zeroed")
        in_loaded = [sem(f"in_loaded{u}") for u in range(2)]
        turned, xT_copied, proj_done, proj_by_act = sem("turned"), sem("xT_copied"), sem("proj_done"), sem("proj_by_act")
        dt_read, conv_chain, conv_done, silued = sem("dt_read"), sem("conv_chain"), sem("conv_done"), sem("silued")
        absx_ready, e_ready, u_ready, ln_ready = sem("absx_ready"), sem("e_ready"), sem("u_ready"), sem("ln_ready")
        dt_chain, prod_ready, dA_ready = sem("dt_chain"), sem("prod_ready"), sem("dA_ready")
        xtok_done, xtok_copied, g_done = sem("xtok_done"), sem("xtok_copied"), sem("g_done")
        spread_ready, inj_ready = sem("spread_ready"), sem("inj_ready")
        da_done, scanned, s_ready = sem("da_done"), sem("scanned"), sem("s_ready")
        y_done, y_read, gated, squared = sem("y_done"), sem("y_read"), sem("gated"), sem("squared")
        ss_done, ss_copied, col_done, col_read, rstd_ready = (sem("ss_done"), sem("ss_copied"), sem("col_done"),
                                                              sem("col_read"), sem("rstd_ready"))
        out_done, out_read, passed = sem("out_done"), sem("out_read"), sem("passed")
        o_stored = [sem(f"o_stored{u}") for u in range(2)]
        NACT = 2 * CT + 1
        NW = 9 + (0 if cols else 1)
        PER_IN = 16 if not cols else 2 * 4 * 16
        PER_OUT = 16 if not cols else 4 * 16

        rows = {n: a.rearrange("(c t p) e -> c p t e", t=TT, p=P) for n, a in (("x", x1), ("o", out))}
        grid = {n: a.rearrange("(b h c t q) e -> b q h c t e", b=B, h=N, t=2, q=2)
                for n, a in (("x", x1), ("o", out), ("p", prev if cols else x1))}
        block = ctx.enter_context(nc.Block())

        def stages(eng, A, Bs, C):
            Bs(0, 0)
            for c in (0, 1):
                A(c, c % 2)
                Bs(c + 1, (c + 1) % 2)
                C(c, c % 2, False)
            with eng.Fori(1, NCHUNK // 2 - 1) as r:
                for u in range(2):
                    A(r * 2 + u, u)
                    Bs(r * 2 + (u + 1), (u + 1) % 2)
                    C(r * 2 + u, u, False)
            c = NCHUNK - 2
            A(c, 0)
            Bs(c + 1, 1)
            C(c, 0, False)
            A(c + 1, 1)
            C(c + 1, 1, True)

        def nothing(*_):
            pass

        @block.sync
        def _(sp):
            def move(name, c, tile, to_dram, done):
                if not cols:
                    a, b = tile[:, :, :], rows[name][c]
                    sp.dma_start(*((b, a) if to_dram else (a, b))).then_inc(done, 16)
                    return
                for b in range(B):
                    for q in range(2):
                        a = tile[q * L:(q + 1) * L, 2 * b:2 * b + 2, :]
                        d = grid[name][b, q, :, c]
                        sp.dma_start(*((d, a) if to_dram else (a, d))).then_inc(done, 16)

            def load(c, u):
                need(sp, turned, 2 * c - 2)
                move("x", c, xin[u], False, in_loaded[u])
                if cols:
                    need(sp, out_read, TT * (c - 1))
                    move("p", c, pv[u], False, in_loaded[u])

            def store(c, u, last):
                sp.wait_ge(out_read, TT * c + TT)
                move("o", c, ot[u], True, o_stored[u])

            sp.dma_start(win[:, :, :], W["in_wT"].rearrange("(k p) n -> p k n", p=P)).then_inc(w_loaded, 16)
            for tile, name in ((cw, "conv_w"), (cb, "conv_b"), (dskip, "D"), (normw, "norm_w")):
                sp.dma_start(tile[:], W[name]).then_inc(w_loaded, 16)
            sp.dma_start(dtb[:, :], W["dt_bias"].partition_broadcast(P)).then_inc(w_loaded, 16)
            sp.dma_start(nega[:, :], W["A_log"].partition_broadcast(P)).then_inc(w_loaded, 16)
            sp.dma_start(out_w[:, :, :], W["out_w"].rearrange("(k p) n -> p k n", p=P)).then_inc(w_loaded, 16)
            sp.dma_start(fcw[:, :, :], W["fc_wT"].rearrange("(k p) n -> p k n", p=P)).then_inc(w_loaded, 16)
            if not cols:
                sp.dma_start(bias[:, :], W["fc_b"].partition_broadcast(P)).then_inc(w_loaded, 16)
            stages(sp, nothing, load, store)
            for u in range(2):
                sp.wait_ge(o_stored[u], NCHUNK // 2 * PER_OUT)

        @block.gpsimd
        def _(pool):
            make_identity(pool, ident, const_set)
            pool.memset(ones[:, :], 1.0).then_inc(const_set, 1)
            pool.memset(eps[:, :], EPS).then_inc(const_set, 1)
            pool.memset(xp[:, :, :, :], 0.0).then_inc(xp_zeroed, 1)
            pool.memset(ones_blk[:, :], 0.0).then_inc(const_set, 1)
            pool.wait_ge(const_set, 5)
            for q in range(2):
                r = slice(q * L, (q + 1) * L)
                pool.memset(ones_blk[r, r], 1.0).then_inc(const_set, 1)
                pool.tensor_copy(diag[r, :], ident[r, r]).then_inc(const_set, 1)
                pool.tensor_copy(diag0[r, :], ident[r, r]).then_inc(const_set, 1)
            pool.wait_ge(const_set, 11)
            pool.memset(diag0[:, 0:1], 0.0).then_inc(const_set, 1)
            pool.wait_ge(const_set, 12)

            def A(c, u):
                pool.wait_ge(dA_ready, c + 1)
                for p in range(PAIR):
                    need(pool, da_done, PAIR * (c - 1) + p + 1)
                    pool.tensor_tensor(spread[:, p], diag0[:, :].unsqueeze(1).broadcast_to((P, NH, L)),
                                       small["dA"][:, p, :].unsqueeze(2).broadcast_to((P, NH, L)), ALU.mult)\
                        .then_inc(spread_ready, 1)
                    need(pool, scanned, PAIR * (c - 1) + p + 1)
                    pool.tensor_tensor(inj[:, p], diag[:, :].unsqueeze(1).broadcast_to((P, NH, L)),
                                       small["dt"][:, p, :].unsqueeze(2).broadcast_to((P, NH, L)), ALU.mult)\
                        .then_inc(inj_ready, 1)

            stages(pool, A, nothing, nothing)

        @block.tensor
        def _(pe):
            pe.wait_ge(const_set, 12)
            pe.wait_ge(w_loaded, 16 * NW)
            pe.wait_ge(fc_summed, 1)
            for m in range(CT):
                for k in range(KT):
                    mm = pe.matmul(bank[m][:, 0:E], out_w[:, k, m * P:(m + 1) * P], fcw[:, k, :],
                                   start=(k == 0), stop=(k == KT - 1))
                mm.then_inc(folded, 1)
            pe.wait_ge(wf_ready, CT)

            def A(c, u):
                pe.wait_ge(silued, 6 * c + 6)
                for s in range(SEQS):
                    if s == 0:
                        need_apart(pe, passed, (ss_copied, c))
                    mm = pe.matmul(G_[(s % 2) * L:(s % 2 + 1) * L, (s // 2) * L:(s // 2 + 1) * L],
                                   bc[u][:, 0, s * L:(s + 1) * L], bc[u][:, 1, s * L:(s + 1) * L],
                                   start=True, stop=True)
                mm.then_inc(g_done, 1)
                for p in range(PAIR):
                    if p < 2:
                        need(pe, out_read, TT * (c - 1) + 2 * p + 2)
                    else:
                        pe.wait_ge(scanned, PAIR * c + p - 1)
                    pe.wait_ge(spread_ready, PAIR * c + p + 1)
                    pe.matmul(PR_[p % 2][:, :], ones_blk[:, :], spread[:, p].rearrange("p h t -> p (h t)"),
                              start=True, stop=True).then_inc(da_done, 1)
                for p in range(PAIR):
                    if p < 2:
                        need(pe, y_read, 4 * (c - 1) + p + 3)
                    else:
                        pe.wait_ge(xtok_copied, PAIR * c + p - 1)
                    for m in range(CT):
                        mm = pe.transpose(XT_[p % 2][:, m * P:(m + 1) * P], xc[u][:, m, p * P:(p + 1) * P],
                                          ident[:, :])
                    mm.then_inc(xtok_done, 1)

            def Bs(c, u):
                pe.wait_ge(in_loaded[u], (c // 2) * PER_IN + PER_IN)
                for k in range(KT):
                    need(pe, xtok_copied, PAIR * (c - 1) + 3 + k)
                    for t in range(TT):
                        mm = pe.transpose(XT_[k][:, t * P:(t + 1) * P], xin[u][:, t, k * P:(k + 1) * P], ident[:, :])
                    mm.then_inc(turned, 1)
                pe.wait_ge(xT_copied, 2 * c + 2)
                need(pe, scanned, PAIR * c)
                need(pe, col_read, c - 1)
                for j in range(2 * CT + 2):
                    if j == 8:
                        pe.wait_ge(dt_read, c + 1)
                    elif j >= 3:
                        pe.wait_ge(proj_by_act, NACT * c + (j - 2 if j < 8 else j - 3))
                    if j == CT + 1:
                        for t in range(TT):
                            for k in range(KT):
                                mm = pe.matmul(PR_[j % 3][:, t * NH:(t + 1) * NH], xT[:, k, t * P:(t + 1) * P],
                                               win[:, k, DT0:DPROJ], start=(k == 0), stop=(k == KT - 1))
                    else:
                        col = XB0 + j * P if j <= CT else (j - CT - 2) * P
                        for k in range(KT):
                            mm = pe.matmul(PR_[j % 3][:, :], win[:, k, col:col + P], xT[:, k, :],
                                           start=(k == 0), stop=(k == KT - 1))
                    mm.then_inc(proj_done, 1)

            def C(c, u, last):
                for half in range(2):
                    for q in range(2):
                        if half == 0 and q == 0:
                            pe.wait_ge(xtok_copied, PAIR * c + PAIR)
                            pe.wait_ge(s_ready, PAIR * c + PAIR)
                        if half == 0:
                            need_apart(pe, passed, (y_read, 4 * (c - 1) + q + 1))
                        elif not last:
                            need_apart(pe, passed, (xT_copied, 2 * c + 3 + q))
                        r = slice(q * L, (q + 1) * L)
                        for hp in range(2):
                            for p in range(PAIR):
                                for h2 in range(2):
                                    h = 4 * half + 2 * hp + h2
                                    col = (hp * PAIR + p) * L
                                    mm = pe.matmul((Y0_, XT_)[half][q][h2 * HD:(h2 + 1) * HD, col:col + L],
                                                   xtok[r, p, h * HD:(h + 1) * HD], S[r, p, h, :],
                                                   start=True, stop=True)
                        mm.then_inc(y_done, 1)
                pe.wait_ge(proj_by_act, NACT * (c + (1 if last else 2)))
                for m in range(CT):
                    if m % 2 == 0:
                        pe.wait_ge(squared, 2 * c + m // 2 + 1)
                    mm = pe.matmul(G_[0:1, :], ones[:, :], sq[:, m, :], start=(m == 0), stop=(m == CT - 1))
                mm.then_inc(ss_done, 1)
                for t in range(TT):
                    for m in range(CT):
                        mm = pe.matmul(PR_[t // 2][:, (t % 2) * E:(t % 2 + 1) * E], y[:, m, t * P:(t + 1) * P],
                                       wf[:, m, :], start=(m == 0), stop=(m == CT - 1))
                    if t % 2:
                        mm.then_inc(out_done, 1)
                    if t == 1:
                        pe.wait_ge(ss_copied, c + 1)
                        for tt in range(TT):
                            mm = pe.matmul(PR_[2][:, tt:tt + 1], ssr[0:1, tt * P:(tt + 1) * P], ones[0:1, :],
                                           start=True, stop=True)
                        mm.then_inc(col_done, 1)

            stages(pe, A, Bs, C)

        @block.scalar
        def _(act):
            act.wait_ge(w_loaded, 16 * NW)
            act.wait_ge(const_set, 12)
            act.wait_ge(nega_chain, 1)
            act.activation(nega[:, :], nega[:, :], ACT.Exp).then_inc(nega_chain, 1)

            def A(c, u):
                need(act, y_done, 4 * c)
                for p in range(PAIR):
                    act.wait_ge(xtok_done, PAIR * c + p + 1)
                    act.activation(xtok[:, p, :], XT_[p % 2][:, :], ACT.Copy).then_inc(xtok_copied, 1)

            def Bs(c, u):
                for k in range(KT):
                    act.wait_ge(turned, 2 * c + k + 1)
                    act.activation(xT[:, k, :], XT_[k][:, :], ACT.Copy).then_inc(xT_copied, 1)
                if isinstance(c, int) and c == 0:
                    act.wait_ge(xp_zeroed, 1)
                need(act, conv_done, (CT + 1) * c)
                for j in range(CT + 1):
                    act.wait_ge(proj_done, (2 * CT + 2) * c + j + 1)
                    act.activation(xp[:, j, :, TAPS - 1:], PR_[j % 3][:, :].rearrange("p (s t) -> p s t", s=SEQS),
                                   ACT.Copy).then_inc(proj_by_act, 1)
                need(act, gated, 2 * (c - 1))
                for m in range(CT):
                    j = CT + 2 + m
                    act.wait_ge(proj_done, (2 * CT + 2) * c + j + 1)
                    act.activation(zs[u][:, m, :], PR_[j % 3][:, :], ACT.Silu).then_inc(proj_by_act, 1)
                need(act, y_read, 4 * (c - 1))
                need(act, g_done, c - 1)
                for m in range(CT):
                    act.wait_ge(conv_done, (CT + 1) * c + m + 1)
                    act.activation(xc[u][:, m, :], cv[:, m, :], ACT.Silu, bias=cb[:, m:m + 1]).then_inc(silued, 1)
                act.wait_ge(conv_done, (CT + 1) * c + CT + 1)
                for n in range(2):
                    r = slice(n * DS, (n + 1) * DS)
                    act.activation(bc[u][:, n, :], cv[r, CT, :], ACT.Silu, bias=cb[r, CT:CT + 1]).then_inc(silued, 1)
                act.wait_ge(absx_ready, c + 1)
                act.activation(small["e"][:, :, :], small["absx"][:, :, :], ACT.Exp, scale=-1.0).then_inc(e_ready, 1)
                if isinstance(c, int) and c == 0:
                    softplus(0)

            def softplus(c):
                act.wait_ge(u_ready, c + 1)
                act.activation(lnu[:, :, :], small["u"][:, :, :], ACT.Ln).then_inc(ln_ready, 1)
                act.wait_ge(prod_ready, c + 1)
                need(act, spread_ready, PAIR * c)
                act.activation(small["dA"][:, :, :], small["prod"][:, :, :], ACT.Exp).then_inc(dA_ready, 1)

            def C(c, u, last):
                need(act, ss_done, c)
                for half in range(2):
                    act.wait_ge(gated, 2 * c + half + 1)
                    s = slice(2 * half, 2 * half + 2)
                    act.activation(sq[:, s, :], y[:, s, :], ACT.Square).then_inc(squared, 1)
                if not last:
                    softplus(c + 1)
                act.wait_ge(ss_done, c + 1)
                act.activation(ssr[:, :], G_[0:1, :], ACT.Copy).then_inc(ss_copied, 1)
                act.wait_ge(col_done, c + 1)
                act.activation(lnss[:, :], PR_[2][:, 0:TT], ACT.Ln, scale=1.0 / DI, bias=eps[:, :])\
                    .then_inc(col_read, 1)
                act.wait_ge(col_read, c + 1)
                need(act, out_read, TT * c)
                act.activation(rstd[:, :], lnss[:, :], ACT.Exp, scale=-0.5).then_inc(rstd_ready, 1)

            stages(act, A, Bs, C)

        @block.vector
        def _(dve):
            dve.wait_ge(w_loaded, 16 * NW)
            dve.tensor_scalar(nega[:, :], nega[:, :], A_LOG_MAX, None, ALU.min).then_inc(nega_chain, 1)
            dve.tensor_tensor(fcw[:, 0:KT, :], fcw[:, 0:KT, :], fcw[:, KT:, :], ALU.add).then_inc(fc_summed, 1)
            for m in range(CT):
                dve.wait_ge(folded, m + 1)
                dve.tensor_scalar(wf[:, m, :], bank[m][:, 0:E], normw[:, m:m + 1], None, ALU.mult)\
                    .then_inc(wf_ready, 1)
            dve.wait_ge(nega_chain, 2)
            dve.tensor_scalar(nega[:, :], nega[:, :], -1.0, None, ALU.mult).then_inc(nega_chain, 1)
            dve.wait_ge(nega_chain, 3)

            def A(c, u):
                def scan(p):
                    dve.wait_ge(da_done, PAIR * c + p + 1)
                    dve.wait_ge(inj_ready, PAIR * c + p + 1)
                    dve.tensor_tensor_scan(decay[p % 2][:, :], PR_[p % 2][:, :],
                                           inj[:, p].rearrange("p h t -> p (h t)"), 0.0, ALU.mult, ALU.add)\
                        .then_inc(scanned, 1)

                def times_g(p):
                    dve.wait_ge(scanned, PAIR * c + p + 1)
                    dve.tensor_tensor(S[:, p], decay[p % 2][:, :].rearrange("p (h t) -> p h t", h=NH),
                                      G_[:, p * L:(p + 1) * L].unsqueeze(1).broadcast_to((P, NH, L)), ALU.mult)\
                        .then_inc(s_ready, 1)

                need(dve, s_ready, PAIR * c)
                scan(0)
                scan(1)
                dve.wait_ge(g_done, c + 1)
                need(dve, y_done, 4 * c)
                for p in range(PAIR):
                    times_g(p)
                    if p + 2 < PAIR:
                        dve.wait_ge(s_ready, PAIR * c + p + 1)
                        scan(p + 2)

            def Bs(c, u):
                chain = Chain(dve, conv_chain, (TAPS - 1) * c)
                need(dve, silued, 6 * c)
                for k in range(TAPS):
                    for m in range(CT + 1):
                        if k == 0:
                            dve.wait_ge(proj_by_act, NACT * c + m + 1)
                        src = xp[:, m, :, k:k + L]
                        dst = cv[:, m, :].rearrange("p (s t) -> p s t", s=SEQS)
                        if k == 0:
                            ins = dve.tensor_scalar(dst, src, cw[:, m, 0:1], None, ALU.mult)
                        else:
                            ins = dve.scalar_tensor_tensor(out=dst, in0=src, scalar=cw[:, m, k:k + 1], in1=dst,
                                                           op0=ALU.mult, op1=ALU.add)
                        if k == TAPS - 1:
                            ins.then_inc(conv_done, 1)
                    if k < TAPS - 1:
                        chain.link(ins)
                dve.wait_ge(proj_done, (2 * CT + 2) * c + CT + 2)
                need(dve, dt_chain, DT_LINKS * c)
                dve.tensor_tensor(small["x_dt"][:, :, :], PR_[(CT + 1) % 3][:, 0:TT * NH]
                                  .rearrange("p (t h) -> p t h", t=TT),
                                  dtb[:, :].unsqueeze(1).broadcast_to((P, TT, NH)), ALU.add).then_inc(dt_read, 1)
                dve.wait_ge(dt_read, c + 1)
                dve.scalar_tensor_tensor(out=small["absx"][:, :, :], in0=small["x_dt"][:, :, :], scalar=-1.0,
                                         in1=small["x_dt"][:, :, :], op0=ALU.mult, op1=ALU.max)\
                    .then_inc(absx_ready, 1)
                if isinstance(c, int) and c == 0:
                    softplus(0)

            DT_LINKS = 7

            def softplus(c):
                s = {n: v[:, :, :] for n, v in small.items()}
                chain = Chain(dve, dt_chain, DT_LINKS * c)
                dve.wait_ge(e_ready, c + 1)
                need(dve, inj_ready, PAIR * c)
                dve.tensor_scalar(s["u"], s["e"], 1.0, None, ALU.add).then_inc(u_ready, 1)
                dve.wait_ge(u_ready, c + 1)
                chain.link(dve.tensor_scalar(s["iz"], s["u"], 1.0, None, ALU.is_equal))
                chain.link(dve.scalar_tensor_tensor(out=s["den"], in0=s["u"], scalar=-1.0, in1=s["iz"],
                                                    op0=ALU.add, op1=ALU.add))
                chain.link(dve.reciprocal(s["rden"], s["den"]))
                dve.wait_ge(ln_ready, c + 1)
                chain.link(dve.tensor_tensor(s["num"], lnu[:, :, :], s["iz"], ALU.add))
                chain.link(dve.tensor_tensor(s["num2"], s["num"], s["e"], ALU.mult))
                chain.link(dve.tensor_tensor(s["lp"], s["num2"], s["rden"], ALU.mult))
                chain.link(dve.scalar_tensor_tensor(out=s["dt"], in0=s["x_dt"], scalar=0.0, in1=s["lp"],
                                                    op0=ALU.max, op1=ALU.add))
                dve.tensor_tensor(s["prod"], s["dt"], nega[:, :].unsqueeze(1).broadcast_to((P, TT, NH)), ALU.mult)\
                    .then_inc(prod_ready, 1)

            def C(c, u, last):
                need(dve, out_done, 2 * c)
                need(dve, squared, 2 * c)
                for half in range(2):
                    for q in range(2):
                        dve.wait_ge(y_done, 4 * c + 2 * half + q + 1)
                        for hp in range(2):
                            m = 2 * half + hp
                            pq = "p (a q t) -> p q a t"
                            ins = dve.scalar_tensor_tensor(
                                out=y[:, m, :].rearrange(pq, q=2, t=L)[:, q],
                                in0=xc[u][:, m, :].rearrange(pq, q=2, t=L)[:, q], scalar=dskip[:, m:m + 1],
                                in1=(Y0_, XT_)[half][q][:, hp * PAIR * L:(hp + 1) * PAIR * L]
                                .rearrange("p (a t) -> p a t", t=L), op0=ALU.mult, op1=ALU.add)
                        ins.then_inc(y_read, 1)
                for half in range(2):
                    dve.wait_ge(y_read, 4 * c + 2 * half + 2)
                    s = slice(2 * half, 2 * half + 2)
                    dve.tensor_tensor(y[:, s, :], y[:, s, :], zs[u][:, s, :], ALU.mult).then_inc(gated, 1)
                if not last:
                    softplus(c + 1)
                dve.wait_ge(rstd_ready, c + 1)
                need(dve, o_stored[u], (c // 2) * PER_OUT)
                for t in range(TT):
                    dve.wait_ge(out_done, 2 * c + t // 2 + 1)
                    dve.scalar_tensor_tensor(out=ot[u][:, t, :], in0=PR_[t // 2][:, (t % 2) * E:(t % 2 + 1) * E],
                                             scalar=rstd[:, t:t + 1], in1=pv[u][:, t, :] if cols else bias[:, :],
                                             op0=ALU.mult, op1=ALU.add).then_inc(out_read, 1)

            stages(dve, A, Bs, C)


def build(nc, T, out):
    def scratch(name, shape):
        return nc.dram_tensor(name, shape, F32, kind="Internal").ap()

    qk = scratch("qk_t", (2, E, TOK))
    v = scratch("v_pairs", (2, PAIRS, P, B, N, DK))
    mixed = scratch("mixed_t", (E, TOK))
    x1 = scratch("x1", (TOK, E))
    by_rows = scratch("by_rows", (TOK, E))
    with nc.cleanup_on_exit():
        block_projections(nc, T["x"], T, qk, v)
        with nc.sbuf_tensor("att", [P, PAIRS, B * N, N], F32) as att:
            block_softmax(nc, qk, att)
            block_trilinear(nc, v, att, mixed)
        block_mlp(nc, T["x"], mixed, T, x1)
    W = {d: {n[3:]: a for n, a in T.items() if n.startswith(d + "_")} for d in ("mh", "mv")}
    W["mh"]["fc_b"] = T["fc_b"]
    block_mamba(nc, W["mh"], x1, by_rows, None, cols=False)
    block_mamba(nc, W["mv"], x1, out, by_rows, cols=True)


def kernel(**inputs):
    import numpy as np
    import concourse.bacc as bacc
    from concourse.bass_utils import run_bass_kernel_spmd

    a = {k: np.asarray(v) for k, v in inputs.items()}

    def col(v):
        return np.ascontiguousarray(v.reshape(-1, P).T)

    def by_head_of_pair(w):
        return np.ascontiguousarray(w.reshape(E, PAIRS, 2, DK).transpose(0, 2, 1, 3).reshape(E, E))

    def rows_of_mixed(w):
        return np.ascontiguousarray(w.reshape(PAIRS, 2, 2, STRIPS, STRIP_D, E).transpose(0, 2, 3, 1, 4, 5)
                                    .reshape(E, E))

    arrays = {"x": np.ascontiguousarray(a["x"].reshape(TOK, E)), "fc_b": a["L1_conv_fc_b"]}
    arrays["Wo"] = rows_of_mixed(a["L0_conv_Wo"])
    for n in ("Wq", "Wk", "W1", "W2", "b2", "ln_agg_g", "ln_agg_b", "ln_out_g", "ln_out_b"):
        arrays[n] = a["L0_conv_" + n]
    for n in ("Wv1", "Wv2"):
        arrays[n] = by_head_of_pair(a["L0_conv_" + n])
    arrays["b1"] = col(a["L0_conv_b1"])
    fc_wT = np.ascontiguousarray(a["L1_conv_fc_w"].T)
    for d, blocks in (("mv", slice(0, 2 * E)), ("mh", slice(2 * E, 4 * E))):
        g = {n: a[f"L1_conv_{d}_{n}"] for n in ("in_w", "conv_w", "conv_b", "dt_bias", "A_log", "D", "norm_w", "out_w")}
        arrays[d + "_in_wT"] = np.ascontiguousarray(g["in_w"].T)
        arrays[d + "_conv_w"] = np.ascontiguousarray(g["conv_w"].reshape(CT + 1, P, TAPS).transpose(1, 0, 2))
        arrays[d + "_conv_b"] = col(g["conv_b"])
        arrays[d + "_D"] = col(np.repeat(g["D"], HD))
        arrays[d + "_norm_w"] = col(g["norm_w"])
        arrays[d + "_dt_bias"], arrays[d + "_A_log"], arrays[d + "_out_w"] = g["dt_bias"], g["A_log"], g["out_w"]
        arrays[d + "_fc_wT"] = np.ascontiguousarray(fc_wT[blocks])
    nc = bacc.Bacc("TRN2", target_bir_lowering=False, num_devices=1)
    T = {n: nc.dram_tensor("in_" + n, v.shape, mybir.dt.from_np(v.dtype), kind="ExternalInput").ap()
         for n, v in arrays.items()}
    out = nc.dram_tensor("out", (TOK, E), F32, kind="ExternalOutput").ap()
    build(nc, T, out)
    r = run_bass_kernel_spmd(nc, [{"in_" + n: v for n, v in arrays.items()}], core_ids=[0])
    return r.results[0]["out"].reshape(B, N, N, E)
```

```python
from contextlib import ExitStack

import concourse.bass as bass
from concourse import mybir

F32 = mybir.dt.float32
ALU = mybir.AluOpType
ACT = mybir.ActivationFunctionType
AX_X = mybir.AxisListType.X

P = 128
BANK = 512
B, N, E = 2, 64, 256
H = 8
DK = E // H
PAIRS = H // 2
TOK = B * N * N
KT = E // P
F = 2 * E
FT = F // P
STRIPS = 4
STRIP_D = DK // (2 * STRIPS)
EPS = 1e-5
SCALE = DK ** -0.5

DI = 2 * E
DS = 64
NH = 8
HD = DI // NH
CT = DI // P
TAPS = 4
XB0 = DI
DT0 = DI + DI + 2 * DS
DPROJ = DT0 + NH
L = 64
CHUNK = 512
TT = CHUNK // P
SEQS = CHUNK // L
NCHUNK = TOK // CHUNK
A_LOG_MAX = 80.0


def need(eng, sem, value):
    if isinstance(value, int) and value <= 0:
        return
    eng.wait_ge(sem, value)


def need_apart(eng, passed, *waits):
    for sem, value in waits:
        need(eng, sem, value)
    eng.sem_inc(passed, 1)


def pairs_of_steps(eng, n, step):
    step(0, 0)
    step(1, 1)
    with eng.Fori(1, n // 2) as r:
        step(r * 2, 0)
        step(r * 2 + 1, 1)


class Tools:

    def __init__(self, nc, ctx, tag):
        self.nc, self.ctx, self.tag = nc, ctx, tag

    def sb(self, name, shape, dt=F32):
        return self.ctx.enter_context(self.nc.sbuf_tensor(f"{self.tag}_{name}", shape, dt))

    def banks(self, n=8):
        return [self.ctx.enter_context(self.nc.psum_tensor(f"{self.tag}_bank{i}", [P, BANK], F32)) for i in range(n)]

    def sem(self, name):
        return self.nc.alloc_semaphore(name=f"{self.tag}_{name}")


class Chain:

    def __init__(self, eng, sem, base=0):
        self.eng, self.sem, self.base, self.n = eng, sem, base, 0

    def mark(self, ins):
        self.n += 1
        ins.then_inc(self.sem, 1)

    def value(self):
        return self.base + self.n

    def wait(self):
        self.eng.wait_ge(self.sem, self.value())

    def link(self, ins):
        self.mark(ins)
        self.wait()


def make_identity(pool, ident, sem):
    pool.memset(ident[:, :], 0.0).then_inc(sem, 1)
    pool.wait_ge(sem, 1)
    pool.affine_select(out=ident[:, :], in_=ident[:, :], compare_op=ALU.not_equal, fill=1.0, base=0,
                       pattern=[[-1, P]], channel_multiplier=1).then_inc(sem, 1)




def block_projections(nc, x, W, qk_dram, v_dram):
    G = CHUNK // N
    STEPS = N // G * B
    with ExitStack() as ctx:
        t_ = Tools(nc, ctx, "prj")
        sb, sem = t_.sb, t_.sem
        bank = t_.banks()
        T_, Q_, V_ = bank[0:2], bank[2:6], bank[6:8]
        ident = sb("ident", [P, P])
        wqk = sb("wqk", [P, 2, KT, E])
        wv = sb("wv", [P, 2, KT, E])
        xin = [sb(f"xin{u}", [P, TT, E]) for u in range(2)]
        xT = [sb(f"xT{u}", [P, KT, CHUNK]) for u in range(2)]
        qk = [sb(f"qk{u}", [P, 4, CHUNK]) for u in range(2)]
        vs = [sb(f"vs{u}", [P, PAIRS, G, DK]) for u in range(2)]
        ident_set, w_loaded = sem("ident_set"), sem("w_loaded")
        x_loaded = [sem(f"x_loaded{u}") for u in range(2)]
        transposed, xT_by_act, xT_by_dve = sem("transposed"), sem("xT_by_act"), sem("xT_by_dve")
        qk_done, qk_by_act, qk_by_dve = sem("qk_done"), sem("qk_by_act"), sem("qk_by_dve")
        v_done, v_by_act, v_by_dve = sem("v_done"), sem("v_by_act"), sem("v_by_dve")
        qk_stored = [sem(f"qk_stored{u}") for u in range(2)]
        v_stored = [sem(f"v_stored{u}") for u in range(2)]
        block = ctx.enter_context(nc.Block())

        rows = x.rearrange("(g t p) c -> g p t c", t=TT, p=P)
        cols = x.rearrange("(b l g t jj) c -> b jj l g t c", b=B, l=N, g=STEPS, t=2)
        STORES = PAIRS * 16

        @block.sync
        def _(sp):
            for m, name in enumerate(("Wq", "Wk")):
                sp.dma_start(wqk[:, m], W[name].rearrange("(k p) n -> p k n", p=P)).then_inc(w_loaded, 16)
            for m, name in enumerate(("Wv1", "Wv2")):
                sp.dma_start(wv[:, m], W[name].rearrange("(k p) n -> p k n", p=P)).then_inc(w_loaded, 16)

            def load_rows(t, u):
                need(sp, transposed, 2 * t - 2)
                sp.dma_start(xin[u][:, :, :], rows[t]).then_inc(x_loaded[u], 16)

            def load_cols(t, u):
                sp.wait_ge(transposed, 2 * t - 2 + 2 * STEPS)
                for b in range(B):
                    for jj in range(2):
                        sp.dma_start(xin[u][jj * N:(jj + 1) * N, 2 * b:2 * b + 2, :],
                                     cols[b, jj, :, t]).then_inc(x_loaded[u], 16)

            pairs_of_steps(sp, STEPS, load_rows)
            pairs_of_steps(sp, STEPS, load_cols)

        @block.gpsimd
        def _(pool):
            make_identity(pool, ident, ident_set)

            def store_rows(t, u):
                pool.wait_ge(qk_by_act, 2 * t + 2)
                pool.wait_ge(qk_by_dve, 2 * t + 2)
                for m in range(4):
                    pool.dma_start(qk_dram[m // 2, (m % 2) * P:(m % 2 + 1) * P, bass.ds(t * CHUNK, CHUNK)],
                                   qk[u][:, m, :]).then_inc(qk_stored[u], 16)
                store_v(0, t, u)

            def store_v(v, t, u):
                pool.wait_ge(v_by_act, t + 1 + v * STEPS)
                pool.wait_ge(v_by_dve, t + 1 + v * STEPS)
                for pr in range(PAIRS):
                    if v == 0:
                        dst = v_dram[0, pr].rearrange("p b i d -> p (b i) d")[:, bass.ds(t * G, G), :]
                        pool.dma_start(dst, vs[u][:, pr]).then_inc(v_stored[u], 16)
                    else:
                        dst = v_dram[1, pr, :, :, bass.ds(t * (G // 2), G // 2), :]
                        pool.dma_start(dst, vs[u][:, pr].rearrange("p (b j) d -> p b j d", b=B))\
                            .then_inc(v_stored[u], 16)

            pairs_of_steps(pool, STEPS, store_rows)
            pairs_of_steps(pool, STEPS, lambda t, u: store_v(1, t, u))
            for u in range(2):
                pool.wait_ge(qk_stored[u], 64 * STEPS // 2)
                pool.wait_ge(v_stored[u], STORES * STEPS)

        def base(v):
            return v * STEPS

        @block.tensor
        def _(pe):
            pe.wait_ge(ident_set, 2)
            pe.wait_ge(w_loaded, 64)

            def step(v, t, u):
                need(pe, xT_by_act, t + base(v))
                need(pe, xT_by_dve, t + base(v))
                for k in range(KT):
                    for tile in range(TT):
                        mm = pe.transpose(T_[k][:, tile * P:(tile + 1) * P], xin[u][:, tile, k * P:(k + 1) * P],
                                          ident[:, :])
                    mm.then_inc(transposed, 1)
                pe.wait_ge(xT_by_act, t + 1 + base(v))
                pe.wait_ge(xT_by_dve, t + 1 + base(v))
                if v == 0:
                    need(pe, qk_by_act, 2 * t)
                    need(pe, qk_by_dve, 2 * t)
                    for m in range(4):
                        for k in range(KT):
                            mm = pe.matmul(Q_[m][:, :], wqk[:, m // 2, k, (m % 2) * P:(m % 2 + 1) * P],
                                           xT[u][:, k, :], start=(k == 0), stop=(k == KT - 1))
                        mm.then_inc(qk_done, 1)
                need(pe, v_by_act, t + base(v))
                need(pe, v_by_dve, t + base(v))
                for g in range(G):
                    for k in range(KT):
                        for h2 in range(2):
                            mm = pe.matmul(V_[g // 4][h2 * N:(h2 + 1) * N, (g % 4) * P:(g % 4 + 1) * P],
                                           xT[u][:, k, g * N:(g + 1) * N], wv[:, v, k, h2 * P:(h2 + 1) * P],
                                           start=(k == 0), stop=(k == KT - 1))
                    if g % 4 == 3:
                        mm.then_inc(v_done, 1)

            def loaded(v, r, u):
                per = 16 if v == 0 else 64
                pe.wait_ge(x_loaded[u], (r + 1) * per + (0 if v == 0 else STEPS // 2 * 16))

            for v in range(2):
                for u in range(2):
                    loaded(v, 0, u)
                    step(v, u, u)
                with pe.Fori(1, STEPS // 2) as r:
                    for u in range(2):
                        loaded(v, r, u)
                        step(v, r * 2 + u, u)

        def evacuate(eng, copy, mine, v, t, r, u):
            by_xT, by_qk, by_v = ((xT_by_act, qk_by_act, v_by_act), (xT_by_dve, qk_by_dve, v_by_dve))[mine]
            eng.wait_ge(transposed, 2 * (t + base(v)) + 1 + mine)
            if v == 0:
                need(eng, v_done, 2 * t - 2)
            else:
                eng.wait_ge(v_done, 2 * t - 2 + 2 * STEPS)
            copy(xT[u][:, mine, :], T_[mine][:, :]).then_inc(by_xT, 1)
            if v == 0:
                need(eng, qk_stored[u], r * 64)
                for m in (2 * mine, 2 * mine + 1):
                    eng.wait_ge(qk_done, 4 * t + m + 1)
                    copy(qk[u][:, m, :], Q_[m][:, :]).then_inc(by_qk, 1)
            need(eng, v_stored[u], r * STORES + v * STEPS // 2 * STORES)
            eng.wait_ge(v_done, 2 * (t + base(v)) + 1 + mine)
            copy(vs[u][:, :, mine * 4:mine * 4 + 4, :].rearrange("p r g d -> p g r d"),
                 V_[mine][:, :].rearrange("p (g r d) -> p g r d", g=4, r=PAIRS)).then_inc(by_v, 1)

        def all_steps(eng, copy, mine):
            for v in range(2):
                for u in range(2):
                    evacuate(eng, copy, mine, v, u, 0, u)
                with eng.Fori(1, STEPS // 2) as r:
                    for u in range(2):
                        evacuate(eng, copy, mine, v, r * 2 + u, r, u)

        @block.scalar
        def _(act):
            all_steps(act, lambda o, i: act.activation(o, i, ACT.Copy), 0)

        @block.vector
        def _(dve):
            all_steps(dve, lambda o, i: dve.tensor_copy(o, i), 1)


def steps(eng, n, step):
    step(0)
    with eng.Fori(1, n) as t:
        step(t)


def block_softmax(nc, qk_dram, att):
    LB = 4
    NB = N // LB
    KL = 16
    JB = 4
    HL = N // 2
    with ExitStack() as ctx:
        t_ = Tools(nc, ctx, "smx")
        sb, sem = t_.sb, t_.sem
        bank = t_.banks()
        S_, T_ = bank[0:4], bank[4:8]
        ident = sb("ident", [P, P])
        q = sb("q", [P, N * N])
        kb = [sb(f"kb{u}", [P, KL, 2, N]) for u in range(2)]
        raw = sb("raw", [P, 2, N, N])
        mx = sb("mx", [P, 2, N])
        rsum = sb("rsum", [P, 2, N])
        rinv = sb("rinv", [P, 2, N])
        ident_set, kb_zeroed, q_loaded = sem("ident_set"), sem("kb_zeroed"), sem("q_loaded")
        k_loaded = [sem(f"k_loaded{u}") for u in range(2)]
        scored, s_by_act, s_by_dve = sem("scored"), sem("s_by_act"), sem("s_by_dve")
        maxed, shifted, exped = sem("maxed"), sem("shifted"), sem("exped")
        summed, inverted, normed = sem("summed"), sem("inverted"), [sem("normed0"), sem("normed1")]
        passed = sem("passed")
        turned, t_by_act, t_by_dve = sem("turned"), sem("t_by_act"), sem("t_by_dve")
        block = ctx.enter_context(nc.Block())

        @block.sync
        def _(sp):
            def load(pr):
                need(sp, scored, pr * (2 * NB))
                for b in range(B):
                    sp.dma_start(q[b * 64:(b + 1) * 64, :],
                                 qk_dram[0, bass.ds(pr * 64, 64), b * N * N:(b + 1) * N * N]).then_inc(q_loaded, 16)
                for c in range(N // KL):
                    need(sp, scored, pr * (2 * NB) + (c - 1) * (2 * KL // LB))
                    for b in range(B):
                        for h2 in range(2):
                            lo = (2 * b + h2) * DK
                            src = qk_dram[1, bass.ds(pr * 64 + h2 * DK, DK),
                                          b * N * N + c * KL * N:b * N * N + (c + 1) * KL * N]
                            sp.dma_start(kb[c % 2][lo:lo + DK, :, h2, :], src.rearrange("p (l j) -> p l j", l=KL))\
                                .then_inc(k_loaded[c % 2], 16)

            sp.wait_ge(kb_zeroed, 2)
            steps(sp, PAIRS, load)

        @block.gpsimd
        def _(pool):
            for u in range(2):
                pool.memset(kb[u][:, :, :, :], 0.0).then_inc(kb_zeroed, 1)
            make_identity(pool, ident, ident_set)

            def step(pr):
                pool.wait_ge(inverted, pr * 2 + 1)
                for half in range(2):
                    v = raw[:, 0, half * HL:(half + 1) * HL, :]
                    pool.tensor_tensor(v, v, rinv[:, 0, :].unsqueeze(1).broadcast_to((P, HL, N)), ALU.mult)\
                        .then_inc(normed[0], 1)

            steps(pool, PAIRS, step)

        @block.tensor
        def _(pe):
            pe.wait_ge(ident_set, 2)
            qv = q[:, :].rearrange("p (i l) -> p l i", l=N)

            def step(pr):
                pe.wait_ge(q_loaded, pr * 32 + 32)
                for g in range(NB):
                    c = g * LB // KL
                    if g * LB % KL == 0:
                        pe.wait_ge(k_loaded[c % 2], pr * 128 + (c // 2) * 64 + 64)
                    need_apart(pe, passed, (s_by_act, pr * NB + g - 1), (s_by_dve, pr * NB + g - 1))
                    for l4 in range(LB):
                        for b in range(B):
                            r = slice(b * 64, (b + 1) * 64)
                            mm = pe.matmul(S_[2 * (g % 2) + b][r, l4 * P:(l4 + 1) * P], qv[r, g * LB + l4, :],
                                           kb[c % 2][r, (g * LB + l4) % KL, :, :], start=True, stop=True)
                            if l4 == LB - 1:
                                mm.then_inc(scored, 1)
                pe.wait_ge(normed[0], pr * 2 + 2)
                pe.wait_ge(normed[1], pr * 2 + 2)
                for g in range(N // JB):
                    need(pe, (t_by_act, t_by_dve)[g % 2], pr * 8 + g // 2 - 1)
                    for j in range(JB):
                        mm = pe.transpose(T_[g % 4][:, j * P:(j + 1) * P],
                                          raw[:, :, :, g * JB + j].rearrange("p h l -> p (h l)"), ident[:, :])
                    mm.then_inc(turned, 1)

            steps(pe, PAIRS, step)

        def copy_scores(eng, copy, b, pr, done):
            need(eng, turned, pr * 16)
            r = slice(b * 64, (b + 1) * 64)
            for g in range(NB):
                eng.wait_ge(scored, pr * (2 * NB) + 2 * g + 1 + b)
                copy(raw[r, :, g * LB:(g + 1) * LB, :],
                     S_[2 * (g % 2) + b][r, :].rearrange("p (l h j) -> p h l j", l=LB, h=2)).then_inc(done, 1)

        def copy_att(eng, copy, parity, pr, done):
            for g in range(parity, N // JB, 2):
                eng.wait_ge(turned, pr * 16 + g + 1)
                dst = att[:, bass.ds(pr, 1), :, g * JB:(g + 1) * JB].rearrange("p o m j -> p (o m) j")
                copy(dst.rearrange("p m j -> p j m"), T_[g % 4][:, :].rearrange("p (j m) -> p j m", j=JB))\
                    .then_inc(done, 1)

        @block.scalar
        def _(act):
            def copy(o, i):
                return act.activation(o, i, ACT.Copy)

            def step(pr):
                copy_scores(act, copy, 0, pr, s_by_act)
                for h in range(2):
                    for half in range(2):
                        act.wait_ge(shifted, pr * 4 + 2 * h + half + 1)
                        v = raw[:, h, half * HL:(half + 1) * HL, :]
                        act.activation(v, v, ACT.Exp, scale=SCALE).then_inc(exped, 1)
                copy_att(act, copy, 0, pr, t_by_act)

            steps(act, PAIRS, step)

        @block.vector
        def _(dve):
            def copy(o, i):
                return dve.tensor_copy(o, i)

            def step(pr):
                copy_scores(dve, copy, 1, pr, s_by_dve)
                dve.wait_ge(s_by_act, pr * NB + NB)
                dve.wait_ge(s_by_dve, pr * NB + NB)
                for h in range(2):
                    dve.tensor_reduce(mx[:, h, :], raw[:, h, :, :].rearrange("p l j -> p j l"), AX_X, ALU.max)\
                        .then_inc(maxed, 1)
                    dve.wait_ge(maxed, pr * 2 + h + 1)
                    for half in range(2):
                        v = raw[:, h, half * HL:(half + 1) * HL, :]
                        dve.tensor_tensor(v, v, mx[:, h, :].unsqueeze(1).broadcast_to((P, HL, N)), ALU.subtract)\
                            .then_inc(shifted, 1)
                for h in range(2):
                    dve.wait_ge(exped, pr * 4 + 2 * h + 2)
                    if h == 0:
                        need(dve, normed[0], pr * 2)
                    dve.tensor_reduce(rsum[:, h, :], raw[:, h, :, :].rearrange("p l j -> p j l"), AX_X, ALU.add)\
                        .then_inc(summed, 1)
                    dve.wait_ge(summed, pr * 2 + h + 1)
                    dve.reciprocal(rinv[:, h, :], rsum[:, h, :]).then_inc(inverted, 1)
                dve.wait_ge(inverted, pr * 2 + 2)
                for half in range(2):
                    v = raw[:, 1, half * HL:(half + 1) * HL, :]
                    dve.tensor_tensor(v, v, rinv[:, 1, :].unsqueeze(1).broadcast_to((P, HL, N)), ALU.mult)\
                        .then_inc(normed[1], 1)
                copy_att(dve, copy, 1, pr, t_by_dve)

            steps(dve, PAIRS, step)


def block_trilinear(nc, v_dram, att, out_dram):
    G = 16
    NG = N // G
    QI = 4
    NQ = G // QI
    HI = G // 2
    M = 2 * STRIP_D
    DD = 22
    with ExitStack() as ctx:
        t_ = Tools(nc, ctx, "tri")
        sb, sem = t_.sb, t_.sem
        bank = t_.banks(NQ)
        v2ps = ctx.enter_context(nc.psum_tensor("tri_v2ps", [P, 3 * BANK], F32))
        v1 = [sb(f"v1_{u}", [P, N, DK]) for u in range(2)]
        v2in = sb("v2in", [P, N, DK])
        v2sb = [sb(f"v2sb{u}", [P, DK - DD, N]) for u in range(2)]
        av = [sb(f"av{u}", [P, DK, N]) for u in range(2)]
        sel = [sb(f"sel{u}", [P, DK // STRIP_D, STRIP_D * M]) for u in range(4)]
        ost = [sb(f"ost{u}", [P, 2, HI * N]) for u in range(2)]
        v1_loaded, v2_loaded = sem("v1_loaded"), sem("v2_loaded")
        v2_in_sb, v2_in_ps = sem("v2_in_sb"), sem("v2_in_ps")
        sel_zeroed, sums_zeroed, sel_ready = sem("sel_zeroed"), sem("sums_zeroed"), sem("sel_ready")
        av_by_dve, av_by_pool, i_done = sem("av_by_dve"), sem("av_by_pool"), sem("i_done")
        o_copied, o_stored = sem("o_copied"), [sem(f"o_stored{u}") for u in range(2)]
        block = ctx.enter_context(nc.Block())
        attf = att[:, :, :, :].rearrange("p r m j -> p (r m j)")
        v2d = v2ps[:, 0:DD * N].rearrange("p (d j) -> p d j", d=DD)

        def groups(eng, c, body):
            first = 0
            if isinstance(c, int) and c == 0:
                body(0, 0)
                first = 1
            with eng.Fori(first, NG) as g:
                body(g, c * N + g * G)

        def combinations(eng, combo):
            combo(0, 0)
            combo(0, 1)
            with eng.Fori(1, PAIRS) as pr:
                combo(pr, 0)
                combo(pr, 1)

        @block.sync
        def _(sp):
            def load(pr, b):
                c = pr * 2 + b
                need(sp, i_done, (c - 1) * N)
                sp.dma_start(v1[b][:, :, :], v_dram[0, bass.ds(pr, 1), :, b].rearrange("o p i d -> (o p) i d"))\
                    .then_inc(v1_loaded, 16)
                need(sp, v2_in_ps, c)
                sp.dma_start(v2in[:, :, :], v_dram[1, bass.ds(pr, 1), :, b].rearrange("o p j d -> (o p) j d"))\
                    .then_inc(v2_loaded, 16)

            def store(pr, b, g):
                for u in range(2):
                    sp.wait_ge(o_copied, ((pr * 2 + b) * NG + g) * NQ + (u + 1) * (NQ // 2))
                    rows = out_dram[bass.ds(pr * (2 * DK), 2 * DK),
                                    bass.ds(g * (G * N) + (b * N * N + u * HI * N), HI * N)]
                    for s in range(STRIPS):
                        sp.dma_start(rows.rearrange("(a s r) t -> s r a t", a=2, s=STRIPS)[s],
                                     ost[u][s * 32:s * 32 + M]).then_inc(o_stored[u], 16)

            def combo(pr, b, last=False):
                store(pr, b, 0)
                if not last:
                    load(*((pr, 1) if b == 0 else (pr + 1, 0)))
                with sp.Fori(1, NG) as g:
                    store(pr, b, g)

            load(0, 0)
            combo(0, 0)
            combo(0, 1)
            with sp.Fori(1, PAIRS - 1) as pr:
                combo(pr, 0)
                combo(pr, 1)
            combo(PAIRS - 1, 0)
            combo(PAIRS - 1, 1, last=True)
            for u in range(2):
                sp.wait_ge(o_stored[u], 16 * STRIPS * B * PAIRS * NG)

        def multiply(eng, v2_ready, ready, v2_of, d0, d1):
            def combo(pr, b):
                def body(g, n):
                    eng.wait_ge(v2_ready, pr * 2 + b + 1)
                    for k in range(G):
                        need(eng, i_done, n + k - 1)
                        a = attf[:, bass.ds((n + k) * N, N)]
                        eng.tensor_tensor(av[k % 2][:, d0:d1, :], a.unsqueeze(1).broadcast_to((P, d1 - d0, N)),
                                          v2_of(b), ALU.mult).then_inc(ready, 1)

                groups(eng, pr * 2 + b, body)

            combinations(eng, combo)

        @block.gpsimd
        def _(pool):
            for u in range(4):
                pool.memset(sel[u][:, :, :], 0.0).then_inc(sel_zeroed, 1)
            multiply(pool, v2_in_sb, av_by_pool, lambda b: v2sb[b][:, :, :], DD, DK)

        @block.vector
        def _(dve):
            for q in range(NQ):
                dve.memset(bank[q][:, :], 0.0).then_inc(sums_zeroed, 1)
            multiply(dve, v2_in_ps, av_by_dve, lambda b: v2d, 0, DD)

        @block.tensor
        def _(pe):
            pe.wait_ge(sums_zeroed, NQ)

            def combo(pr, b):
                def body(g, n):
                    for k in range(G):
                        q = k // QI
                        if k % QI == 0:
                            need(pe, o_copied, ((pr * 2 + b) * NG + g) * NQ + q - NQ + 1)
                        pe.wait_ge(sel_ready, (n + k) * 2 + 2)
                        pe.wait_ge(av_by_dve, n + k + 1)
                        for a in range(2):
                            if a == 1:
                                pe.wait_ge(av_by_pool, n + k + 1)
                            col = a * (QI * N) + (k % QI) * N
                            for d4 in range(STRIP_D):
                                for s in range(STRIPS):
                                    dg = a * STRIPS + s
                                    mm = pe.matmul(bank[q][s * 32:s * 32 + M, col:col + N],
                                                   sel[k % 4][:, dg, d4 * M:(d4 + 1) * M],
                                                   av[k % 2][:, dg * STRIP_D + d4, :],
                                                   start=(d4 == 0), stop=(d4 == STRIP_D - 1))
                        mm.then_inc(i_done, 1)

                groups(pe, pr * 2 + b, body)

            combinations(pe, combo)

        @block.scalar
        def _(act):
            act.wait_ge(sel_zeroed, 4)

            def turn_v2(pr, b):
                c = pr * 2 + b
                act.wait_ge(v2_loaded, c * 16 + 16)
                need(act, av_by_pool, (c - 1) * N)
                turned = v2in[:, :, :].rearrange("p j d -> p d j")
                act.activation(v2sb[b][:, :, :], turned[:, DD:], ACT.Copy).then_inc(v2_in_sb, 1)
                need(act, av_by_dve, c * N)
                for lo in range(0, DD, BANK // N):
                    hi = min(lo + BANK // N, DD)
                    ins = act.activation(v2d[:, lo:hi], turned[:, lo:hi], ACT.Copy)
                ins.then_inc(v2_in_ps, 1)

            def copy_sums(gi, q):
                u = q // 2
                need(act, o_stored[u], gi * (16 * STRIPS))
                act.wait_ge(i_done, gi * G + (q + 1) * QI)
                lo = (q % 2) * QI * N
                act.activation(ost[u][:, :, lo:lo + QI * N], bank[q][:, :].rearrange("p (a t) -> p a t", a=2),
                               ACT.Copy).then_inc(o_copied, 1)

            def combo(pr, b, last=False):
                c = pr * 2 + b

                def body(g, n):
                    gi = c * NG + g
                    act.wait_ge(v1_loaded, c * 16 + 16)
                    for k in range(G):
                        need(act, i_done, n + k - 3)
                        for h2 in range(2):
                            r = slice(h2 * N, (h2 + 1) * N)
                            src = v1[b][r, bass.ds(g * G + k, 1), :].rearrange("p o (g f) -> p (o g) f", f=STRIP_D)
                            lo = h2 * STRIP_D
                            act.activation(sel[k % 4][r, :, lo:lo + (STRIP_D - 1) * (M + 1) + 1:M + 1], src,
                                           ACT.Copy).then_inc(sel_ready, 1)
                        if k == 2 and not (isinstance(gi, int) and gi == 0):
                            copy_sums(gi - 1, NQ - 1)
                        if k in (6, 10, 14):
                            copy_sums(gi, (k - 6) // QI)

                groups(act, c, body)
                if not last:
                    turn_v2(*((pr, 1) if b == 0 else (pr + 1, 0)))

            turn_v2(0, 0)
            combo(0, 0)
            combo(0, 1)
            with act.Fori(1, PAIRS - 1) as pr:
                combo(pr, 0)
                combo(pr, 1)
            combo(PAIRS - 1, 0)
            combo(PAIRS - 1, 1, last=True)
            copy_sums(B * PAIRS * NG - 1, NQ - 1)


def pipeline(eng, n, front, back):
    front(0, 0)
    for c in (0, 1):
        front(c + 1, (c + 1) % 2)
        back(c, c % 2)
    with eng.Fori(1, n // 2 - 1) as r:
        for u in range(2):
            front(r * 2 + (u + 1), (u + 1) % 2)
            back(r * 2 + u, u)
    front(n - 1, (n - 1) % 2)
    back(n - 2, n % 2)
    back(n - 1, (n - 1) % 2)


def block_mlp(nc, x, attn_dram, W, x1):
    with ExitStack() as ctx:
        t_ = Tools(nc, ctx, "mlp")
        sb, sem = t_.sb, t_.sem
        bank = t_.banks()
        WO_, HID_, OUT_ = bank[0:2], bank[2:6], bank[6:8]
        ident = sb("ident", [P, P])
        wo, w1, w2 = sb("wo", [P, KT, E]), sb("w1", [P, KT, F]), sb("w2", [P, FT, E])
        b1 = sb("b1", [P, FT])
        row = {n: sb(n, [P, E]) for n in ("g1", "be1", "b2", "g2", "be2")}
        eps = sb("eps", [P, 1])
        att = [sb(f"att{u}", [P, KT, CHUNK]) for u in range(2)]
        xin = [sb(f"xin{u}", [P, TT, E]) for u in range(2)]
        h = [sb(f"h{u}", [P, TT, E]) for u in range(2)]
        hb = [sb(f"hb{u}", [P, TT, E]) for u in range(2)]
        hT = [sb(f"hT{u}", [P, KT, CHUNK]) for u in range(2)]
        hid = sb("hid", [P, FT, CHUNK])
        o = [sb(f"o{u}", [P, TT, E]) for u in range(2)]
        stats = [sb(f"stats{n}", [P, TT, 6]) for n in range(2)]
        mv = [sb(f"mv{n}", [P, TT, 2]) for n in range(2)]
        std = [sb(f"std{n}", [P, TT]) for n in range(2)]
        rstd = [sb(f"rstd{n}", [P, TT]) for n in range(2)]
        ident_set, w_loaded, eps_set = sem("ident_set"), sem("w_loaded"), sem("eps_set")
        in_loaded = [sem(f"in_loaded{u}") for u in range(2)]
        wo_done, added = sem("wo_done"), sem("added")
        moments, rooted = [sem(f"moments{n}") for n in range(2)], [sem(f"rooted{n}") for n in range(2)]
        f_chain, b_chain = sem("f_chain"), sem("b_chain")
        h_ready, h_turned, hT_ready = sem("h_ready"), sem("h_turned"), sem("hT_ready")
        hid_done, hid_ready, w2_done, w2_added = sem("hid_done"), sem("hid_ready"), sem("w2_done"), sem("w2_added")
        o_ready, b2_added = sem("o_ready"), sem("b2_added")
        passed = sem("passed")
        o_stored = [sem(f"o_stored{u}") for u in range(2)]
        NW = 9
        LINKS = (4, 4)
        rows_in = x.rearrange("(c t p) e -> c p t e", t=TT, p=P)
        rows_out = x1.rearrange("(c t p) e -> c p t e", t=TT, p=P)
        attv = attn_dram.rearrange("(k p) t -> p k t", p=P)
        block = ctx.enter_context(nc.Block())

        @block.sync
        def _(sp):
            def load(c, u):
                need(sp, added, 2 * c - 2)
                sp.dma_start(att[u][:, :, :], attv[:, :, bass.ds(c * CHUNK, CHUNK)]).then_inc(in_loaded[u], 16)
                sp.dma_start(xin[u][:, :, :], rows_in[c]).then_inc(in_loaded[u], 16)
                if isinstance(c, int) and c == 0:
                    sp.dma_start(w1[:, :, :], W["W1"].rearrange("(k p) n -> p k n", p=P)).then_inc(w_loaded, 16)
                    sp.dma_start(w2[:, :, :], W["W2"].rearrange("(k p) n -> p k n", p=P)).then_inc(w_loaded, 16)
                    sp.dma_start(b1[:, :], W["b1"]).then_inc(w_loaded, 16)
                    for n, name in (("g1", "ln_agg_g"), ("be1", "ln_agg_b"), ("b2", "b2"), ("g2", "ln_out_g"),
                                    ("be2", "ln_out_b")):
                        sp.dma_start(row[n][:, :], W[name].partition_broadcast(P)).then_inc(w_loaded, 16)

            def store(c, u):
                sp.wait_ge(o_ready, c + 1)
                sp.dma_start(rows_out[c], o[u][:, :, :]).then_inc(o_stored[u], 16)

            sp.dma_start(wo[:, :, :], W["Wo"].rearrange("(k p) n -> p k n", p=P)).then_inc(w_loaded, 16)
            pipeline(sp, NCHUNK, load, store)
            for u in range(2):
                sp.wait_ge(o_stored[u], NCHUNK // 2 * 16)

        @block.gpsimd
        def _(pool):
            pool.memset(eps[:, :], EPS).then_inc(eps_set, 1)
            make_identity(pool, ident, ident_set)

        @block.tensor
        def _(pe):
            pe.wait_ge(ident_set, 2)
            pe.wait_ge(w_loaded, 16 * NW)

            def times_wo(c, u):
                pe.wait_ge(in_loaded[u], (c // 2) * 32 + 32)
                need(pe, hT_ready, 2 * c)
                for t in range(TT):
                    for k in range(KT):
                        mm = pe.matmul(WO_[t // 2][:, (t % 2) * E:(t % 2 + 1) * E], att[u][:, k, t * P:(t + 1) * P],
                                       wo[:, k, :], start=(k == 0), stop=(k == KT - 1))
                    if t % 2:
                        mm.then_inc(wo_done, 1)

            def turn_h(c, u):
                pe.wait_ge(h_ready, c + 1)
                for k in range(KT):
                    for t in range(TT):
                        mm = pe.transpose(WO_[k][:, t * P:(t + 1) * P], h[u][:, t, k * P:(k + 1) * P], ident[:, :])
                    mm.then_inc(h_turned, 1)

            def mlp(c, u):
                pe.wait_ge(hT_ready, 2 * c + 2)
                for m in range(FT):
                    need(pe, hid_ready, FT * (c - 1) + m + 1)
                    for k in range(KT):
                        mm = pe.matmul(HID_[m][:, :], w1[:, k, m * P:(m + 1) * P], hT[u][:, k, :],
                                       start=(k == 0), stop=(k == KT - 1))
                    mm.then_inc(hid_done, 1)
                pe.wait_ge(hid_ready, FT * c + FT)
                need(pe, w2_added, 2 * c)
                for t in range(TT):
                    for k in range(FT):
                        mm = pe.matmul(OUT_[t // 2][:, (t % 2) * E:(t % 2 + 1) * E], hid[:, k, t * P:(t + 1) * P],
                                       w2[:, k, :], start=(k == 0), stop=(k == FT - 1))
                    if t % 2:
                        mm.then_inc(w2_done, 1)

            times_wo(0, 0)
            turn_h(0, 0)

            def step(c, u):
                times_wo(c + 1, 1 - u)
                mlp(c, u)
                turn_h(c + 1, 1 - u)

            step(0, 0)
            step(1, 1)
            with pe.Fori(1, NCHUNK // 2 - 1) as r:
                step(r * 2, 0)
                step(r * 2 + 1, 1)
            step(NCHUNK - 2, 0)
            mlp(NCHUNK - 1, 1)

        @block.scalar
        def _(act):
            act.wait_ge(eps_set, 1)
            act.wait_ge(w_loaded, 16 * NW)

            def root(n, c):
                act.wait_ge(moments[n], c + 1)
                act.activation(std[n][:, :], mv[n][:, :, 1], ACT.Sqrt, bias=eps[:, :]).then_inc(rooted[n], 1)

            def copy_hT(c, u):
                for k in range(KT):
                    act.wait_ge(h_turned, 2 * c + k + 1)
                    act.activation(hT[u][:, k, :], WO_[k][:, :], ACT.Copy).then_inc(hT_ready, 1)

            def relu(c, u):
                need(act, w2_done, 2 * c)
                for m in range(FT):
                    act.wait_ge(hid_done, FT * c + m + 1)
                    act.activation(hid[:, m, :], HID_[m][:, :], ACT.Relu, bias=b1[:, m:m + 1]).then_inc(hid_ready, 1)

            root(0, 0)
            copy_hT(0, 0)

            def step(c, u):
                relu(c, u)
                root(0, c + 1)
                copy_hT(c + 1, 1 - u)
                root(1, c)

            step(0, 0)
            step(1, 1)
            with act.Fori(1, NCHUNK // 2 - 1) as r:
                step(r * 2, 0)
                step(r * 2 + 1, 1)
            step(NCHUNK - 2, 0)
            relu(NCHUNK - 1, 1)
            root(1, NCHUNK - 1)

        @block.vector
        def _(dve):
            dve.wait_ge(w_loaded, 16 * NW)

            def wide(v):
                return v[:, :].unsqueeze(1).broadcast_to((P, TT, E))

            def layer_norm(n, c, chain, v, out, gain, bias, done):
                for t in range(TT):
                    ins = dve.bn_stats(stats[n][:, t, :], v[:, t, :])
                chain.mark(ins)
                need_apart(dve, passed, (f_chain if n == 0 else b_chain, chain.value()))
                for t in range(TT):
                    ins = dve.bn_aggr(mv[n][:, t, :], stats[n][:, t, :])
                ins.then_inc(moments[n], 1)
                dve.wait_ge(moments[n], c + 1)
                dve.wait_ge(rooted[n], c + 1)
                chain.link(dve.reciprocal(rstd[n][:, :], std[n][:, :]))
                for t in range(TT):
                    ins = dve.tensor_scalar(out[:, t, :], v[:, t, :], mv[n][:, t, 0:1], rstd[n][:, t:t + 1],
                                            ALU.subtract, ALU.mult)
                chain.link(ins)
                chain.link(dve.tensor_tensor(out[:, :, :], out[:, :, :], wide(gain), ALU.mult))
                dve.tensor_tensor(out[:, :, :], out[:, :, :], wide(bias), ALU.add).then_inc(done, 1)

            def front(c, u):
                chain = Chain(dve, f_chain, c * LINKS[0])
                dve.wait_ge(in_loaded[u], (c // 2) * 32 + 32)
                need(dve, h_turned, 2 * c - 2)
                for half in range(2):
                    dve.wait_ge(wo_done, 2 * c + half + 1)
                    s = slice(2 * half, 2 * half + 2)
                    dve.tensor_tensor(h[u][:, s, :], WO_[half][:, :].rearrange("p (t e) -> p t e", t=2),
                                      xin[u][:, s, :], ALU.add).then_inc(added, 1)
                dve.wait_ge(added, 2 * c + 2)
                layer_norm(0, c, chain, h[u], h[u], row["g1"], row["be1"], h_ready)
                dve.wait_ge(h_ready, c + 1)

            def back(c, u):
                chain = Chain(dve, b_chain, c * LINKS[1])
                dve.tensor_tensor(hb[u][:, :, :], h[u][:, :, :], wide(row["b2"]), ALU.add).then_inc(b2_added, 1)
                dve.wait_ge(b2_added, c + 1)
                for half in range(2):
                    dve.wait_ge(w2_done, 2 * c + half + 1)
                    s = slice(2 * half, 2 * half + 2)
                    dve.tensor_tensor(hb[u][:, s, :], OUT_[half][:, :].rearrange("p (t e) -> p t e", t=2),
                                      hb[u][:, s, :], ALU.add).then_inc(w2_added, 1)
                dve.wait_ge(w2_added, 2 * c + 2)
                need(dve, o_stored[u], (c // 2) * 16)
                layer_norm(1, c, chain, hb[u], o[u], row["g2"], row["be2"], o_ready)

            pipeline(dve, NCHUNK, front, back)


def block_mamba(nc, W, x1, out, prev, cols):
    with ExitStack() as ctx:
        t_ = Tools(nc, ctx, "mv" if cols else "mh")
        sb, sem = t_.sb, t_.sem
        bank = t_.banks()
        XT_ = bank[0:2]
        PR_ = bank[2:5]
        G_ = bank[5]
        Y0_ = bank[6:8]
        PAIR = SEQS // 2
        ident, ones_blk = sb("ident", [P, P]), sb("ones_blk", [P, P])
        diag, diag0 = sb("diag", [P, L]), sb("diag0", [P, L])
        ones = sb("ones", [P, 32])
        pick = sb("pick", [P, 1])
        eps = sb("eps", [P, 1])
        win = sb("win", [P, KT, DPROJ])
        wf = sb("wf", [P, CT, E])
        out_w, fcw = sb("out_w", [P, KT, DI]), sb("fcw", [P, 2 * KT, E])
        cw, cb = sb("cw", [P, CT + 1, TAPS]), sb("cb", [P, CT + 1])
        dskip, normw = sb("dskip", [P, CT]), sb("normw", [P, CT])
        dtb, nega, bias = sb("dtb", [P, NH]), sb("nega", [P, NH]), sb("bias", [P, E])
        xin = [sb(f"xin{u}", [P, TT, E]) for u in range(2)]
        pv = [sb(f"pv{u}", [P, TT, E]) for u in range(2)] if cols else None
        ot = [sb(f"ot{u}", [P, TT, E]) for u in range(2)]
        xT = sb("xT", [P, KT, CHUNK])
        xp = sb("xp", [P, CT + 1, SEQS, L + TAPS - 1])
        cv = sb("cv", [P, CT + 1, CHUNK])
        xc = [sb(f"xc{u}", [P, CT, CHUNK]) for u in range(2)]
        bc = [sb(f"bc{u}", [DS, 2, CHUNK]) for u in range(2)]
        zs = [sb(f"zs{u}", [P, CT, CHUNK]) for u in range(2)]
        small = {n: sb(n, [P, TT, NH]) for n in ("x_dt", "absx", "e", "u", "iz", "den", "rden", "num", "num2", "lp",
                                                 "dt", "prod", "dA")}
        lnu = sb("lnu", [P, TT, NH])
        xtok = sb("xtok", [P, PAIR, DI])
        spread = sb("spread", [P, PAIR, NH, L])
        inj = sb("inj", [P, PAIR, NH, L])
        decay = [sb(f"decay{u}", [P, NH * L]) for u in range(2)]
        S = sb("S", [P, PAIR, NH, L])
        y, sq = sb("y", [P, CT, CHUNK]), sb("sq", [P, CT, CHUNK])
        ssr = sb("ssr", [P, CHUNK])
        rms, rstd = sb("rms", [P, TT]), sb("rstd", [P, TT])

        const_set, w_loaded, folded, wf_ready = sem("const_set"), sem("w_loaded"), sem("folded"), sem("wf_ready")
        fc_summed, nega_chain, xp_zeroed = sem("fc_summed"), sem("nega_chain"), sem("xp_zeroed")
        in_loaded = [sem(f"in_loaded{u}") for u in range(2)]
        turned, xT_copied, proj_done, proj_by_act = sem("turned"), sem("xT_copied"), sem("proj_done"), sem("proj_by_act")
        dt_read, conv_chain, conv_done, silued = sem("dt_read"), sem("conv_chain"), sem("conv_done"), sem("silued")
        absx_ready, e_ready, u_ready, ln_ready = sem("absx_ready"), sem("e_ready"), sem("u_ready"), sem("ln_ready")
        dt_chain, prod_ready, dA_ready = sem("dt_chain"), sem("prod_ready"), sem("dA_ready")
        xtok_done, xtok_copied, g_done = sem("xtok_done"), sem("xtok_copied"), sem("g_done")
        spread_ready, inj_ready = sem("spread_ready"), sem("inj_ready")
        da_done, scanned, s_ready = sem("da_done"), sem("scanned"), sem("s_ready")
        y_done, y_read, gated, squared, z_silued = (sem("y_done"), sem("y_read"), sem("gated"), sem("squared"),
                                                    sem("z_silued"))
        ss_done, ss_copied, col_done, col_read, rstd_ready = (sem("ss_done"), sem("ss_copied"), sem("col_done"),
                                                              sem("col_read"), sem("rstd_ready"))
        out_done, out_read, passed = sem("out_done"), sem("out_read"), sem("passed")
        o_stored = [sem(f"o_stored{u}") for u in range(2)]
        pv_loaded = [sem(f"pv_loaded{u}") for u in range(2)] if cols else None
        NCONST = 13 + CT
        NACT = 2 * CT + 1
        NW = 9 + (0 if cols else 1)
        PER_IO = 16 if not cols else 4 * 16

        rows = {n: a.rearrange("(c t p) e -> c p t e", t=TT, p=P) for n, a in (("x", x1), ("o", out))}
        grid = {n: a.rearrange("(b h c t q) e -> b q h c t e", b=B, h=N, t=2, q=2)
                for n, a in (("x", x1), ("o", out), ("p", prev if cols else x1))}
        block = ctx.enter_context(nc.Block())

        def stages(eng, step):
            step(-1, 1, False)
            step(0, 0, False)
            step(1, 1, False)
            with eng.Fori(1, NCHUNK // 2 - 1) as r:
                for u in range(2):
                    step(r * 2 + u, u, False)
            step(NCHUNK - 2, 0, False)
            step(NCHUNK - 1, 1, True)

        def started(c):
            return not (isinstance(c, int) and c < 0)

        @block.sync
        def _(sp):
            def move(name, c, tile, to_dram, done):
                if not cols:
                    a, b = tile[:, :, :], rows[name][c]
                    sp.dma_start(*((b, a) if to_dram else (a, b))).then_inc(done, 16)
                    return
                for b in range(B):
                    for q in range(2):
                        a = tile[q * L:(q + 1) * L, 2 * b:2 * b + 2, :]
                        d = grid[name][b, q, :, c]
                        sp.dma_start(*((d, a) if to_dram else (a, d))).then_inc(done, 16)

            def load(c, u):
                need(sp, turned, 2 * c - 2)
                move("x", c, xin[u], False, in_loaded[u])

            def load_prev(c, u):
                if cols:
                    need(sp, out_read, TT * (c - 1))
                    move("p", c, pv[u], False, pv_loaded[u])

            def step(c, u, last):
                if not started(c):
                    return
                if not (isinstance(c, int) and c + 2 >= NCHUNK):
                    load(c + 2, u)
                sp.wait_ge(out_read, TT * c + TT)
                move("o", c, ot[u], True, o_stored[u])
                if not (isinstance(c, int) and c + 2 >= NCHUNK):
                    load_prev(c + 2, u)

            load(0, 0)
            sp.dma_start(win[:, :, :], W["in_wT"].rearrange("(k p) n -> p k n", p=P)).then_inc(w_loaded, 16)
            for tile, name in ((cw, "conv_w"), (cb, "conv_b"), (dskip, "D"), (normw, "norm_w")):
                sp.dma_start(tile[:], W[name]).then_inc(w_loaded, 16)
            sp.dma_start(dtb[:, :], W["dt_bias"].partition_broadcast(P)).then_inc(w_loaded, 16)
            sp.dma_start(nega[:, :], W["A_log"].partition_broadcast(P)).then_inc(w_loaded, 16)
            sp.dma_start(out_w[:, :, :], W["out_w"].rearrange("(k p) n -> p k n", p=P)).then_inc(w_loaded, 16)
            sp.dma_start(fcw[:, :, :], W["fc_wT"].rearrange("(k p) n -> p k n", p=P)).then_inc(w_loaded, 16)
            if not cols:
                sp.dma_start(bias[:, :], W["fc_b"].partition_broadcast(P)).then_inc(w_loaded, 16)
            load(1, 1)
            load_prev(0, 0)
            load_prev(1, 1)
            stages(sp, step)
            for u in range(2):
                sp.wait_ge(o_stored[u], NCHUNK // 2 * PER_IO)

        @block.gpsimd
        def _(pool):
            make_identity(pool, ident, const_set)
            pool.memset(ones[:, :], 1.0).then_inc(const_set, 1)
            pool.memset(pick[:, :], 0.0).then_inc(const_set, 1)
            pool.memset(eps[:, :], EPS).then_inc(const_set, 1)
            pool.memset(xp[:, :, :, :], 0.0).then_inc(xp_zeroed, 1)
            pool.memset(ones_blk[:, :], 0.0).then_inc(const_set, 1)
            pool.wait_ge(const_set, 6)
            for m in range(CT):
                pool.memset(pick[m * 32:m * 32 + 1, :], 1.0).then_inc(const_set, 1)
            pool.wait_ge(const_set, 6 + CT)
            for q in range(2):
                r = slice(q * L, (q + 1) * L)
                pool.memset(ones_blk[r, r], 1.0).then_inc(const_set, 1)
                pool.tensor_copy(diag[r, :], ident[r, r]).then_inc(const_set, 1)
                pool.tensor_copy(diag0[r, :], ident[r, r]).then_inc(const_set, 1)
            pool.wait_ge(const_set, 12 + CT)
            pool.memset(diag0[:, 0:1], 0.0).then_inc(const_set, 1)
            pool.wait_ge(const_set, NCONST)

            def step(c, u, last):
                if not last:
                    A(c + 1)

            def A(c):
                pool.wait_ge(dA_ready, c + 1)
                for p in range(PAIR):
                    need(pool, da_done, PAIR * (c - 1) + p + 1)
                    pool.tensor_tensor(spread[:, p], diag0[:, :].unsqueeze(1).broadcast_to((P, NH, L)),
                                       small["dA"][:, p, :].unsqueeze(2).broadcast_to((P, NH, L)), ALU.mult)\
                        .then_inc(spread_ready, 1)
                    need(pool, scanned, PAIR * (c - 1) + p + 1)
                    pool.tensor_tensor(inj[:, p], diag[:, :].unsqueeze(1).broadcast_to((P, NH, L)),
                                       small["dt"][:, p, :].unsqueeze(2).broadcast_to((P, NH, L)), ALU.mult)\
                        .then_inc(inj_ready, 1)

            stages(pool, step)

        @block.tensor
        def _(pe):
            pe.wait_ge(const_set, NCONST)
            pe.wait_ge(w_loaded, 16 * NW)
            pe.wait_ge(fc_summed, 1)
            for m in range(CT):
                for k in range(KT):
                    mm = pe.matmul(bank[m][:, 0:E], out_w[:, k, m * P:(m + 1) * P], fcw[:, k, :],
                                   start=(k == 0), stop=(k == KT - 1))
                mm.then_inc(folded, 1)
            pe.wait_ge(wf_ready, CT)

            def products_of_b_c(c, u):
                need_apart(pe, passed, (silued, 6 * c + 6), (col_read, c))
                for s in range(SEQS):
                    mm = pe.matmul(G_[(s % 2) * L:(s % 2 + 1) * L, (s // 2) * L:(s // 2 + 1) * L],
                                   bc[u][:, 0, s * L:(s + 1) * L], bc[u][:, 1, s * L:(s + 1) * L],
                                   start=True, stop=True)
                mm.then_inc(g_done, 1)

            def spread_decay(c, p):
                if p < 2:
                    pe.wait_ge(proj_by_act, NACT * (c + 1))
                else:
                    pe.wait_ge(scanned, PAIR * c + p - 1)
                pe.wait_ge(spread_ready, PAIR * c + p + 1)
                pe.matmul(PR_[p % 2][:, :], ones_blk[:, :], spread[:, p].rearrange("p h t -> p (h t)"),
                          start=True, stop=True).then_inc(da_done, 1)

            def turn_x(c, u):
                pe.wait_ge(silued, 6 * c + CT)
                for p in range(PAIR):
                    if p < 2:
                        need(pe, y_read, 4 * (c - 1) + p + 3)
                    else:
                        pe.wait_ge(xtok_copied, PAIR * c + p - 1)
                    for m in range(CT):
                        mm = pe.transpose(XT_[p % 2][:, m * P:(m + 1) * P], xc[u][:, m, p * P:(p + 1) * P],
                                          ident[:, :])
                    mm.then_inc(xtok_done, 1)

            def sum_squares(c):
                pe.wait_ge(squared, 2 * c + 2)
                for m in range(CT):
                    mm = pe.matmul(G_[m * 32:(m + 1) * 32, :], ones[:, :], sq[:, m, :], start=True, stop=True)
                mm.then_inc(ss_done, 1)

            def project(c, t):
                for m in range(CT):
                    mm = pe.matmul(Y0_[t // 2][:, (t % 2) * E:(t % 2 + 1) * E], y[:, m, t * P:(t + 1) * P],
                                   wf[:, m, :], start=(m == 0), stop=(m == CT - 1))
                if t % 2:
                    mm.then_inc(out_done, 1)

            def columns(c):
                pe.wait_ge(ss_copied, c + 1)
                for t in range(TT):
                    mm = pe.matmul(G_[:, t:t + 1], ssr[:, t * P:(t + 1) * P], pick[:, :], start=True, stop=True)
                mm.then_inc(col_done, 1)

            def turn_x1(c, u):
                pe.wait_ge(in_loaded[u], (c // 2) * PER_IO + PER_IO)
                for k in range(KT):
                    need(pe, xtok_copied, PAIR * (c - 1) + 3 + k)
                    for t in range(TT):
                        mm = pe.transpose(XT_[k][:, t * P:(t + 1) * P], xin[u][:, t, k * P:(k + 1) * P], ident[:, :])
                    mm.then_inc(turned, 1)

            def in_proj(c, j):
                if j == 0:
                    pe.wait_ge(xT_copied, 2 * c + 2)
                if j < 2:
                    need(pe, scanned, PAIR * (c - 1) + 3 + j)
                elif j == 3:
                    pe.wait_ge(dt_read, c + 1)
                elif j > 3:
                    pe.wait_ge(proj_by_act, NACT * c + j - 3)
                if j == 0:
                    for t in range(TT):
                        for k in range(KT):
                            mm = pe.matmul(PR_[0][:, t * NH:(t + 1) * NH], xT[:, k, t * P:(t + 1) * P],
                                           win[:, k, DT0:DPROJ], start=(k == 0), stop=(k == KT - 1))
                else:
                    col = XB0 + (j - 1) * P if j <= CT + 1 else (j - CT - 2) * P
                    for k in range(KT):
                        mm = pe.matmul(PR_[j % 3][:, :], win[:, k, col:col + P], xT[:, k, :],
                                       start=(k == 0), stop=(k == KT - 1))
                mm.then_inc(proj_done, 1)

            def y_products(c, half, q):
                if half == 0 and q == 0:
                    pe.wait_ge(xtok_copied, PAIR * c + PAIR)
                    pe.wait_ge(s_ready, PAIR * c + PAIR)
                if half == 0:
                    need_apart(pe, passed, (out_read, TT * (c - 1) + 2 * q + 2))
                r = slice(q * L, (q + 1) * L)
                for hp in range(2):
                    for p in range(PAIR):
                        for h2 in range(2):
                            h = 4 * half + 2 * hp + h2
                            col = (hp * PAIR + p) * L
                            mm = pe.matmul((Y0_, XT_)[half][q][h2 * HD:(h2 + 1) * HD, col:col + L],
                                           xtok[r, p, h * HD:(h + 1) * HD], S[r, p, h, :],
                                           start=True, stop=True)
                mm.then_inc(y_done, 1)

            def step(c, u, last):
                for j in range(2 * CT + 2):
                    if not last:
                        in_proj(c + 1, j)
                    if started(c) and 2 <= j < 6:
                        y_products(c, (j - 2) // 2, j % 2)
                if started(c):
                    sum_squares(c)
                    project(c, 0)
                    columns(c)
                    for t in range(1, TT):
                        project(c, t)
                if not last:
                    turn_x(c + 1, 1 - u)
                    products_of_b_c(c + 1, 1 - u)
                    spread_decay(c + 1, 0)
                    spread_decay(c + 1, 1)
                    if not (isinstance(c, int) and c + 2 >= NCHUNK):
                        turn_x1(c + 2, u)
                    spread_decay(c + 1, 2)
                    spread_decay(c + 1, 3)

            turn_x1(0, 0)
            stages(pe, step)

        @block.scalar
        def _(act):
            act.wait_ge(w_loaded, 16 * NW)
            act.wait_ge(const_set, NCONST)
            act.wait_ge(nega_chain, 1)
            act.activation(nega[:, :], nega[:, :], ACT.Exp).then_inc(nega_chain, 1)

            def copy_x1(c):
                for k in range(KT):
                    act.wait_ge(turned, 2 * c + k + 1)
                    act.activation(xT[:, k, :], XT_[k][:, :], ACT.Copy).then_inc(xT_copied, 1)

            def copy_x(c, m):
                act.wait_ge(proj_done, (2 * CT + 2) * c + m + 2)
                act.activation(xp[:, m, :, TAPS - 1:], PR_[(m + 1) % 3][:, :].rearrange("p (s t) -> p s t", s=SEQS),
                               ACT.Copy).then_inc(proj_by_act, 1)

            def softplus_and_copies(c):
                act.wait_ge(absx_ready, c + 1)
                act.activation(small["e"][:, :, :], small["absx"][:, :, :], ACT.Exp, scale=-1.0).then_inc(e_ready, 1)
                if isinstance(c, int) and c == 0:
                    act.wait_ge(xp_zeroed, 1)
                need(act, conv_done, (CT + 1) * c)
                copy_x(c, 0)
                act.wait_ge(u_ready, c + 1)
                act.activation(lnu[:, :, :], small["u"][:, :, :], ACT.Ln).then_inc(ln_ready, 1)
                copy_x(c, 1)
                act.wait_ge(prod_ready, c + 1)
                need(act, spread_ready, PAIR * c)
                act.activation(small["dA"][:, :, :], small["prod"][:, :, :], ACT.Exp).then_inc(dA_ready, 1)
                for m in range(2, CT + 1):
                    copy_x(c, m)

            def copy_z(c, u, m):
                need(act, gated, 2 * (c - 1))
                j = CT + 2 + m
                act.wait_ge(proj_done, (2 * CT + 2) * c + j + 1)
                act.activation(zs[u][:, m, :], PR_[j % 3][:, :], ACT.Copy).then_inc(proj_by_act, 1)

            def square(c, half):
                if half == 0:
                    need(act, ss_done, c)
                act.wait_ge(gated, 2 * c + half + 1)
                s = slice(2 * half, 2 * half + 2)
                act.activation(sq[:, s, :], y[:, s, :], ACT.Square).then_inc(squared, 1)

            def mean_square(c):
                act.wait_ge(ss_done, c + 1)
                act.activation(ssr[:, :], G_[:, :], ACT.Copy).then_inc(ss_copied, 1)
                act.wait_ge(col_done, c + 1)
                need(act, rstd_ready, c)
                act.activation(rms[:, :], G_[:, 0:TT], ACT.Sqrt, scale=1.0 / DI, bias=eps[:, :]).then_inc(col_read, 1)

            def silus(c, u):
                need(act, y_read, 4 * (c - 1))
                need(act, g_done, c - 1)
                for m in range(CT):
                    act.wait_ge(conv_done, (CT + 1) * c + m + 1)
                    act.activation(xc[u][:, m, :], cv[:, m, :], ACT.Silu, bias=cb[:, m:m + 1]).then_inc(silued, 1)
                act.wait_ge(conv_done, (CT + 1) * c + CT + 1)
                for n in range(2):
                    r = slice(n * DS, (n + 1) * DS)
                    act.activation(bc[u][:, n, :], cv[r, CT, :], ACT.Silu, bias=cb[r, CT:CT + 1]).then_inc(silued, 1)

            def silu_z(c, u):
                act.wait_ge(proj_by_act, NACT * (c + 1))
                act.activation(zs[u][:, :, :], zs[u][:, :, :], ACT.Silu).then_inc(z_silued, 1)

            def copy_xtok(c):
                need(act, y_done, 4 * c)
                for p in range(PAIR):
                    act.wait_ge(xtok_done, PAIR * c + p + 1)
                    act.activation(xtok[:, p, :], XT_[p % 2][:, :], ACT.Copy).then_inc(xtok_copied, 1)

            def step(c, u, last):
                if not last:
                    softplus_and_copies(c + 1)
                if started(c):
                    square(c, 0)
                if not last:
                    copy_z(c + 1, 1 - u, 0)
                    copy_z(c + 1, 1 - u, 1)
                if started(c):
                    square(c, 1)
                if not last:
                    copy_z(c + 1, 1 - u, 2)
                    copy_z(c + 1, 1 - u, 3)
                if started(c):
                    mean_square(c)
                if not last:
                    silus(c + 1, 1 - u)
                    copy_xtok(c + 1)
                    silu_z(c + 1, 1 - u)
                    if not (isinstance(c, int) and c + 2 >= NCHUNK):
                        copy_x1(c + 2)

            copy_x1(0)
            stages(act, step)

        @block.vector
        def _(dve):
            dve.wait_ge(w_loaded, 16 * NW)
            dve.tensor_scalar(nega[:, :], nega[:, :], A_LOG_MAX, None, ALU.min).then_inc(nega_chain, 1)
            dve.tensor_tensor(fcw[:, 0:KT, :], fcw[:, 0:KT, :], fcw[:, KT:, :], ALU.add).then_inc(fc_summed, 1)
            for m in range(CT):
                dve.wait_ge(folded, m + 1)
                dve.tensor_scalar(wf[:, m, :], bank[m][:, 0:E], normw[:, m:m + 1], None, ALU.mult)\
                    .then_inc(wf_ready, 1)
            dve.wait_ge(nega_chain, 2)
            dve.tensor_scalar(nega[:, :], nega[:, :], -1.0, None, ALU.mult).then_inc(nega_chain, 1)
            dve.wait_ge(nega_chain, 3)

            def A(c):
                def scan(p):
                    dve.wait_ge(da_done, PAIR * c + p + 1)
                    dve.wait_ge(inj_ready, PAIR * c + p + 1)
                    dve.tensor_tensor_scan(decay[p % 2][:, :], PR_[p % 2][:, :],
                                           inj[:, p].rearrange("p h t -> p (h t)"), 0.0, ALU.mult, ALU.add)\
                        .then_inc(scanned, 1)

                def times_g(p):
                    dve.wait_ge(scanned, PAIR * c + p + 1)
                    dve.tensor_tensor(S[:, p], decay[p % 2][:, :].rearrange("p (h t) -> p h t", h=NH),
                                      G_[:, p * L:(p + 1) * L].unsqueeze(1).broadcast_to((P, NH, L)), ALU.mult)\
                        .then_inc(s_ready, 1)

                need(dve, s_ready, PAIR * c)
                scan(0)
                scan(1)
                dve.wait_ge(g_done, c + 1)
                need(dve, y_done, 4 * c)
                for p in range(PAIR):
                    times_g(p)
                    if p + 2 < PAIR:
                        dve.wait_ge(s_ready, PAIR * c + p + 1)
                        scan(p + 2)

            CONV = ([(0, 0), (0, 1), (1, 0), (0, 2), (1, 1), (0, 3), (1, 2), (0, 4), (1, 3), (1, 4)]
                    + [(k, m) for k in range(2, TAPS) for m in range(CT + 1)])
            LINKED = (TAPS - 1) * (CT + 1)

            def conv(c, i):
                k, m = CONV[i]
                if k == 0:
                    dve.wait_ge(proj_by_act, NACT * c + m + 1)
                else:
                    dve.wait_ge(conv_chain, LINKED * c + CONV.index((k - 1, m)) + 1)
                src = xp[:, m, :, k:k + L]
                dst = cv[:, m, :].rearrange("p (s t) -> p s t", s=SEQS)
                if k == 0:
                    ins = dve.tensor_scalar(dst, src, cw[:, m, 0:1], None, ALU.mult)
                else:
                    ins = dve.scalar_tensor_tensor(out=dst, in0=src, scalar=cw[:, m, k:k + 1], in1=dst,
                                                   op0=ALU.mult, op1=ALU.add)
                ins.then_inc(conv_done if k == TAPS - 1 else conv_chain, 1)

            DT_LINKS = 7

            def convolve_and_dt(c, y_of_last):
                s = {n: v[:, :, :] for n, v in small.items()}
                chain = Chain(dve, dt_chain, DT_LINKS * c)
                dve.wait_ge(proj_done, (2 * CT + 2) * c + 1)
                need(dve, dt_chain, DT_LINKS * c)
                dve.tensor_tensor(s["x_dt"], PR_[0][:, 0:TT * NH].rearrange("p (t h) -> p t h", t=TT),
                                  dtb[:, :].unsqueeze(1).broadcast_to((P, TT, NH)), ALU.add).then_inc(dt_read, 1)
                dve.wait_ge(dt_read, c + 1)
                dve.scalar_tensor_tensor(out=s["absx"], in0=s["x_dt"], scalar=-1.0, in1=s["x_dt"],
                                         op0=ALU.mult, op1=ALU.max).then_inc(absx_ready, 1)
                dve.wait_ge(e_ready, c + 1)
                need(dve, inj_ready, PAIR * c)
                dve.tensor_scalar(s["u"], s["e"], 1.0, None, ALU.add).then_inc(u_ready, 1)
                dve.wait_ge(u_ready, c + 1)
                chain.link(dve.tensor_scalar(s["iz"], s["u"], 1.0, None, ALU.is_equal))
                chain.link(dve.scalar_tensor_tensor(out=s["den"], in0=s["u"], scalar=-1.0, in1=s["iz"],
                                                    op0=ALU.add, op1=ALU.add))
                chain.mark(dve.reciprocal(s["rden"], s["den"]))
                need(dve, silued, 6 * c)
                conv(c, 0)
                chain.wait()
                dve.wait_ge(ln_ready, c + 1)
                chain.link(dve.tensor_tensor(s["num"], lnu[:, :, :], s["iz"], ALU.add))
                chain.link(dve.tensor_tensor(s["num2"], s["num"], s["e"], ALU.mult))
                chain.link(dve.tensor_tensor(s["lp"], s["num2"], s["rden"], ALU.mult))
                chain.link(dve.scalar_tensor_tensor(out=s["dt"], in0=s["x_dt"], scalar=0.0, in1=s["lp"],
                                                    op0=ALU.max, op1=ALU.add))
                dve.tensor_tensor(s["prod"], s["dt"], nega[:, :].unsqueeze(1).broadcast_to((P, TT, NH)), ALU.mult)\
                    .then_inc(prod_ready, 1)
                for i in range(1, 7):
                    conv(c, i)
                y_of_last(0)
                conv(c, 7)
                conv(c, 8)
                y_of_last(1)
                for i in range(9, len(CONV)):
                    conv(c, i)

            def C(c, u, half):
                if half == 0:
                    need(dve, out_done, 2 * c)
                    need(dve, squared, 2 * c)
                    dve.wait_ge(z_silued, c + 1)
                for q in range(2):
                    dve.wait_ge(y_done, 4 * c + 2 * half + q + 1)
                    for hp in range(2):
                        m = 2 * half + hp
                        pq = "p (a q t) -> p q a t"
                        ins = dve.scalar_tensor_tensor(
                            out=y[:, m, :].rearrange(pq, q=2, t=L)[:, q],
                            in0=xc[u][:, m, :].rearrange(pq, q=2, t=L)[:, q], scalar=dskip[:, m:m + 1],
                            in1=(Y0_, XT_)[half][q][:, hp * PAIR * L:(hp + 1) * PAIR * L]
                            .rearrange("p (a t) -> p a t", t=L), op0=ALU.mult, op1=ALU.add)
                    ins.then_inc(y_read, 1)
                dve.wait_ge(y_read, 4 * c + 2 * half + 2)
                s = slice(2 * half, 2 * half + 2)
                dve.tensor_tensor(y[:, s, :], y[:, s, :], zs[u][:, s, :], ALU.mult).then_inc(gated, 1)

            def E_(c, u):
                if cols:
                    dve.wait_ge(pv_loaded[u], (c // 2) * PER_IO + PER_IO)
                dve.wait_ge(col_read, c + 1)
                need(dve, out_read, TT * c)
                dve.reciprocal(rstd[:, :], rms[:, :]).then_inc(rstd_ready, 1)
                dve.wait_ge(rstd_ready, c + 1)
                need(dve, o_stored[u], (c // 2) * PER_IO)
                for t in range(TT):
                    dve.wait_ge(out_done, 2 * c + t // 2 + 1)
                    dve.scalar_tensor_tensor(out=ot[u][:, t, :], in0=Y0_[t // 2][:, (t % 2) * E:(t % 2 + 1) * E],
                                             scalar=rstd[:, t:t + 1], in1=pv[u][:, t, :] if cols else bias[:, :],
                                             op0=ALU.mult, op1=ALU.add).then_inc(out_read, 1)

            def step(c, u, last):
                def y_of_last(half):
                    if started(c):
                        C(c, u, half)

                if last:
                    y_of_last(0)
                    y_of_last(1)
                else:
                    convolve_and_dt(c + 1, y_of_last)
                if started(c):
                    E_(c, u)
                if not last:
                    A(c + 1)

            stages(dve, step)


def build(nc, T, out):
    def scratch(name, shape):
        return nc.dram_tensor(name, shape, F32, kind="Internal").ap()

    qk = scratch("qk_t", (2, E, TOK))
    v = scratch("v_pairs", (2, PAIRS, P, B, N, DK))
    mixed = scratch("mixed_t", (E, TOK))
    x1 = scratch("x1", (TOK, E))
    by_rows = scratch("by_rows", (TOK, E))
    with nc.cleanup_on_exit():
        block_projections(nc, T["x"], T, qk, v)
        with nc.sbuf_tensor("att", [P, PAIRS, B * N, N], F32) as att:
            block_softmax(nc, qk, att)
            block_trilinear(nc, v, att, mixed)
        block_mlp(nc, T["x"], mixed, T, x1)
    W = {d: {n[3:]: a for n, a in T.items() if n.startswith(d + "_")} for d in ("mh", "mv")}
    W["mh"]["fc_b"] = T["fc_b"]
    block_mamba(nc, W["mh"], x1, by_rows, None, cols=False)
    block_mamba(nc, W["mv"], x1, out, by_rows, cols=True)


def kernel(**inputs):
    import numpy as np
    import concourse.bacc as bacc
    from concourse.bass_utils import run_bass_kernel_spmd

    a = {k: np.asarray(v) for k, v in inputs.items()}

    def col(v):
        return np.ascontiguousarray(v.reshape(-1, P).T)

    def by_head_of_pair(w):
        return np.ascontiguousarray(w.reshape(E, PAIRS, 2, DK).transpose(0, 2, 1, 3).reshape(E, E))

    def rows_of_mixed(w):
        return np.ascontiguousarray(w.reshape(PAIRS, 2, 2, STRIPS, STRIP_D, E).transpose(0, 2, 3, 1, 4, 5)
                                    .reshape(E, E))

    arrays = {"x": np.ascontiguousarray(a["x"].reshape(TOK, E)), "fc_b": a["L1_conv_fc_b"]}
    arrays["Wo"] = rows_of_mixed(a["L0_conv_Wo"])
    for n in ("Wq", "Wk", "W1", "W2", "b2", "ln_agg_g", "ln_agg_b", "ln_out_g", "ln_out_b"):
        arrays[n] = a["L0_conv_" + n]
    for n in ("Wv1", "Wv2"):
        arrays[n] = by_head_of_pair(a["L0_conv_" + n])
    arrays["b1"] = col(a["L0_conv_b1"])
    fc_wT = np.ascontiguousarray(a["L1_conv_fc_w"].T)
    for d, blocks in (("mv", slice(0, 2 * E)), ("mh", slice(2 * E, 4 * E))):
        g = {n: a[f"L1_conv_{d}_{n}"] for n in ("in_w", "conv_w", "conv_b", "dt_bias", "A_log", "D", "norm_w", "out_w")}
        arrays[d + "_in_wT"] = np.ascontiguousarray(g["in_w"].T)
        arrays[d + "_conv_w"] = np.ascontiguousarray(g["conv_w"].reshape(CT + 1, P, TAPS).transpose(1, 0, 2))
        arrays[d + "_conv_b"] = col(g["conv_b"])
        arrays[d + "_D"] = col(np.repeat(g["D"], HD))
        arrays[d + "_norm_w"] = col(g["norm_w"])
        arrays[d + "_dt_bias"], arrays[d + "_A_log"], arrays[d + "_out_w"] = g["dt_bias"], g["A_log"], g["out_w"]
        arrays[d + "_fc_wT"] = np.ascontiguousarray(fc_wT[blocks])
    nc = bacc.Bacc("TRN2", target_bir_lowering=False, num_devices=1)
    T = {n: nc.dram_tensor("in_" + n, v.shape, mybir.dt.from_np(v.dtype), kind="ExternalInput").ap()
         for n, v in arrays.items()}
    out = nc.dram_tensor("out", (TOK, E), F32, kind="ExternalOutput").ap()
    build(nc, T, out)
    r = run_bass_kernel_spmd(nc, [{"in_" + n: v for n, v in arrays.items()}], core_ids=[0])
    return r.results[0]["out"].reshape(B, N, N, E)
```

```python
from contextlib import ExitStack

import concourse.bass as bass
from concourse import mybir

F32 = mybir.dt.float32
F32R = mybir.dt.float32r
ALU = mybir.AluOpType
ACT = mybir.ActivationFunctionType
AX_X = mybir.AxisListType.X

P = 128
BANK = 512
B, N, E = 2, 64, 256
H = 8
DK = E // H
PAIRS = H // 2
TOK = B * N * N
KT = E // P
F = 2 * E
FT = F // P
STRIPS = 4
STRIP_D = DK // (2 * STRIPS)
SPLIT = (("hi", "hi"), ("lo", "hi"), ("hi", "lo"))
EPS = 1e-5
SCALE = DK ** -0.5

DI = 2 * E
DS = 64
NH = 8
HD = DI // NH
CT = DI // P
TAPS = 4
XB0 = DI
DT0 = DI + DI + 2 * DS
DPROJ = DT0 + NH
L = 64
CHUNK = 512
TT = CHUNK // P
SEQS = CHUNK // L
NCHUNK = TOK // CHUNK
A_LOG_MAX = 80.0


def need(eng, sem, value):
    if isinstance(value, int) and value <= 0:
        return
    eng.wait_ge(sem, value)


def need_apart(eng, passed, *waits):
    for sem, value in waits:
        need(eng, sem, value)
    eng.sem_inc(passed, 1)


class FirstV:

    def __init__(self, nc, ctx, v_dram):
        t_ = Tools(nc, ctx, "tri")
        self.v1, self.v2in = t_.sb("v1_0", [P, N, DK]), t_.sb("v2in", [P, N, DK])
        self.v1_loaded, self.v2_loaded = t_.sem("v1_loaded"), t_.sem("v2_loaded")
        self.v1_dram = v_dram.rearrange("(b i l) (v r h d) -> v r b h l i d", b=B, i=N, v=2, r=PAIRS, h=2)[0]
        self.v2_dram = v_dram.rearrange("(b l j) (v r h d) -> v r b h l j d", b=B, l=N, v=2, r=PAIRS, h=2)[1]

    @staticmethod
    def load(sp, tile, src, pr, b, done):
        for h2 in range(2):
            sp.dma_start(tile[h2 * N:(h2 + 1) * N, :, :],
                         src[bass.ds(pr, 1), b, h2].rearrange("o l i d -> (o l) i d")).then_inc(done, 16)


class Tools:

    def __init__(self, nc, ctx, tag):
        self.nc, self.ctx, self.tag = nc, ctx, tag

    def sb(self, name, shape, dt=F32):
        return self.ctx.enter_context(self.nc.sbuf_tensor(f"{self.tag}_{name}", shape, dt))

    def banks(self, n=8):
        return [self.ctx.enter_context(self.nc.psum_tensor(f"{self.tag}_bank{i}", [P, BANK], F32)) for i in range(n)]

    def sem(self, name):
        return self.nc.alloc_semaphore(name=f"{self.tag}_{name}")


class Chain:

    def __init__(self, eng, sem, base=0):
        self.eng, self.sem, self.base, self.n = eng, sem, base, 0

    def mark(self, ins):
        self.n += 1
        ins.then_inc(self.sem, 1)

    def value(self):
        return self.base + self.n

    def wait(self):
        self.eng.wait_ge(self.sem, self.value())

    def link(self, ins):
        self.mark(ins)
        self.wait()


def make_identity(pool, ident, sem):
    pool.memset(ident[:, :], 0.0).then_inc(sem, 1)
    pool.wait_ge(sem, 1)
    pool.affine_select(out=ident[:, :], in_=ident[:, :], compare_op=ALU.not_equal, fill=1.0, base=0,
                       pattern=[[-1, P]], channel_multiplier=1).then_inc(sem, 1)




def block_projections(nc, x, W, qk_dram, v_dram):
    STEPS = TOK // CHUNK
    with ExitStack() as ctx:
        t_ = Tools(nc, ctx, "prj")
        sb, sem = t_.sb, t_.sem
        bank = t_.banks()
        T_, Q_, V_ = bank[0:2], bank[2:6], bank[6:8]
        ident = sb("ident", [P, P])
        wqk = sb("wqk", [P, 2, KT, E])
        wv = sb("wv", [P, KT, 2, E])
        wqk_ = {n: sb(f"wqk_{n}", [P, 2, KT, E], F32R) for n in ("hi", "lo")}
        wv_ = {n: sb(f"wv_{n}", [P, KT, 2 * E], F32R) for n in ("hi", "lo")}
        xin = [sb(f"xin{u}", [P, TT, E]) for u in range(2)]
        xT = {n: [sb(f"xT{u}_{n}", [P, KT, CHUNK], F32R) for u in range(2)] for n in ("hi", "lo")}
        w_split = sem("w_split")
        qk = [sb(f"qk{u}", [P, 4, CHUNK]) for u in range(2)]
        vs = [sb(f"vs{u}", [P, TT, 2 * E]) for u in range(2)]
        ident_set, qk_w_loaded, v_w_loaded = sem("ident_set"), sem("qk_w_loaded"), sem("v_w_loaded")
        x_loaded = [sem(f"x_loaded{u}") for u in range(2)]
        transposed, xT_hi_ready, xT_lo_ready = sem("transposed"), sem("xT_hi_ready"), sem("xT_lo_ready")
        qk_done, qk_by_act, qk_by_dve = sem("qk_done"), sem("qk_by_act"), sem("qk_by_dve")
        v_done, v_by_act, v_by_dve = sem("v_done"), sem("v_by_act"), sem("v_by_dve")
        qk_stored = [sem(f"qk_stored{u}") for u in range(2)]
        v_stored = [sem(f"v_stored{u}") for u in range(2)]
        block = ctx.enter_context(nc.Block())
        rows = x.rearrange("(g t p) c -> g p t c", t=TT, p=P)
        qk_out = qk_dram.rearrange("(m p) t -> p m t", p=P)
        v_out = v_dram.rearrange("(g t p) c -> g p t c", t=TT, p=P)

        def stages(eng, step):
            step(0, 0, False)
            step(1, 1, False)
            with eng.Fori(1, STEPS // 2 - 1) as r:
                step(r * 2, 0, False)
                step(r * 2 + 1, 1, False)
            step(STEPS - 2, 0, False)
            step(STEPS - 1, 1, True)

        @block.sync
        def _(sp):
            def load(t, u):
                need(sp, transposed, 2 * t - 2)
                sp.dma_start(xin[u][:, :, :], rows[t]).then_inc(x_loaded[u], 16)

            load(0, 0)
            for m, name in enumerate(("Wq", "Wk")):
                sp.dma_start(wqk[:, m], W[name].rearrange("(k p) n -> p k n", p=P)).then_inc(qk_w_loaded, 16)
            load(1, 1)
            for m, name in enumerate(("Wv1", "Wv2")):
                sp.dma_start(wv[:, :, m], W[name].rearrange("(k p) n -> p k n", p=P)).then_inc(v_w_loaded, 16)
            with sp.Fori(1, STEPS // 2) as r:
                load(r * 2, 0)
                load(r * 2 + 1, 1)

        @block.gpsimd
        def _(pool):
            make_identity(pool, ident, ident_set)

            def store(t, u, last):
                pool.wait_ge(qk_by_act, 2 * t + 2)
                pool.wait_ge(qk_by_dve, 2 * t + 2)
                pool.dma_start(qk_out[:, :, bass.ds(t * CHUNK, CHUNK)], qk[u][:, :, :]).then_inc(qk_stored[u], 16)
                pool.wait_ge(v_by_act, 2 * t + 2)
                pool.wait_ge(v_by_dve, 2 * t + 2)
                pool.dma_start(v_out[t], vs[u][:, :, :]).then_inc(v_stored[u], 16)

            stages(pool, store)
            for u in range(2):
                pool.wait_ge(qk_stored[u], 16 * STEPS // 2)
                pool.wait_ge(v_stored[u], 16 * STEPS // 2)

        TERMS = [(k, xn, wn) for k in range(KT) for xn, wn in SPLIT]

        @block.tensor
        def _(pe):
            def turn(t, u):
                pe.wait_ge(x_loaded[u], (t // 2) * 16 + 16)
                need(pe, xT_lo_ready, 2 * t)
                for k in range(KT):
                    for tile in range(TT):
                        mm = pe.transpose(T_[k][:, tile * P:(tile + 1) * P], xin[u][:, tile, k * P:(k + 1) * P],
                                          ident[:, :])
                    mm.then_inc(transposed, 1)

            def step(t, u, last):
                pe.wait_ge(xT_lo_ready, 2 * t + 2)
                need(pe, qk_by_act, 2 * t)
                need(pe, qk_by_dve, 2 * t)
                for m in range(4):
                    for i, (k, xn, wn) in enumerate(TERMS):
                        mm = pe.matmul(Q_[m][:, :], wqk_[wn][:, m // 2, k, (m % 2) * P:(m % 2 + 1) * P],
                                       xT[xn][u][:, k, :], start=(i == 0), stop=(i == len(TERMS) - 1))
                    mm.then_inc(qk_done, 1)
                if not last:
                    turn(t + 1, 1 - u)
                if isinstance(t, int) and t == 0:
                    pe.wait_ge(w_split, 4)
                for tile in range(TT):
                    need(pe, (v_by_act, v_by_dve)[tile % 2], 2 * t + tile // 2)
                    for i, (k, xn, wn) in enumerate(TERMS):
                        mm = pe.matmul(V_[tile % 2][:, :], xT[xn][u][:, k, tile * P:(tile + 1) * P],
                                       wv_[wn][:, k, :], start=(i == 0), stop=(i == len(TERMS) - 1))
                    mm.then_inc(v_done, 1)

            pe.wait_ge(ident_set, 2)
            turn(0, 0)
            pe.wait_ge(w_split, 2)
            stages(pe, step)

        def evacuate(eng, copy, mine):
            by_qk, by_v = ((qk_by_act, v_by_act), (qk_by_dve, v_by_dve))[mine]

            def copy_xT(t, u):
                need(eng, v_done, TT * (t - 1))
                for k in range(KT):
                    if mine == 0:
                        eng.wait_ge(transposed, 2 * t + k + 1)
                        copy(xT["hi"][u][:, k, :], T_[k][:, :]).then_inc(xT_hi_ready, 1)
                    else:
                        eng.wait_ge(xT_hi_ready, 2 * t + k + 1)
                        eng.tensor_tensor(xT["lo"][u][:, k, :], T_[k][:, :], xT["hi"][u][:, k, :], ALU.subtract)\
                            .then_inc(xT_lo_ready, 1)

            def step(t, u, last):
                need(eng, qk_stored[u], (t // 2) * 16)
                for m in (2 * mine, 2 * mine + 1):
                    eng.wait_ge(qk_done, 4 * t + m + 1)
                    copy(qk[u][:, m, :], Q_[m][:, :]).then_inc(by_qk, 1)
                if not last:
                    copy_xT(t + 1, 1 - u)
                need(eng, v_stored[u], (t // 2) * 16)
                for tile in (mine, mine + 2):
                    eng.wait_ge(v_done, TT * t + tile + 1)
                    copy(vs[u][:, tile, :], V_[mine][:, :]).then_inc(by_v, 1)

            if mine == 1:
                for n, (src, loaded, parts) in enumerate(((wqk[:, :, :, :], qk_w_loaded, wqk_),
                                                          (wv[:, :, :, :].rearrange("p k v n -> p k (v n)"),
                                                           v_w_loaded, wv_))):
                    hi, lo = (parts[h][:] for h in ("hi", "lo"))
                    eng.wait_ge(loaded, 32)
                    copy(hi, src).then_inc(w_split, 1)
                    eng.wait_ge(w_split, 2 * n + 1)
                    eng.tensor_tensor(lo, src, hi, ALU.subtract).then_inc(w_split, 1)
                    if n == 0:
                        copy_xT(0, 0)
            else:
                copy_xT(0, 0)
            stages(eng, step)

        @block.scalar
        def _(act):
            evacuate(act, lambda o, i: act.activation(o, i, ACT.Copy), 0)

        @block.vector
        def _(dve):
            evacuate(dve, lambda o, i: dve.tensor_copy(o, i), 1)


def block_softmax(nc, qk_dram, att, first):
    LB = 4
    NB = N // LB
    KL = 8
    JB = 4
    HL = N // 2
    with ExitStack() as ctx:
        t_ = Tools(nc, ctx, "smx")
        sb, sem = t_.sb, t_.sem
        bank = t_.banks()
        S_, T_ = bank[0:4], bank[4:8]
        NS = len(S_)
        ident = sb("ident", [P, P])
        q = sb("q", [P, N * N])
        kb = [sb(f"kb{u}", [P, KL, 2, N]) for u in range(2)]
        last_att = att[:, PAIRS - 1].rearrange("p (h l) j -> p h l j", h=2)
        raw_odd = sb("raw", [P, 2, N, N])
        raws = [last_att, raw_odd[:, :, :, :]]
        mx = sb("mx", [P, 2, N])
        rsum = sb("rsum", [P, 2, N])
        rinv = sb("rinv", [P, 2, N])
        ident_set, kb_zeroed, q_loaded = sem("ident_set"), sem("kb_zeroed"), sem("q_loaded")
        k_loaded = [sem(f"k_loaded{u}") for u in range(2)]
        scored, s_copied = sem("scored"), sem("s_copied")
        maxed, shifted, exped = sem("maxed"), sem("shifted"), sem("exped")
        summed, inverted, normed = sem("summed"), sem("inverted"), [sem("normed0"), sem("normed1")]
        passed = sem("passed")
        turned, t_copied = sem("turned"), sem("t_copied")
        block = ctx.enter_context(nc.Block())

        @block.sync
        def _(sp):
            def load(pr):
                need(sp, scored, pr * NB)
                for b in range(B):
                    sp.dma_start(q[b * 64:(b + 1) * 64, :],
                                 qk_dram[pr * 64:(pr + 1) * 64, b * N * N:(b + 1) * N * N]).then_inc(q_loaded, 16)
                for c in range(N // KL):
                    need(sp, scored, pr * NB + (c - 1) * (KL // LB))
                    for b in range(B):
                        for h2 in range(2):
                            lo = (2 * b + h2) * DK
                            src = qk_dram[E + pr * 64 + h2 * DK:E + pr * 64 + (h2 + 1) * DK,
                                          b * N * N + c * KL * N:b * N * N + (c + 1) * KL * N]
                            sp.dma_start(kb[c % 2][lo:lo + DK, :, h2, :], src.rearrange("p (l j) -> p l j", l=KL))\
                                .then_inc(k_loaded[c % 2], 16)

            sp.wait_ge(kb_zeroed, 2)
            for pr in range(PAIRS):
                load(pr)
                if pr == 0:
                    first.load(sp, first.v2in, first.v2_dram, 0, 0, first.v2_loaded)
                    first.load(sp, first.v1, first.v1_dram, 0, 0, first.v1_loaded)

        @block.gpsimd
        def _(pool):
            for u in range(2):
                pool.memset(kb[u][:, :, :, :], 0.0).then_inc(kb_zeroed, 1)
            make_identity(pool, ident, ident_set)

            for pr in range(PAIRS):
                pool.wait_ge(inverted, pr * 2 + 1)
                for half in range(2):
                    v = raws[pr % 2][:, 0, half * HL:(half + 1) * HL, :]
                    pool.tensor_tensor(v, v, rinv[:, 0, :].unsqueeze(1).broadcast_to((P, HL, N)), ALU.mult)\
                        .then_inc(normed[0], 1)

        @block.tensor
        def _(pe):
            pe.wait_ge(ident_set, 2)
            qv = q[:, :].rearrange("p (i l) -> p l i", l=N)

            def scores(pr):
                pe.wait_ge(q_loaded, pr * 32 + 32)
                for g in range(NB):
                    c = g * LB // KL
                    if g * LB % KL == 0:
                        pe.wait_ge(k_loaded[c % 2], (pr * (N // KL // 2) + c // 2) * 64 + 64)
                    need_apart(pe, passed, (s_copied, pr * NB + g - NS + 1))
                    for l4 in range(LB):
                        for b in range(B):
                            r = slice(b * 64, (b + 1) * 64)
                            mm = pe.matmul(S_[g % NS][r, l4 * P:(l4 + 1) * P], qv[r, g * LB + l4, :],
                                           kb[c % 2][r, (g * LB + l4) % KL, :, :], start=True, stop=True)
                    mm.then_inc(scored, 1)

            def transposes(pr):
                pe.wait_ge(normed[0], pr * 2 + 2)
                pe.wait_ge(normed[1], pr * 2 + 2)
                for g in range(N // JB):
                    need(pe, t_copied, pr * (N // JB) + g - len(T_) + 1)
                    for j in range(JB):
                        mm = pe.transpose(T_[g % 4][:, j * P:(j + 1) * P],
                                          raws[pr % 2][:, :, :, g * JB + j].rearrange("p h l -> p (h l)"), ident[:, :])
                    mm.then_inc(turned, 1)

            scores(0)
            for pr in range(PAIRS):
                if pr + 1 < PAIRS:
                    scores(pr + 1)
                transposes(pr)

        @block.scalar
        def _(act):
            def copy_scores(pr, first, last):
                for g in range(first, last):
                    if g == 0:
                        need(act, turned, (pr - 1) * (N // JB))
                    act.wait_ge(scored, pr * NB + g + 1)
                    act.activation(raws[pr % 2][:, :, g * LB:(g + 1) * LB, :],
                                   S_[g % NS][:, :].rearrange("p (l h j) -> p h l j", l=LB, h=2), ACT.Copy)\
                        .then_inc(s_copied, 1)

            def exps(pr, h):
                for half in range(2):
                    act.wait_ge(shifted, pr * 4 + 2 * h + half + 1)
                    v = raws[pr % 2][:, h, half * HL:(half + 1) * HL, :]
                    act.activation(v, v, ACT.Exp, scale=SCALE).then_inc(exped, 1)

            def copy_att(pr):
                for g in range(N // JB):
                    act.wait_ge(turned, pr * (N // JB) + g + 1)
                    act.activation(att[:, pr, :, g * JB:(g + 1) * JB].rearrange("p m j -> p j m"),
                                   T_[g % 4][:, :].rearrange("p (j m) -> p j m", j=JB), ACT.Copy).then_inc(t_copied, 1)

            copy_scores(0, 0, NB)
            for pr in range(PAIRS):
                exps(pr, 0)
                if pr + 1 < PAIRS:
                    copy_scores(pr + 1, 0, NB // 4)
                exps(pr, 1)
                if pr + 1 < PAIRS:
                    copy_scores(pr + 1, NB // 4, NB)
                copy_att(pr)

        @block.vector
        def _(dve):
            for pr in range(PAIRS):
                raw = raws[pr % 2]
                dve.wait_ge(s_copied, pr * NB + NB)
                for h in range(2):
                    dve.tensor_reduce(mx[:, h, :], raw[:, h, :, :].rearrange("p l j -> p j l"), AX_X, ALU.max)\
                        .then_inc(maxed, 1)
                    dve.wait_ge(maxed, pr * 2 + h + 1)
                    for half in range(2):
                        v = raw[:, h, half * HL:(half + 1) * HL, :]
                        dve.tensor_tensor(v, v, mx[:, h, :].unsqueeze(1).broadcast_to((P, HL, N)), ALU.subtract)\
                            .then_inc(shifted, 1)
                for h in range(2):
                    dve.wait_ge(exped, pr * 4 + 2 * h + 2)
                    if h == 0:
                        need(dve, normed[0], pr * 2)
                    dve.tensor_reduce(rsum[:, h, :], raw[:, h, :, :].rearrange("p l j -> p j l"), AX_X, ALU.add)\
                        .then_inc(summed, 1)
                    dve.wait_ge(summed, pr * 2 + h + 1)
                    dve.reciprocal(rinv[:, h, :], rsum[:, h, :]).then_inc(inverted, 1)
                dve.wait_ge(inverted, pr * 2 + 2)
                for half in range(2):
                    v = raw[:, 1, half * HL:(half + 1) * HL, :]
                    dve.tensor_tensor(v, v, rinv[:, 1, :].unsqueeze(1).broadcast_to((P, HL, N)), ALU.mult)\
                        .then_inc(normed[1], 1)


def block_trilinear(nc, first, att, out_dram):
    G = 16
    NG = N // G
    QI = 4
    NQ = G // QI
    HI = G // 2
    M = 2 * STRIP_D
    DD = 22
    with ExitStack() as ctx:
        t_ = Tools(nc, ctx, "tri")
        sb, sem = t_.sb, t_.sem
        bank = t_.banks(NQ)
        v2ps = ctx.enter_context(nc.psum_tensor("tri_v2ps", [P, 3 * BANK], F32))
        v1 = [first.v1, sb("v1_1", [P, N, DK])]
        v2in = first.v2in
        v2sb = sb("v2sb", [P, DK - DD, N])
        av = [sb(f"av{u}", [P, DK, N]) for u in range(4)]
        sel = [sb(f"sel{u}", [P, DK // STRIP_D, STRIP_D * M]) for u in range(4)]
        ost = [sb(f"ost{u}", [P, 2, HI * N]) for u in range(2)]
        v1_loaded, v2_loaded = first.v1_loaded, first.v2_loaded
        v2_in_sb, v2_in_ps = sem("v2_in_sb"), sem("v2_in_ps")
        sel_zeroed, sums_zeroed, sel_ready = sem("sel_zeroed"), sem("sums_zeroed"), sem("sel_ready")
        av_by_dve, av_by_pool, i_done = sem("av_by_dve"), sem("av_by_pool"), sem("i_done")
        o_copied, o_stored = sem("o_copied"), [sem(f"o_stored{u}") for u in range(2)]
        block = ctx.enter_context(nc.Block())
        attf = att[:, :, :, :].rearrange("p r m j -> p (r m j)")
        v2d = v2ps[:, 0:DD * N].rearrange("p (d j) -> p d j", d=DD)

        def groups(eng, c, body):
            first = 0
            if isinstance(c, int) and c == 0:
                body(0, 0)
                first = 1
            with eng.Fori(first, NG) as g:
                body(g, c * N + g * G)

        def combinations(eng, combo):
            combo(0, 0)
            combo(0, 1)
            with eng.Fori(1, PAIRS) as pr:
                combo(pr, 0)
                combo(pr, 1)

        @block.sync
        def _(sp):
            def load(pr, b):
                c = pr * 2 + b
                need(sp, i_done, (c - 1) * N)
                first.load(sp, v1[b], first.v1_dram, pr, b, v1_loaded)
                need(sp, v2_in_ps, c)
                first.load(sp, v2in, first.v2_dram, pr, b, v2_loaded)

            def store(pr, b, g):
                for u in range(2):
                    sp.wait_ge(o_copied, ((pr * 2 + b) * NG + g) * NQ + (u + 1) * (NQ // 2))
                    rows = out_dram[bass.ds(pr * (2 * DK), 2 * DK),
                                    bass.ds(g * (G * N) + (b * N * N + u * HI * N), HI * N)]
                    for s in range(STRIPS):
                        sp.dma_start(rows.rearrange("(a s r) t -> s r a t", a=2, s=STRIPS)[s],
                                     ost[u][s * 32:s * 32 + M]).then_inc(o_stored[u], 16)

            def combo(pr, b, last=False):
                store(pr, b, 0)
                if not last:
                    load(*((pr, 1) if b == 0 else (pr + 1, 0)))
                with sp.Fori(1, NG) as g:
                    store(pr, b, g)

            combo(0, 0)
            combo(0, 1)
            with sp.Fori(1, PAIRS - 1) as pr:
                combo(pr, 0)
                combo(pr, 1)
            combo(PAIRS - 1, 0)
            combo(PAIRS - 1, 1, last=True)
            for u in range(2):
                sp.wait_ge(o_stored[u], 16 * STRIPS * B * PAIRS * NG)

        def multiply(eng, v2_ready, ready, v2, d0, d1):
            def combo(pr, b):
                def body(g, n):
                    eng.wait_ge(v2_ready, pr * 2 + b + 1)
                    for k in range(G):
                        need(eng, i_done, n + k - 3)
                        a = attf[:, bass.ds((n + k) * N, N)]
                        eng.tensor_tensor(av[k % 4][:, d0:d1, :], a.unsqueeze(1).broadcast_to((P, d1 - d0, N)),
                                          v2, ALU.mult).then_inc(ready, 1)

                groups(eng, pr * 2 + b, body)

            combinations(eng, combo)

        @block.gpsimd
        def _(pool):
            for u in range(4):
                pool.memset(sel[u][:, :, :], 0.0).then_inc(sel_zeroed, 1)
            multiply(pool, v2_in_sb, av_by_pool, v2sb[:, :, :], DD, DK)

        @block.vector
        def _(dve):
            for q in range(NQ):
                dve.memset(bank[q][:, :], 0.0).then_inc(sums_zeroed, 1)
            multiply(dve, v2_in_ps, av_by_dve, v2d, 0, DD)

        @block.tensor
        def _(pe):
            pe.wait_ge(sums_zeroed, NQ)

            def combo(pr, b):
                def body(g, n):
                    for k in range(G):
                        q = k // QI
                        if k % QI == 0:
                            need(pe, o_copied, ((pr * 2 + b) * NG + g) * NQ + q - NQ + 1)
                        pe.wait_ge(sel_ready, (n + k) * 2 + 2)
                        pe.wait_ge(av_by_dve, n + k + 1)
                        for a in range(2):
                            if a == 1:
                                pe.wait_ge(av_by_pool, n + k + 1)
                            col = a * (QI * N) + (k % QI) * N
                            for d4 in range(STRIP_D):
                                for s in range(STRIPS):
                                    dg = a * STRIPS + s
                                    mm = pe.matmul(bank[q][s * 32:s * 32 + M, col:col + N],
                                                   sel[k % 4][:, dg, d4 * M:(d4 + 1) * M],
                                                   av[k % 4][:, dg * STRIP_D + d4, :],
                                                   start=(d4 == 0), stop=(d4 == STRIP_D - 1))
                        mm.then_inc(i_done, 1)

                groups(pe, pr * 2 + b, body)

            combinations(pe, combo)

        @block.scalar
        def _(act):
            act.wait_ge(sel_zeroed, 4)

            def turn_v2(pr, b):
                c = pr * 2 + b
                act.wait_ge(v2_loaded, c * 32 + 32)
                need(act, av_by_pool, c * N)
                turned = v2in[:, :, :].rearrange("p j d -> p d j")
                act.activation(v2sb[:, :, :], turned[:, DD:], ACT.Copy).then_inc(v2_in_sb, 1)
                need(act, av_by_dve, c * N)
                for lo in range(0, DD, BANK // N):
                    hi = min(lo + BANK // N, DD)
                    ins = act.activation(v2d[:, lo:hi], turned[:, lo:hi], ACT.Copy)
                ins.then_inc(v2_in_ps, 1)

            def copy_sums(gi, q):
                u = q // 2
                need(act, o_stored[u], gi * (16 * STRIPS))
                act.wait_ge(i_done, gi * G + (q + 1) * QI)
                lo = (q % 2) * QI * N
                act.activation(ost[u][:, :, lo:lo + QI * N], bank[q][:, :].rearrange("p (a t) -> p a t", a=2),
                               ACT.Copy).then_inc(o_copied, 1)

            def combo(pr, b, last=False):
                c = pr * 2 + b

                def body(g, n):
                    gi = c * NG + g
                    act.wait_ge(v1_loaded, c * 32 + 32)
                    for k in range(G):
                        need(act, i_done, n + k - 3)
                        for h2 in range(2):
                            r = slice(h2 * N, (h2 + 1) * N)
                            src = v1[b][r, bass.ds(g * G + k, 1), :].rearrange("p o (g f) -> p (o g) f", f=STRIP_D)
                            lo = h2 * STRIP_D
                            act.activation(sel[k % 4][r, :, lo:lo + (STRIP_D - 1) * (M + 1) + 1:M + 1], src,
                                           ACT.Copy).then_inc(sel_ready, 1)
                        if k == 2 and not (isinstance(gi, int) and gi == 0):
                            copy_sums(gi - 1, NQ - 1)
                        if k in (6, 10, 14):
                            copy_sums(gi, (k - 6) // QI)

                groups(act, c, body)
                if not last:
                    turn_v2(*((pr, 1) if b == 0 else (pr + 1, 0)))

            turn_v2(0, 0)
            combo(0, 0)
            combo(0, 1)
            with act.Fori(1, PAIRS - 1) as pr:
                combo(pr, 0)
                combo(pr, 1)
            combo(PAIRS - 1, 0)
            combo(PAIRS - 1, 1, last=True)
            copy_sums(B * PAIRS * NG - 1, NQ - 1)


def pipeline(eng, n, front, back):
    front(0, 0)
    for c in (0, 1):
        front(c + 1, (c + 1) % 2)
        back(c, c % 2)
    with eng.Fori(1, n // 2 - 1) as r:
        for u in range(2):
            front(r * 2 + (u + 1), (u + 1) % 2)
            back(r * 2 + u, u)
    front(n - 1, (n - 1) % 2)
    back(n - 2, n % 2)
    back(n - 1, (n - 1) % 2)


def block_mlp(nc, x, attn_dram, W, x1):
    with ExitStack() as ctx:
        t_ = Tools(nc, ctx, "mlp")
        sb, sem = t_.sb, t_.sem
        bank = t_.banks()
        WO_, HID_, OUT_ = bank[0:2], bank[2:6], bank[6:8]
        ident = sb("ident", [P, P])
        wo, w1, w2 = sb("wo", [P, KT, E]), sb("w1", [P, KT, F]), sb("w2", [P, FT, E])
        b1 = sb("b1", [P, FT])
        row = {n: sb(n, [P, E]) for n in ("g1", "be1", "b2", "g2", "be2")}
        eps = sb("eps", [P, 1])
        att = [sb(f"att{u}", [P, KT, CHUNK]) for u in range(2)]
        xin = [sb(f"xin{u}", [P, TT, E]) for u in range(2)]
        h = [sb(f"h{u}", [P, TT, E]) for u in range(2)]
        hb = [sb(f"hb{u}", [P, TT, E]) for u in range(2)]
        hT = [sb(f"hT{u}", [P, KT, CHUNK]) for u in range(2)]
        hid = sb("hid", [P, FT, CHUNK])
        o = [sb(f"o{u}", [P, TT, E]) for u in range(2)]
        stats = [sb(f"stats{n}", [P, TT, 6]) for n in range(2)]
        mv = [sb(f"mv{n}", [P, TT, 2]) for n in range(2)]
        std = [sb(f"std{n}", [P, TT]) for n in range(2)]
        rstd = [sb(f"rstd{n}", [P, TT]) for n in range(2)]
        ident_set, w_loaded, eps_set = sem("ident_set"), sem("w_loaded"), sem("eps_set")
        wo_loaded, rows_loaded = sem("wo_loaded"), sem("rows_loaded")
        in_loaded = [sem(f"in_loaded{u}") for u in range(2)]
        wo_done, added = sem("wo_done"), sem("added")
        moments, rooted = [sem(f"moments{n}") for n in range(2)], [sem(f"rooted{n}") for n in range(2)]
        f_chain, b_chain = sem("f_chain"), sem("b_chain")
        h_ready, h_turned, hT_ready = sem("h_ready"), sem("h_turned"), sem("hT_ready")
        hid_done, hid_ready, w2_done, w2_added = sem("hid_done"), sem("hid_ready"), sem("w2_done"), sem("w2_added")
        o_ready, b2_added = sem("o_ready"), sem("b2_added")
        passed = sem("passed")
        o_stored = [sem(f"o_stored{u}") for u in range(2)]
        LINKS = (4, 4)
        rows_in = x.rearrange("(c t p) e -> c p t e", t=TT, p=P)
        rows_out = x1.rearrange("(c t p) e -> c p t e", t=TT, p=P)
        attv = attn_dram.rearrange("(k p) t -> p k t", p=P)
        block = ctx.enter_context(nc.Block())

        @block.sync
        def _(sp):
            def load(c, u):
                need(sp, added, 2 * c - 2)
                sp.dma_start(att[u][:, :, :], attv[:, :, bass.ds(c * CHUNK, CHUNK)]).then_inc(in_loaded[u], 16)
                sp.dma_start(xin[u][:, :, :], rows_in[c]).then_inc(in_loaded[u], 16)

            def store(c, u):
                sp.wait_ge(o_ready, c + 1)
                sp.dma_start(rows_out[c], o[u][:, :, :]).then_inc(o_stored[u], 16)

            sp.dma_start(wo[:, :, :], W["Wo"].rearrange("(k p) n -> p k n", p=P)).then_inc(wo_loaded, 16)
            load(0, 0)
            for n, name in (("g1", "ln_agg_g"), ("be1", "ln_agg_b"), ("b2", "b2"), ("g2", "ln_out_g"),
                            ("be2", "ln_out_b")):
                sp.dma_start(row[n][:, :], W[name].partition_broadcast(P)).then_inc(rows_loaded, 16)
            sp.dma_start(b1[:, :], W["b1"]).then_inc(rows_loaded, 16)
            load(1, 1)
            sp.dma_start(w1[:, :, :], W["W1"].rearrange("(k p) n -> p k n", p=P)).then_inc(w_loaded, 16)
            sp.dma_start(w2[:, :, :], W["W2"].rearrange("(k p) n -> p k n", p=P)).then_inc(w_loaded, 16)
            for c in (0, 1):
                load(c + 2, c)
                store(c, c)
            with sp.Fori(1, NCHUNK // 2 - 1) as r:
                for u in range(2):
                    load(r * 2 + (u + 2), u)
                    store(r * 2 + u, u)
            store(NCHUNK - 2, 0)
            store(NCHUNK - 1, 1)
            for u in range(2):
                sp.wait_ge(o_stored[u], NCHUNK // 2 * 16)

        @block.gpsimd
        def _(pool):
            pool.memset(eps[:, :], EPS).then_inc(eps_set, 1)
            make_identity(pool, ident, ident_set)

        @block.tensor
        def _(pe):
            pe.wait_ge(ident_set, 2)
            pe.wait_ge(wo_loaded, 16)

            def times_wo(c, u):
                pe.wait_ge(in_loaded[u], (c // 2) * 32 + 32)
                need(pe, hT_ready, 2 * c)
                for t in range(TT):
                    for k in range(KT):
                        mm = pe.matmul(WO_[t // 2][:, (t % 2) * E:(t % 2 + 1) * E], att[u][:, k, t * P:(t + 1) * P],
                                       wo[:, k, :], start=(k == 0), stop=(k == KT - 1))
                    if t % 2:
                        mm.then_inc(wo_done, 1)

            def turn_h(c, u):
                pe.wait_ge(h_ready, c + 1)
                for k in range(KT):
                    for t in range(TT):
                        mm = pe.transpose(WO_[k][:, t * P:(t + 1) * P], h[u][:, t, k * P:(k + 1) * P], ident[:, :])
                    mm.then_inc(h_turned, 1)

            def mlp(c, u, turn_next):
                pe.wait_ge(hT_ready, 2 * c + 2)
                for m in range(FT):
                    need(pe, hid_ready, FT * (c - 1) + m + 1)
                    for k in range(KT):
                        mm = pe.matmul(HID_[m][:, :], w1[:, k, m * P:(m + 1) * P], hT[u][:, k, :],
                                       start=(k == 0), stop=(k == KT - 1))
                    mm.then_inc(hid_done, 1)
                need(pe, w2_added, 2 * c)
                for t in range(TT):
                    for k in range(FT):
                        if t == 0:
                            pe.wait_ge(hid_ready, FT * c + k + 1)
                        mm = pe.matmul(OUT_[t // 2][:, (t % 2) * E:(t % 2 + 1) * E], hid[:, k, t * P:(t + 1) * P],
                                       w2[:, k, :], start=(k == 0), stop=(k == FT - 1))
                    if t % 2:
                        mm.then_inc(w2_done, 1)
                    if t == 2:
                        turn_next()

            times_wo(0, 0)
            turn_h(0, 0)
            pe.wait_ge(w_loaded, 32)

            def step(c, u):
                times_wo(c + 1, 1 - u)
                mlp(c, u, lambda: turn_h(c + 1, 1 - u))

            step(0, 0)
            step(1, 1)
            with pe.Fori(1, NCHUNK // 2 - 1) as r:
                step(r * 2, 0)
                step(r * 2 + 1, 1)
            step(NCHUNK - 2, 0)
            mlp(NCHUNK - 1, 1, lambda: None)

        @block.scalar
        def _(act):
            act.wait_ge(eps_set, 1)
            act.wait_ge(rows_loaded, 16 * 6)

            def root(n, c):
                act.wait_ge(moments[n], c + 1)
                act.activation(std[n][:, :], mv[n][:, :, 1], ACT.Sqrt, bias=eps[:, :]).then_inc(rooted[n], 1)

            def copy_hT(c, u):
                for k in range(KT):
                    act.wait_ge(h_turned, 2 * c + k + 1)
                    act.activation(hT[u][:, k, :], WO_[k][:, :], ACT.Copy).then_inc(hT_ready, 1)

            def relu(c, u, last=False):
                need(act, w2_done, 2 * c)
                for m in range(FT):
                    act.wait_ge(hid_done, FT * c + m + 1)
                    act.activation(hid[:, m, :], HID_[m][:, :], ACT.Relu, bias=b1[:, m:m + 1]).then_inc(hid_ready, 1)
                    if m == 1 and not last:
                        root(0, c + 1)

            root(0, 0)
            copy_hT(0, 0)

            def step(c, u):
                relu(c, u)
                copy_hT(c + 1, 1 - u)
                root(1, c)

            step(0, 0)
            step(1, 1)
            with act.Fori(1, NCHUNK // 2 - 1) as r:
                step(r * 2, 0)
                step(r * 2 + 1, 1)
            step(NCHUNK - 2, 0)
            relu(NCHUNK - 1, 1, last=True)
            root(1, NCHUNK - 1)

        @block.vector
        def _(dve):
            dve.wait_ge(rows_loaded, 16 * 6)

            def wide(v):
                return v[:, :].unsqueeze(1).broadcast_to((P, TT, E))

            def layer_norm(n, c, chain, v, out, gain, bias, done):
                for t in range(TT):
                    ins = dve.bn_stats(stats[n][:, t, :], v[:, t, :])
                chain.mark(ins)
                need_apart(dve, passed, (f_chain if n == 0 else b_chain, chain.value()))
                for t in range(TT):
                    ins = dve.bn_aggr(mv[n][:, t, :], stats[n][:, t, :])
                ins.then_inc(moments[n], 1)
                dve.wait_ge(moments[n], c + 1)
                dve.wait_ge(rooted[n], c + 1)
                chain.link(dve.reciprocal(rstd[n][:, :], std[n][:, :]))
                for t in range(TT):
                    ins = dve.tensor_scalar(out[:, t, :], v[:, t, :], mv[n][:, t, 0:1], rstd[n][:, t:t + 1],
                                            ALU.subtract, ALU.mult)
                chain.link(ins)
                chain.link(dve.tensor_tensor(out[:, :, :], out[:, :, :], wide(gain), ALU.mult))
                dve.tensor_tensor(out[:, :, :], out[:, :, :], wide(bias), ALU.add).then_inc(done, 1)

            def front(c, u):
                chain = Chain(dve, f_chain, c * LINKS[0])
                dve.wait_ge(in_loaded[u], (c // 2) * 32 + 32)
                need(dve, h_turned, 2 * c - 2)
                for half in range(2):
                    dve.wait_ge(wo_done, 2 * c + half + 1)
                    s = slice(2 * half, 2 * half + 2)
                    dve.tensor_tensor(h[u][:, s, :], WO_[half][:, :].rearrange("p (t e) -> p t e", t=2),
                                      xin[u][:, s, :], ALU.add).then_inc(added, 1)
                dve.wait_ge(added, 2 * c + 2)
                layer_norm(0, c, chain, h[u], h[u], row["g1"], row["be1"], h_ready)
                dve.wait_ge(h_ready, c + 1)

            def back(c, u):
                chain = Chain(dve, b_chain, c * LINKS[1])
                dve.tensor_tensor(hb[u][:, :, :], h[u][:, :, :], wide(row["b2"]), ALU.add).then_inc(b2_added, 1)
                dve.wait_ge(b2_added, c + 1)
                for half in range(2):
                    dve.wait_ge(w2_done, 2 * c + half + 1)
                    s = slice(2 * half, 2 * half + 2)
                    dve.tensor_tensor(hb[u][:, s, :], OUT_[half][:, :].rearrange("p (t e) -> p t e", t=2),
                                      hb[u][:, s, :], ALU.add).then_inc(w2_added, 1)
                dve.wait_ge(w2_added, 2 * c + 2)
                need(dve, o_stored[u], (c // 2) * 16)
                layer_norm(1, c, chain, hb[u], o[u], row["g2"], row["be2"], o_ready)

            pipeline(dve, NCHUNK, front, back)


def block_mamba(nc, W, x1, out, prev, cols):
    with ExitStack() as ctx:
        t_ = Tools(nc, ctx, "mv" if cols else "mh")
        sb, sem = t_.sb, t_.sem
        bank = t_.banks()
        XT_ = bank[0:2]
        PR_ = bank[2:5]
        G_ = bank[5]
        Y0_ = bank[6:8]
        PAIR = SEQS // 2
        ident, ones_blk, ones_blk_r = sb("ident", [P, P]), sb("ones_blk", [P, P]), sb("ones_blk_r", [P, P], F32R)
        diag, diag0 = sb("diag", [P, L]), sb("diag0", [P, L])
        ones = sb("ones", [P, 32])
        pick = sb("pick", [P, 1])
        eps = sb("eps", [P, 1])
        win_hi, win_lo = sb("win_hi", [P, KT, DPROJ], F32R), sb("win_lo", [P, KT, DPROJ], F32R)
        wf = sb("wf", [P, CT, E])
        out_w, fcw = sb("out_w", [P, KT, DI]), sb("fcw", [P, 2 * KT, E])
        cw, cb = sb("cw", [P, CT + 1, TAPS]), sb("cb", [P, CT + 1])
        dskip, normw = sb("dskip", [P, CT]), sb("normw", [P, CT])
        dtb, nega, bias = sb("dtb", [P, NH]), sb("nega", [P, NH]), sb("bias", [P, E])
        xin = [sb(f"xin{u}", [P, TT, E]) for u in range(2)]
        pv = [sb(f"pv{u}", [P, TT, E]) for u in range(2)] if cols else None
        ot = [sb(f"ot{u}", [P, TT, E]) for u in range(2)]
        xT_hi, xT_lo = sb("xT_hi", [P, KT, CHUNK], F32R), sb("xT_lo", [P, KT, CHUNK], F32R)
        xp = sb("xp", [P, CT + 1, SEQS, L + TAPS - 1])
        cv = sb("cv", [P, CT + 1, CHUNK])
        xc = [sb(f"xc{u}", [P, CT, CHUNK]) for u in range(2)]
        bc = [sb(f"bc{u}", [DS, 2, CHUNK]) for u in range(2)]
        zs = [sb(f"zs{u}", [P, CT, CHUNK]) for u in range(2)]
        small = {n: sb(n, [P, TT, NH]) for n in ("x_dt", "absx", "e", "u", "iz", "den", "rden", "num", "num2", "lp",
                                                 "dt", "prod", "dA")}
        dtT = sb("dtT", [NH, CHUNK])
        dtT_copied, dt_turned = sem("dtT_copied"), sem("dt_turned")
        dA_split, win_split, x_split = sem("dA_split"), sem("win_split"), sem("x_split")
        lnu = sb("lnu", [P, TT, NH])
        xtok = sb("xtok", [P, PAIR, DI])
        dA_hi, dA_lo = sb("dA_hi", [P, TT, NH], F32R), sb("dA_lo", [P, TT, NH], F32R)
        spread = [sb(f"spread{n}", [P, PAIR, NH, L], F32R) for n in ("hi", "lo")]
        inj = sb("inj", [P, PAIR, NH, L])
        decay = [sb(f"decay{p}", [P, NH * L]) for p in range(PAIR)]
        S = sb("S", [P, PAIR, NH, L])
        y, sq = sb("y", [P, CT, CHUNK]), sb("sq", [P, CT, CHUNK])
        win = xp[:, :, :, :].rearrange("p m s t -> p (m s t)")[:, 0:KT * DPROJ].rearrange("p (k n) -> p k n", k=KT)
        ssr = sb("ssr", [P, CHUNK])
        rms, rstd = sb("rms", [P, TT]), sb("rstd", [P, TT])

        const_set, w_loaded, folded, wf_ready = sem("const_set"), sem("w_loaded"), sem("folded"), sem("wf_ready")
        win_loaded, out_w_loaded = sem("win_loaded"), sem("out_w_loaded")
        fc_summed, nega_chain, xp_zeroed = sem("fc_summed"), sem("nega_chain"), sem("xp_zeroed")
        in_loaded = [sem(f"in_loaded{u}") for u in range(2)]
        turned, xT_copied, proj_done, proj_by_act = sem("turned"), sem("xT_copied"), sem("proj_done"), sem("proj_by_act")
        dt_read, conv_chain, conv_done, silued = sem("dt_read"), sem("conv_chain"), sem("conv_done"), sem("silued")
        absx_ready, e_ready, u_ready, ln_ready = sem("absx_ready"), sem("e_ready"), sem("u_ready"), sem("ln_ready")
        dt_chain, prod_ready, dA_ready = sem("dt_chain"), sem("prod_ready"), sem("dA_ready")
        xtok_done, xtok_copied, g_done = sem("xtok_done"), sem("xtok_copied"), sem("g_done")
        spread_ready, inj_ready = sem("spread_ready"), sem("inj_ready")
        da_done, scanned, s_ready = sem("da_done"), sem("scanned"), sem("s_ready")
        y_done, y_read, gated, squared, z_silued = (sem("y_done"), sem("y_read"), sem("gated"), sem("squared"),
                                                    sem("z_silued"))
        ss_done, ss_copied, col_done, col_read, rstd_ready = (sem("ss_done"), sem("ss_copied"), sem("col_done"),
                                                              sem("col_read"), sem("rstd_ready"))
        out_done, out_read, passed = sem("out_done"), sem("out_read"), sem("passed")
        o_stored = [sem(f"o_stored{u}") for u in range(2)]
        pv_loaded = [sem(f"pv_loaded{u}") for u in range(2)] if cols else None
        NCONST = 13 + CT
        NACT = 2 * CT + 1
        PER_IO = 16 if not cols else 4 * 16

        rows = {n: a.rearrange("(c t p) e -> c p t e", t=TT, p=P) for n, a in (("x", x1), ("o", out))}
        grid = {n: a.rearrange("(b h c t q) e -> b q h c t e", b=B, h=N, t=2, q=2)
                for n, a in (("x", x1), ("o", out), ("p", prev if cols else x1))}
        block = ctx.enter_context(nc.Block())

        def stages(eng, step):
            step(-1, 1, False)
            step(0, 0, False)
            step(1, 1, False)
            with eng.Fori(1, NCHUNK // 2 - 1) as r:
                for u in range(2):
                    step(r * 2 + u, u, False)
            step(NCHUNK - 2, 0, False)
            step(NCHUNK - 1, 1, True)

        def is_chunk(c):
            return not (isinstance(c, int) and c >= NCHUNK)

        def started(c):
            return not (isinstance(c, int) and c < 0)

        @block.sync
        def _(sp):
            def move(name, c, tile, to_dram, done):
                if not cols:
                    a, b = tile[:, :, :], rows[name][c]
                    sp.dma_start(*((b, a) if to_dram else (a, b))).then_inc(done, 16)
                    return
                for b in range(B):
                    for q in range(2):
                        a = tile[q * L:(q + 1) * L, 2 * b:2 * b + 2, :]
                        d = grid[name][b, q, :, c]
                        sp.dma_start(*((d, a) if to_dram else (a, d))).then_inc(done, 16)

            def load(c, u):
                need(sp, turned, 2 * c - 2)
                move("x", c, xin[u], False, in_loaded[u])

            def load_prev(c, u):
                if cols:
                    need(sp, out_read, TT * (c - 1))
                    move("p", c, pv[u], False, pv_loaded[u])

            def step(c, u, last):
                if not started(c):
                    return
                if is_chunk(c + 2):
                    load(c + 2, u)
                sp.wait_ge(out_read, TT * c + TT)
                move("o", c, ot[u], True, o_stored[u])
                if is_chunk(c + 2):
                    load_prev(c + 2, u)

            load(0, 0)
            sp.dma_start(win, W["in_wT"].rearrange("(k p) n -> p k n", p=P)).then_inc(win_loaded, 16)
            sp.dma_start(dtb[:, :], W["dt_bias"].partition_broadcast(P)).then_inc(w_loaded, 16)
            sp.dma_start(nega[:, :], W["A_log"].partition_broadcast(P)).then_inc(w_loaded, 16)
            sp.dma_start(cw[:], W["conv_w"]).then_inc(w_loaded, 16)
            sp.dma_start(cb[:], W["conv_b"]).then_inc(w_loaded, 16)
            out_side = [(out_w[:, :, :], W["out_w"].rearrange("(k p) n -> p k n", p=P)),
                        (fcw[:, :, :], W["fc_wT"].rearrange("(k p) n -> p k n", p=P)),
                        (dskip[:, :], W["D"]), (normw[:, :], W["norm_w"])]
            if not cols:
                out_side.append((bias[:, :], W["fc_b"].partition_broadcast(P)))
            for dst, src in out_side:
                sp.dma_start(dst, src).then_inc(out_w_loaded, 16)
            load(1, 1)
            load_prev(0, 0)
            load_prev(1, 1)
            stages(sp, step)
            for u in range(2):
                sp.wait_ge(o_stored[u], NCHUNK // 2 * PER_IO)

        @block.gpsimd
        def _(pool):
            make_identity(pool, ident, const_set)
            pool.memset(ones[:, :], 1.0).then_inc(const_set, 1)
            pool.memset(pick[:, :], 0.0).then_inc(const_set, 1)
            pool.memset(eps[:, :], EPS).then_inc(const_set, 1)
            pool.memset(ones_blk[:, :], 0.0).then_inc(const_set, 1)
            pool.wait_ge(const_set, 6)
            for m in range(CT):
                pool.memset(pick[m * 32:m * 32 + 1, :], 1.0).then_inc(const_set, 1)
            pool.wait_ge(const_set, 6 + CT)
            for q in range(2):
                r = slice(q * L, (q + 1) * L)
                pool.memset(ones_blk[r, r], 1.0).then_inc(const_set, 1)
                pool.tensor_copy(diag[r, :], ident[r, r]).then_inc(const_set, 1)
                pool.tensor_copy(diag0[r, :], ident[r, r]).then_inc(const_set, 1)
            pool.wait_ge(const_set, 12 + CT)
            pool.memset(diag0[:, 0:1], 0.0).then_inc(const_set, 1)
            pool.wait_ge(const_set, NCONST)
            pool.tensor_copy(ones_blk_r[:, :], ones_blk[:, :]).then_inc(const_set, 1)
            pool.wait_ge(win_split, 4)
            pool.memset(xp[:, :, :, :], 0.0).then_inc(xp_zeroed, 1)

            def step(c, u, last):
                if not last:
                    A(c + 1)

            def A(c):
                need_apart(pool, passed, (dA_ready, c + 1), (spread_ready, 2 * PAIR * c))
                pool.tensor_copy(dA_hi[:, :, :], small["dA"][:, :, :]).then_inc(dA_split, 1)
                pool.wait_ge(dA_split, 2 * c + 1)
                pool.tensor_tensor(dA_lo[:, :, :], small["dA"][:, :, :], dA_hi[:, :, :], ALU.subtract)\
                    .then_inc(dA_split, 1)
                pool.wait_ge(dA_split, 2 * c + 2)
                for p in range(PAIR):
                    need(pool, da_done, PAIR * (c - 1) + p + 1)
                    for part, dA in zip(spread, (dA_hi, dA_lo)):
                        pool.tensor_tensor(part[:, p], diag0[:, :].unsqueeze(1).broadcast_to((P, NH, L)),
                                           dA[:, p, :].unsqueeze(2).broadcast_to((P, NH, L)), ALU.mult)\
                            .then_inc(spread_ready, 1)
                    need(pool, scanned, PAIR * (c - 1) + p + 1)
                    pool.tensor_tensor(inj[:, p], diag[:, :].unsqueeze(1).broadcast_to((P, NH, L)),
                                       small["dt"][:, p, :].unsqueeze(2).broadcast_to((P, NH, L)), ALU.mult)\
                        .then_inc(inj_ready, 1)

            stages(pool, step)

        @block.tensor
        def _(pe):
            pe.wait_ge(const_set, NCONST + 1)
            def fold():
                pe.wait_ge(fc_summed, 1)
                for m in range(CT):
                    for k in range(KT):
                        mm = pe.matmul(Y0_[m // 2][:, (m % 2) * E:(m % 2 + 1) * E], out_w[:, k, m * P:(m + 1) * P],
                                       fcw[:, k, :], start=(k == 0), stop=(k == KT - 1))
                mm.then_inc(folded, 1)
                pe.wait_ge(wf_ready, CT)

            def products_of_b_c(c, u):
                need_apart(pe, passed, (silued, 6 * c + 6), (col_read, c))
                for s in range(SEQS):
                    mm = pe.matmul(G_[(s % 2) * L:(s % 2 + 1) * L, (s // 2) * L:(s // 2 + 1) * L],
                                   bc[u][:, 0, s * L:(s + 1) * L], bc[u][:, 1, s * L:(s + 1) * L],
                                   start=True, stop=True)
                mm.then_inc(g_done, 1)

            def spread_decay(c, p):
                if p == 0:
                    pe.wait_ge(proj_by_act, NACT * (c + 1))
                elif p == 3:
                    pe.wait_ge(scanned, PAIR * c + 1)
                pe.wait_ge(spread_ready, 2 * (PAIR * c + p + 1))
                for n in range(2):
                    mm = pe.matmul(PR_[(p + 1) % 3][:, :], ones_blk_r[:, :], spread[n][:, p].rearrange("p h t -> p (h t)"),
                                   start=(n == 0), stop=(n == 1))
                mm.then_inc(da_done, 1)

            def turn_x(c, u):
                pe.wait_ge(silued, 6 * c + CT)
                for p in range(PAIR):
                    if p < 2 and is_chunk(c + 1):
                        pe.wait_ge(x_split, 2 * (c + 1) + p + 1)
                    elif p < 2:
                        pe.wait_ge(y_read, 4 * (c - 1) + p + 3)
                    else:
                        pe.wait_ge(xtok_copied, PAIR * c + p - 1)
                    for m in range(CT):
                        mm = pe.transpose(XT_[p % 2][:, m * P:(m + 1) * P], xc[u][:, m, p * P:(p + 1) * P],
                                          ident[:, :])
                    mm.then_inc(xtok_done, 1)

            def sum_squares(c):
                pe.wait_ge(squared, 2 * c + 2)
                for m in range(CT):
                    mm = pe.matmul(G_[m * 32:(m + 1) * 32, :], ones[:, :], sq[:, m, :], start=True, stop=True)
                mm.then_inc(ss_done, 1)

            def project(c, t):
                for m in range(CT):
                    mm = pe.matmul(Y0_[t // 2][:, (t % 2) * E:(t % 2 + 1) * E], y[:, m, t * P:(t + 1) * P],
                                   wf[:, m, :], start=(m == 0), stop=(m == CT - 1))
                if t % 2:
                    mm.then_inc(out_done, 1)

            def columns(c):
                pe.wait_ge(ss_copied, c + 1)
                for t in range(TT):
                    mm = pe.matmul(G_[:, t:t + 1], ssr[:, t * P:(t + 1) * P], pick[:, :], start=True, stop=True)
                mm.then_inc(col_done, 1)

            def turn_x1(c, u):
                pe.wait_ge(in_loaded[u], (c // 2) * PER_IO + PER_IO)
                for k in range(KT):
                    need(pe, y_read, 4 * (c - 2) + 3 + k)
                    for t in range(TT):
                        mm = pe.transpose(XT_[k][:, t * P:(t + 1) * P], xin[u][:, t, k * P:(k + 1) * P], ident[:, :])
                    mm.then_inc(turned, 1)

            def in_proj(c, j):
                if j == 0:
                    pe.wait_ge(x_split, 2 * c + 2)
                if j < 2:
                    need(pe, scanned, PAIR * (c - 1) + 3 + j)
                elif j == 3:
                    pe.wait_ge(dt_read, c + 1)
                elif j > 3:
                    pe.wait_ge(proj_by_act, NACT * c + j - 3)
                xT_, win_ = {"hi": xT_hi, "lo": xT_lo}, {"hi": win_hi, "lo": win_lo}
                terms = [(k, xT_[xn], win_[wn]) for k in range(KT) for xn, wn in SPLIT]
                if j == 0:
                    for i, (k, x, w) in enumerate(terms):
                        mm = pe.matmul(PR_[0][0:NH, :], w[:, k, DT0:DPROJ], x[:, k, :],
                                       start=(i == 0), stop=(i == len(terms) - 1))
                else:
                    col = XB0 + (j - 1) * P if j <= CT + 1 else (j - CT - 2) * P
                    for i, (k, x, w) in enumerate(terms):
                        mm = pe.matmul(PR_[j % 3][:, :], w[:, k, col:col + P], x[:, k, :],
                                       start=(i == 0), stop=(i == len(terms) - 1))
                mm.then_inc(proj_done, 1)

            def turn_dt(c):
                need_apart(pe, passed, (dtT_copied, c + 1))
                for t in range(TT):
                    mm = pe.transpose(PR_[0][:, t * NH:(t + 1) * NH], dtT[:, t * P:(t + 1) * P], ident[0:NH, 0:NH])
                mm.then_inc(dt_turned, 1)

            def y_products(c, half, q):
                if half == 0 and q == 0:
                    pe.wait_ge(xtok_copied, PAIR * c + PAIR)
                    pe.wait_ge(s_ready, PAIR * c + PAIR)
                if half == 0:
                    need_apart(pe, passed, (out_read, TT * (c - 1) + 2 * q + 2))
                r = slice(q * L, (q + 1) * L)
                for hp in range(2):
                    for p in range(PAIR):
                        for h2 in range(2):
                            h = 4 * half + 2 * hp + h2
                            col = (hp * PAIR + p) * L
                            mm = pe.matmul((Y0_, XT_)[half][q][h2 * HD:(h2 + 1) * HD, col:col + L],
                                           xtok[r, p, h * HD:(h + 1) * HD], S[r, p, h, :],
                                           start=True, stop=True)
                mm.then_inc(y_done, 1)

            def step(c, u, last):
                for j in range(2 * CT + 2):
                    if not last:
                        in_proj(c + 1, j)
                    if not last and j == 1:
                        turn_dt(c + 1)
                    if started(c) and 2 <= j < 6:
                        y_products(c, (j - 2) // 2, j % 2)
                if started(c):
                    sum_squares(c)
                if is_chunk(c + 2):
                    turn_x1(c + 2, u)
                if started(c):
                    project(c, 0)
                    columns(c)
                    for t in range(1, TT):
                        project(c, t)
                if not last:
                    turn_x(c + 1, 1 - u)
                    products_of_b_c(c + 1, 1 - u)
                    for p in range(PAIR):
                        spread_decay(c + 1, p)
                if not started(c):
                    fold()

            turn_x1(0, 0)
            pe.wait_ge(win_split, 4)
            stages(pe, step)

        @block.scalar
        def _(act):

            def copy_x1(c):
                for k in range(KT):
                    act.wait_ge(turned, 2 * c + k + 1)
                    act.activation(xT_hi[:, k, :], XT_[k][:, :], ACT.Copy).then_inc(xT_copied, 1)

            def copy_x(c, m):
                act.wait_ge(proj_done, (2 * CT + 2) * c + m + 2)
                act.activation(xp[:, m, :, TAPS - 1:], PR_[(m + 1) % 3][:, :].rearrange("p (s t) -> p s t", s=SEQS),
                               ACT.Copy).then_inc(proj_by_act, 1)

            def softplus_and_copies(c):
                act.wait_ge(proj_done, (2 * CT + 2) * c + 1)
                act.activation(dtT[:, :], PR_[0][0:NH, :], ACT.Copy).then_inc(dtT_copied, 1)
                act.wait_ge(absx_ready, c + 1)
                act.activation(small["e"][:, :, :], small["absx"][:, :, :], ACT.Exp, scale=-1.0).then_inc(e_ready, 1)
                if isinstance(c, int) and c == 0:
                    act.wait_ge(xp_zeroed, 1)
                need(act, conv_done, (CT + 1) * c)
                copy_x(c, 0)
                act.wait_ge(u_ready, c + 1)
                act.activation(lnu[:, :, :], small["u"][:, :, :], ACT.Ln).then_inc(ln_ready, 1)
                copy_x(c, 1)
                act.wait_ge(prod_ready, c + 1)
                need(act, dA_split, 2 * c)
                act.activation(small["dA"][:, :, :], small["prod"][:, :, :], ACT.Exp).then_inc(dA_ready, 1)
                for m in range(2, CT + 1):
                    copy_x(c, m)

            def copy_z(c, u, m):
                need(act, gated, 2 * (c - 1))
                j = CT + 2 + m
                act.wait_ge(proj_done, (2 * CT + 2) * c + j + 1)
                act.activation(zs[u][:, m, :], PR_[j % 3][:, :], ACT.Copy).then_inc(proj_by_act, 1)

            def square(c, half):
                if half == 0:
                    need(act, ss_done, c)
                act.wait_ge(gated, 2 * c + half + 1)
                s = slice(2 * half, 2 * half + 2)
                act.activation(sq[:, s, :], y[:, s, :], ACT.Square).then_inc(squared, 1)

            def copy_sums(c):
                act.wait_ge(ss_done, c + 1)
                act.activation(ssr[:, :], G_[:, :], ACT.Copy).then_inc(ss_copied, 1)

            def mean_square(c):
                act.wait_ge(col_done, c + 1)
                need(act, rstd_ready, c)
                act.activation(rms[:, :], G_[:, 0:TT], ACT.Sqrt, scale=1.0 / DI, bias=eps[:, :]).then_inc(col_read, 1)

            def silus(c, u):
                need(act, y_read, 4 * (c - 1))
                need(act, g_done, c - 1)
                for m in range(CT):
                    act.wait_ge(conv_done, (CT + 1) * c + m + 1)
                    act.activation(xc[u][:, m, :], cv[:, m, :], ACT.Silu, bias=cb[:, m:m + 1]).then_inc(silued, 1)
                act.wait_ge(conv_done, (CT + 1) * c + CT + 1)
                for n in range(2):
                    r = slice(n * DS, (n + 1) * DS)
                    act.activation(bc[u][:, n, :], cv[r, CT, :], ACT.Silu, bias=cb[r, CT:CT + 1]).then_inc(silued, 1)

            def silu_z(c, u):
                act.wait_ge(proj_by_act, NACT * (c + 1))
                act.activation(zs[u][:, :, :], zs[u][:, :, :], ACT.Silu).then_inc(z_silued, 1)

            def copy_xtok(c):
                need(act, y_done, 4 * c)
                for p in range(PAIR):
                    act.wait_ge(xtok_done, PAIR * c + p + 1)
                    act.activation(xtok[:, p, :], XT_[p % 2][:, :], ACT.Copy).then_inc(xtok_copied, 1)

            def step(c, u, last):
                if not last:
                    softplus_and_copies(c + 1)
                if started(c):
                    square(c, 0)
                if not last:
                    copy_z(c + 1, 1 - u, 0)
                    copy_z(c + 1, 1 - u, 1)
                if started(c):
                    square(c, 1)
                if not last:
                    copy_z(c + 1, 1 - u, 2)
                    copy_z(c + 1, 1 - u, 3)
                if started(c):
                    copy_sums(c)
                if is_chunk(c + 2):
                    copy_x1(c + 2)
                if started(c):
                    mean_square(c)
                if not last:
                    silus(c + 1, 1 - u)
                    copy_xtok(c + 1)
                    silu_z(c + 1, 1 - u)

            copy_x1(0)
            act.wait_ge(w_loaded, 16 * 4)
            act.wait_ge(const_set, NCONST + 1)
            act.wait_ge(nega_chain, 1)
            act.activation(nega[:, :], nega[:, :], ACT.Exp).then_inc(nega_chain, 1)
            stages(act, step)

        @block.vector
        def _(dve):
            dve.wait_ge(win_loaded, 16)
            for k in range(KT):
                dve.tensor_copy(win_hi[:, k], win[:, k]).then_inc(win_split, 1)
            dve.wait_ge(win_split, 2)
            for k in range(KT):
                dve.tensor_tensor(win_lo[:, k], win[:, k], win_hi[:, k], ALU.subtract).then_inc(win_split, 1)

            def set_nega():
                dve.wait_ge(w_loaded, 16 * 4)
                dve.tensor_scalar(nega[:, :], nega[:, :], A_LOG_MAX, None, ALU.min).then_inc(nega_chain, 1)
                dve.wait_ge(nega_chain, 2)
                dve.tensor_scalar(nega[:, :], nega[:, :], -1.0, None, ALU.mult).then_inc(nega_chain, 1)
                dve.wait_ge(nega_chain, 3)

            def sum_fc():
                dve.wait_ge(out_w_loaded, 16 * (4 if cols else 5))
                dve.tensor_tensor(fcw[:, 0:KT, :], fcw[:, 0:KT, :], fcw[:, KT:, :], ALU.add).then_inc(fc_summed, 1)

            def scale_by_norm():
                dve.wait_ge(folded, 1)
                for m in range(CT):
                    dve.tensor_scalar(wf[:, m, :], Y0_[m // 2][:, (m % 2) * E:(m % 2 + 1) * E], normw[:, m:m + 1],
                                      None, ALU.mult).then_inc(wf_ready, 1)

            def A(c):
                def scan(p):
                    dve.wait_ge(da_done, PAIR * c + p + 1)
                    dve.wait_ge(inj_ready, PAIR * c + p + 1)
                    dve.tensor_tensor_scan(decay[p][:, :], PR_[(p + 1) % 3][:, :],
                                           inj[:, p].rearrange("p h t -> p (h t)"), 0.0, ALU.mult, ALU.add)\
                        .then_inc(scanned, 1)

                def times_g(p):
                    dve.wait_ge(scanned, PAIR * c + p + 1)
                    dve.tensor_tensor(S[:, p], decay[p][:, :].rearrange("p (h t) -> p h t", h=NH),
                                      G_[:, p * L:(p + 1) * L].unsqueeze(1).broadcast_to((P, NH, L)), ALU.mult)\
                        .then_inc(s_ready, 1)

                need(dve, s_ready, PAIR * c)
                for p in range(PAIR):
                    scan(p)
                dve.wait_ge(g_done, c + 1)
                need(dve, y_done, 4 * c)
                for p in range(PAIR):
                    times_g(p)

            def split_x1(c):
                for k in range(KT):
                    dve.wait_ge(xT_copied, 2 * c + k + 1)
                    dve.tensor_tensor(xT_lo[:, k, :], XT_[k][:, :], xT_hi[:, k, :], ALU.subtract).then_inc(x_split, 1)

            CONV = ([(0, 0), (0, 1), (1, 0), (0, 2), (1, 1), (0, 3), (1, 2), (0, 4), (1, 3), (1, 4)]
                    + [(k, m) for k in range(2, TAPS) for m in range(CT + 1)])
            LINKED = (TAPS - 1) * (CT + 1)

            def conv(c, i):
                k, m = CONV[i]
                if k == 0:
                    dve.wait_ge(proj_by_act, NACT * c + m + 1)
                else:
                    dve.wait_ge(conv_chain, LINKED * c + CONV.index((k - 1, m)) + 1)
                src = xp[:, m, :, k:k + L]
                dst = cv[:, m, :].rearrange("p (s t) -> p s t", s=SEQS)
                if k == 0:
                    ins = dve.tensor_scalar(dst, src, cw[:, m, 0:1], None, ALU.mult)
                else:
                    ins = dve.scalar_tensor_tensor(out=dst, in0=src, scalar=cw[:, m, k:k + 1], in1=dst,
                                                   op0=ALU.mult, op1=ALU.add)
                ins.then_inc(conv_done if k == TAPS - 1 else conv_chain, 1)

            DT_LINKS = 7

            def convolve_and_dt(c, y_of_last):
                s = {n: v[:, :, :] for n, v in small.items()}
                chain = Chain(dve, dt_chain, DT_LINKS * c)
                dve.wait_ge(dt_turned, c + 1)
                need(dve, dt_chain, DT_LINKS * c)
                dve.tensor_tensor(s["x_dt"], PR_[0][:, 0:TT * NH].rearrange("p (t h) -> p t h", t=TT),
                                  dtb[:, :].unsqueeze(1).broadcast_to((P, TT, NH)), ALU.add).then_inc(dt_read, 1)
                dve.wait_ge(dt_read, c + 1)
                dve.scalar_tensor_tensor(out=s["absx"], in0=s["x_dt"], scalar=-1.0, in1=s["x_dt"],
                                         op0=ALU.mult, op1=ALU.max).then_inc(absx_ready, 1)
                dve.wait_ge(e_ready, c + 1)
                need(dve, inj_ready, PAIR * c)
                dve.tensor_scalar(s["u"], s["e"], 1.0, None, ALU.add).then_inc(u_ready, 1)
                dve.wait_ge(u_ready, c + 1)
                chain.link(dve.tensor_scalar(s["iz"], s["u"], 1.0, None, ALU.is_equal))
                chain.link(dve.scalar_tensor_tensor(out=s["den"], in0=s["u"], scalar=-1.0, in1=s["iz"],
                                                    op0=ALU.add, op1=ALU.add))
                chain.mark(dve.reciprocal(s["rden"], s["den"]))
                need(dve, silued, 6 * c)
                conv(c, 0)
                chain.wait()
                dve.wait_ge(ln_ready, c + 1)
                chain.link(dve.tensor_tensor(s["num"], lnu[:, :, :], s["iz"], ALU.add))
                chain.link(dve.tensor_tensor(s["num2"], s["num"], s["e"], ALU.mult))
                chain.link(dve.tensor_tensor(s["lp"], s["num2"], s["rden"], ALU.mult))
                chain.link(dve.scalar_tensor_tensor(out=s["dt"], in0=s["x_dt"], scalar=0.0, in1=s["lp"],
                                                    op0=ALU.max, op1=ALU.add))
                dve.tensor_tensor(s["prod"], s["dt"], nega[:, :].unsqueeze(1).broadcast_to((P, TT, NH)), ALU.mult)\
                    .then_inc(prod_ready, 1)
                for i in range(1, 5):
                    conv(c, i)
                y_of_last(0)
                conv(c, 5)
                conv(c, 6)
                y_of_last(1)
                for i in range(7, len(CONV)):
                    conv(c, i)
                    if i == 12 and is_chunk(c + 1):
                        split_x1(c + 1)

            def C(c, u, half):
                if half == 0:
                    need(dve, out_done, 2 * c)
                    need(dve, squared, 2 * c)
                    dve.wait_ge(z_silued, c + 1)
                for q in range(2):
                    dve.wait_ge(y_done, 4 * c + 2 * half + q + 1)
                    for hp in range(2):
                        m = 2 * half + hp
                        pq = "p (a q t) -> p q a t"
                        ins = dve.scalar_tensor_tensor(
                            out=y[:, m, :].rearrange(pq, q=2, t=L)[:, q],
                            in0=xc[u][:, m, :].rearrange(pq, q=2, t=L)[:, q], scalar=dskip[:, m:m + 1],
                            in1=(Y0_, XT_)[half][q][:, hp * PAIR * L:(hp + 1) * PAIR * L]
                            .rearrange("p (a t) -> p a t", t=L), op0=ALU.mult, op1=ALU.add)
                    ins.then_inc(y_read, 1)
                dve.wait_ge(y_read, 4 * c + 2 * half + 2)
                s = slice(2 * half, 2 * half + 2)
                dve.tensor_tensor(y[:, s, :], y[:, s, :], zs[u][:, s, :], ALU.mult).then_inc(gated, 1)

            def E_(c, u):
                if cols:
                    dve.wait_ge(pv_loaded[u], (c // 2) * PER_IO + PER_IO)
                dve.wait_ge(col_read, c + 1)
                need(dve, out_read, TT * c)
                dve.reciprocal(rstd[:, :], rms[:, :]).then_inc(rstd_ready, 1)
                dve.wait_ge(rstd_ready, c + 1)
                need(dve, o_stored[u], (c // 2) * PER_IO)
                for t in range(TT):
                    dve.wait_ge(out_done, 2 * c + t // 2 + 1)
                    dve.scalar_tensor_tensor(out=ot[u][:, t, :], in0=Y0_[t // 2][:, (t % 2) * E:(t % 2 + 1) * E],
                                             scalar=rstd[:, t:t + 1], in1=pv[u][:, t, :] if cols else bias[:, :],
                                             op0=ALU.mult, op1=ALU.add).then_inc(out_read, 1)

            def step(c, u, last):
                def y_of_last(half):
                    if started(c):
                        C(c, u, half)

                if last:
                    y_of_last(0)
                    y_of_last(1)
                else:
                    convolve_and_dt(c + 1, y_of_last)
                if started(c):
                    E_(c, u)
                if not started(c):
                    sum_fc()
                if not last:
                    A(c + 1)
                if not started(c):
                    scale_by_norm()

            split_x1(0)
            set_nega()
            stages(dve, step)


def build(nc, T, out):
    def scratch(name, shape):
        return nc.dram_tensor(name, shape, F32, kind="Internal").ap()

    qk = scratch("qk_t", (2 * E, TOK))
    v = scratch("v", (TOK, 2 * E))
    mixed = scratch("mixed_t", (E, TOK))
    x1 = scratch("x1", (TOK, E))
    by_rows = scratch("by_rows", (TOK, E))
    with nc.cleanup_on_exit():
        block_projections(nc, T["x"], T, qk, v)
        with ExitStack() as ctx:
            att = ctx.enter_context(nc.sbuf_tensor("att", [P, PAIRS, B * N, N], F32))
            first = FirstV(nc, ctx, v)
            block_softmax(nc, qk, att, first)
            block_trilinear(nc, first, att, mixed)
        block_mlp(nc, T["x"], mixed, T, x1)
    W = {d: {n[3:]: a for n, a in T.items() if n.startswith(d + "_")} for d in ("mh", "mv")}
    W["mh"]["fc_b"] = T["fc_b"]
    block_mamba(nc, W["mh"], x1, by_rows, None, cols=False)
    block_mamba(nc, W["mv"], x1, out, by_rows, cols=True)


def kernel(**inputs):
    import numpy as np
    import concourse.bacc as bacc
    from concourse.bass_utils import run_bass_kernel_spmd

    a = {k: np.asarray(v) for k, v in inputs.items()}

    def col(v):
        return np.ascontiguousarray(v.reshape(-1, P).T)

    def rows_of_mixed(w):
        return np.ascontiguousarray(w.reshape(PAIRS, 2, 2, STRIPS, STRIP_D, E).transpose(0, 2, 3, 1, 4, 5)
                                    .reshape(E, E))

    arrays = {"x": np.ascontiguousarray(a["x"].reshape(TOK, E)), "fc_b": a["L1_conv_fc_b"]}
    arrays["Wo"] = rows_of_mixed(a["L0_conv_Wo"])
    for n in ("Wq", "Wk", "Wv1", "Wv2", "W1", "W2", "b2", "ln_agg_g", "ln_agg_b", "ln_out_g", "ln_out_b"):
        arrays[n] = a["L0_conv_" + n]
    arrays["b1"] = col(a["L0_conv_b1"])
    fc_wT = np.ascontiguousarray(a["L1_conv_fc_w"].T)
    for d, blocks in (("mv", slice(0, 2 * E)), ("mh", slice(2 * E, 4 * E))):
        g = {n: a[f"L1_conv_{d}_{n}"] for n in ("in_w", "conv_w", "conv_b", "dt_bias", "A_log", "D", "norm_w", "out_w")}
        arrays[d + "_in_wT"] = np.ascontiguousarray(g["in_w"].T)
        arrays[d + "_conv_w"] = np.ascontiguousarray(g["conv_w"].reshape(CT + 1, P, TAPS).transpose(1, 0, 2))
        arrays[d + "_conv_b"] = col(g["conv_b"])
        arrays[d + "_D"] = col(np.repeat(g["D"], HD))
        arrays[d + "_norm_w"] = col(g["norm_w"])
        arrays[d + "_dt_bias"], arrays[d + "_A_log"], arrays[d + "_out_w"] = g["dt_bias"], g["A_log"], g["out_w"]
        arrays[d + "_fc_wT"] = np.ascontiguousarray(fc_wT[blocks])
    nc = bacc.Bacc("TRN2", target_bir_lowering=False, num_devices=1)
    T = {n: nc.dram_tensor("in_" + n, v.shape, mybir.dt.from_np(v.dtype), kind="ExternalInput").ap()
         for n, v in arrays.items()}
    out = nc.dram_tensor("out", (TOK, E), F32, kind="ExternalOutput").ap()
    build(nc, T, out)
    r = run_bass_kernel_spmd(nc, [{"in_" + n: v for n, v in arrays.items()}], core_ids=[0])
    return r.results[0]["out"].reshape(B, N, N, E)
```
